# Optimizing a Trainium2 kernel written in Bass

```python
import numpy as np
import jax
import jax.numpy as jnp

def _softmax(x, axis=-1):
    return jax.nn.softmax(x, axis=axis)

def _gelu(x):
    return jax.nn.gelu(x, approximate=True)

def _silu(x):
    return jax.nn.silu(x)

def _sigmoid(x):
    return jax.nn.sigmoid(x)

def _layernorm(x, axis=-1, eps=1e-05):
    m = jnp.mean(x, axis=axis, keepdims=True)
    v = jnp.var(x, axis=axis, keepdims=True)
    return (x - m) / jnp.sqrt(v + eps)

def _scatter_add(tgt, idx, src, axis=0):
    return tgt.at[idx].add(src)

def _segment_sum(src, seg, n):
    return jax.ops.segment_sum(src, seg, n)
kernel_name = 'mk_decoder_preln_d4_seqx_r8_615453'

def setup_inputs(seed: int=0):
    np.random.seed(seed)
    _w = jnp.asarray

    def _rec_inputs():
        import jax
        import jax.numpy as jnp
        _rk = jax.random.key(seed)
        x = 0.0003765 + 1 * jax.random.normal(jax.random.fold_in(_rk, 1), (4, 256, 128), jnp.float32)
        _lenS = 256 - jax.random.randint(jax.random.fold_in(_rk, 7), (4,), 0, max(1, 256 // 4) + 1, jnp.int32)
        _lenS2 = 512 - jax.random.randint(jax.random.fold_in(_rk, 8), (4,), 0, max(1, 512 // 4) + 1, jnp.int32)
        _ctx_1024P = jax.random.normal(jax.random.fold_in(_rk, 11), (4, 16, 128), jnp.float32)
        _ctx_1024c = jax.random.dirichlet(jax.random.fold_in(_rk, 511), 0.3 * jnp.ones((16,), jnp.float32), (4, 512))
        _ctx_1024t = jnp.einsum('bsk,bkd->bsd', _ctx_1024c, _ctx_1024P)
        _ctx_1024t = _ctx_1024t * jax.lax.rsqrt(jnp.mean(jnp.square(_ctx_1024t)) + 1e-12) * 0.953939
        ctx_1024 = -0.000292821 + 1.00034 * (_ctx_1024t + 0.3 * jax.random.normal(jax.random.fold_in(_rk, 611), (4, 512, 128), jnp.float32))
        _validS = jnp.arange(256)[None, :] < _lenS[:, None]
        _validS2 = jnp.arange(512)[None, :] < _lenS2[:, None]
        _causal = jnp.tril(jnp.ones((256, 256), dtype=bool))
        mask_Bx1xSxS2_ik1 = jnp.where(jnp.broadcast_to(_validS2[:, None, None, :], (4, 1, 256, 512)), 1, 0).astype(jnp.int32)
        mask_BxS2_bf1 = jnp.ones((4, 512), dtype=bool)
        mask_Bx1xSxS2_bf0 = jnp.logical_not(jnp.ones((4, 1, 256, 512), dtype=bool))
        return (x, ctx_1024, mask_Bx1xSxS2_ik1, mask_BxS2_bf1, mask_Bx1xSxS2_bf0)
    x, ctx_1024, mask_Bx1xSxS2_ik1, mask_BxS2_bf1, mask_Bx1xSxS2_bf0 = _rec_inputs()

    def _L0_attn_setup():
        import jax, jax.numpy as jnp
        import numpy as np
        import math
        B, T, E = (1, 256, 128)
        H = 8
        D = E // H // 2
        LAMBDA_INIT = 0.8 - 0.6 * math.exp(-0.3 * 1)
        SCALE_BASE = 512.0
        THETA = 10000.0

        def _rope_tables(T, d):
            inv_freq = 1.0 / THETA ** (jnp.arange(0, d, 2, dtype=jnp.float32) / d)
            pos = jnp.arange(T, dtype=jnp.float32)
            freqs = pos[:, None] * inv_freq[None, :]
            freqs = jnp.repeat(freqs, 2, axis=-1)
            sv = (jnp.arange(0, d, 2, dtype=jnp.float32) + 0.4 * d) / (1.4 * d)
            power = (pos - T // 2) / SCALE_BASE
            scale = sv[None, :] ** power[:, None]
            scale = jnp.concatenate([scale, scale], axis=-1)
            return (freqs, scale)

        def _rotate_half(x):
            x1 = x[..., 0::2]
            x2 = x[..., 1::2]
            return jnp.stack([-x2, x1], axis=-1).reshape(x.shape)

        def _apply_rope(t, freqs, scale):
            f = freqs[None, :, None, :]
            s = scale[None, :, None, :]
            return t * jnp.cos(f) * s + _rotate_half(t) * jnp.sin(f) * s
        key = jax.random.key(seed)
        ks = jax.random.split(key, 9)
        w = 0.02
        return {'x': jax.random.normal(ks[0], (B, T, E), dtype=jnp.float32), 'Wq': jax.random.normal(ks[1], (E, E), dtype=jnp.float32) * w, 'Wk': jax.random.normal(ks[2], (E, E), dtype=jnp.float32) * w, 'Wv': jax.random.normal(ks[3], (E, E), dtype=jnp.float32) * w, 'Wo': jax.random.normal(ks[4], (E, E), dtype=jnp.float32) * w, 'lambda_q1': jax.random.normal(ks[5], (D,), dtype=jnp.float32) * 0.1, 'lambda_k1': jax.random.normal(ks[6], (D,), dtype=jnp.float32) * 0.1, 'lambda_q2': jax.random.normal(ks[7], (D,), dtype=jnp.float32) * 0.1, 'lambda_k2': jax.random.normal(ks[8], (D,), dtype=jnp.float32) * 0.1}
    _L0_attn_all = _L0_attn_setup()
    _L0_attn_in = {k: v for k, v in _L0_attn_all.items() if k in ('Wq', 'Wk', 'Wv', 'Wo', 'lambda_q1', 'lambda_k1', 'lambda_q2', 'lambda_k2')}
    del _L0_attn_all

    def _L0_xattn_setup():
        import jax, jax.numpy as jnp
        import numpy as np
        EMBED = 128
        HEADS = 16
        HEAD_DIM = EMBED // HEADS
        key = jax.random.key(seed)
        ks = jax.random.split(key, 6)
        N, S, E = (2, 256, EMBED)
        value = jax.random.normal(ks[0], (N, S, E), dtype=jnp.float32)
        k = jax.random.normal(ks[1], (N, S, E), dtype=jnp.float32)
        q = jax.random.normal(ks[2], (N, S, E), dtype=jnp.float32)
        mask = jax.random.randint(ks[3], (N, 1, S, S), 0, 2, dtype=jnp.int32)
        W_fc = jax.random.normal(ks[4], (E, E), dtype=jnp.float32) * (1.0 / np.sqrt(E))
        b_fc = jax.random.normal(ks[5], (E,), dtype=jnp.float32) * 0.01
        return {'value': value, 'key': k, 'query': q, 'mask': mask, 'W_fc': W_fc, 'b_fc': b_fc}
    _L0_xattn_all = _L0_xattn_setup()
    _L0_xattn_in = {k: v for k, v in _L0_xattn_all.items() if k in ('W_fc', 'b_fc')}
    del _L0_xattn_all

    def _L0_ffn_setup():
        import jax, jax.numpy as jnp
        import numpy as np
        import math
        D_MODEL, D_FF, N_EXPERTS, TOP_K, N_SHARED = (128, 512, 8, 2, 1)
        B, T = (4, 128)
        SCALE = 1.0 / math.sqrt(N_SHARED + TOP_K / N_EXPERTS)
        key = jax.random.key(seed)
        ks = jax.random.split(key, 10)
        s1 = 1.0 / math.sqrt(D_MODEL)
        s2 = 1.0 / math.sqrt(D_FF)
        return {'x': jax.random.normal(ks[0], (B, T, D_MODEL), dtype=jnp.float32), 'w_router': jax.random.normal(ks[1], (N_EXPERTS, D_MODEL), dtype=jnp.float32) * s1, 'W1': jax.random.normal(ks[2], (N_EXPERTS, D_FF, D_MODEL), dtype=jnp.float32) * s1, 'b1': jax.random.normal(ks[3], (N_EXPERTS, D_FF), dtype=jnp.float32) * 0.02, 'W2': jax.random.normal(ks[4], (N_EXPERTS, D_MODEL, D_FF), dtype=jnp.float32) * s2, 'b2': jax.random.normal(ks[5], (N_EXPERTS, D_MODEL), dtype=jnp.float32) * 0.02, 'Ws1': jax.random.normal(ks[6], (D_FF, D_MODEL), dtype=jnp.float32) * s1, 'bs1': jax.random.normal(ks[7], (D_FF,), dtype=jnp.float32) * 0.02, 'Ws2': jax.random.normal(ks[8], (D_MODEL, D_FF), dtype=jnp.float32) * s2, 'bs2': jax.random.normal(ks[9], (D_MODEL,), dtype=jnp.float32) * 0.02}
    _L0_ffn_all = _L0_ffn_setup()
    _L0_ffn_in = {k: v for k, v in _L0_ffn_all.items() if k in ('w_router', 'W1', 'b1', 'W2', 'b2', 'Ws1', 'bs1', 'Ws2', 'bs2')}
    del _L0_ffn_all

    def _L1_attn_setup():
        import jax, jax.numpy as jnp
        import numpy as np
        B, T, C, H = (4, 128, 128, 16)
        D = C // H

        def _expmap0_split(u):
            mink = -u[..., :1] ** 2 + jnp.sum(u[..., 1:] ** 2, axis=-1, keepdims=True)
            nomin = jnp.sqrt(jnp.maximum(mink, 1e-08))
            time = jnp.cosh(nomin)
            space = jnp.sinh(nomin) * u[..., 1:] / nomin
            return (time, space)
        key = jax.random.key(seed)
        ks = jax.random.split(key, 6)
        s = 1.0 / np.sqrt(C)
        return {'x': jax.random.normal(ks[0], (B, T, C), jnp.float32), 'W_qkv': jax.random.normal(ks[1], (C, 3 * C), jnp.float32) * s, 'b_qkv': jnp.zeros((3 * C,), jnp.float32), 'W_out': jax.random.normal(ks[2], (C, C), jnp.float32) * s, 'b_out': jnp.zeros((C,), jnp.float32), 'w_sur': jax.random.normal(ks[3], (C,), jnp.float32) * s, 'b_sur': jnp.zeros((), jnp.float32), 'threshold': jnp.float32(0.5)}
    _L1_attn_all = _L1_attn_setup()
    _L1_attn_in = {k: v for k, v in _L1_attn_all.items() if k in ('W_qkv', 'b_qkv', 'W_out', 'b_out', 'w_sur', 'b_sur', 'threshold')}
    del _L1_attn_all

    def _L1_xattn_setup():
        import jax, jax.numpy as jnp
        import numpy as np
        N_HEADS = 16
        D_MODEL = 128
        HEAD_DIM = D_MODEL // N_HEADS
        MASK_FILL = -100000000.0

        def _split_heads(x):
            B, S, _ = x.shape
            return x.reshape(B, S, N_HEADS, HEAD_DIM).transpose(0, 2, 1, 3)
        key = jax.random.key(seed)
        ks = jax.random.split(key, 12)
        B, L, P = (2, 256, 256)
        s = 1.0 / np.sqrt(D_MODEL).astype(np.float32)
        inp = {'q': jax.random.normal(ks[0], (B, L, D_MODEL), dtype=jnp.float32), 'k': jax.random.normal(ks[1], (B, P, D_MODEL), dtype=jnp.float32), 'v': jax.random.normal(ks[2], (B, P, D_MODEL), dtype=jnp.float32), 'attention_mask': jnp.ones((B, P), dtype=bool), 'Wq': jax.random.normal(ks[3], (D_MODEL, D_MODEL), dtype=jnp.float32) * s, 'bq': jnp.zeros((D_MODEL,), dtype=jnp.float32), 'Wk': jax.random.normal(ks[4], (D_MODEL, D_MODEL), dtype=jnp.float32) * s, 'bk': jnp.zeros((D_MODEL,), dtype=jnp.float32), 'Wv': jax.random.normal(ks[5], (D_MODEL, D_MODEL), dtype=jnp.float32) * s, 'bv': jnp.zeros((D_MODEL,), dtype=jnp.float32), 'Wo': jax.random.normal(ks[6], (D_MODEL, D_MODEL), dtype=jnp.float32) * s, 'bo': jnp.zeros((D_MODEL,), dtype=jnp.float32)}
        return inp
    _L1_xattn_all = _L1_xattn_setup()
    _L1_xattn_in = {k: v for k, v in _L1_xattn_all.items() if k in ('Wq', 'bq', 'Wk', 'bk', 'Wv', 'bv', 'Wo', 'bo')}
    del _L1_xattn_all

    def _L1_ffn_setup():
        import jax, jax.numpy as jnp
        import numpy as np
        TOP_K = 2
        EPS = 1e-20
        key = jax.random.key(seed)
        ks = jax.random.split(key, 8)
        B, S, H, E, D = (4, 256, 128, 8, 256)
        s = 0.02
        return {'x': jax.random.normal(ks[0], (B, S, H), dtype=jnp.float32), 'Wr': jax.random.normal(ks[1], (H, E), dtype=jnp.float32) * s, 'Wg': jax.random.normal(ks[2], (E, H, D), dtype=jnp.float32) * s, 'Wu': jax.random.normal(ks[3], (E, H, D), dtype=jnp.float32) * s, 'Wd': jax.random.normal(ks[4], (E, D, H), dtype=jnp.float32) * s, 'Sg': jax.random.normal(ks[5], (H, D), dtype=jnp.float32) * s, 'Su': jax.random.normal(ks[6], (H, D), dtype=jnp.float32) * s, 'Sd': jax.random.normal(ks[7], (D, H), dtype=jnp.float32) * s}
    _L1_ffn_all = _L1_ffn_setup()
    _L1_ffn_in = {k: v for k, v in _L1_ffn_all.items() if k in ('Wr', 'Wg', 'Wu', 'Wd', 'Sg', 'Su', 'Sd')}
    del _L1_ffn_all

    def _L2_attn_setup():
        import jax, jax.numpy as jnp
        import numpy as np
        S, B, E, H = (256, 2, 128, 16)
        D = E // H
        key = jax.random.key(seed)
        ks = jax.random.split(key, 8)
        x = jax.random.normal(ks[0], (S, B, E), dtype=jnp.float32)
        in_proj_weight = jax.random.normal(ks[1], (3 * E, E), dtype=jnp.float32) * 0.02
        in_proj_bias = jax.random.normal(ks[2], (3 * E,), dtype=jnp.float32) * 0.02
        gamma = 1.0 + jax.random.normal(ks[3], (1, 1, 3 * E), dtype=jnp.float32) * 0.1
        linear_alpha = 1.0 + jax.random.normal(ks[4], (1, 1, E), dtype=jnp.float32) * 0.1
        linear_gamma = 1.0 + jax.random.normal(ks[5], (1, 1, E), dtype=jnp.float32) * 0.1
        out_proj_weight = jax.random.normal(ks[6], (E, E), dtype=jnp.float32) * 0.02
        out_proj_bias = jax.random.normal(ks[7], (E,), dtype=jnp.float32) * 0.02
        return {'x': x, 'in_proj_weight': in_proj_weight, 'in_proj_bias': in_proj_bias, 'gamma': gamma, 'linear_alpha': linear_alpha, 'linear_gamma': linear_gamma, 'out_proj_weight': out_proj_weight, 'out_proj_bias': out_proj_bias}
    _L2_attn_all = _L2_attn_setup()
    _L2_attn_in = {k: v for k, v in _L2_attn_all.items() if k in ('in_proj_weight', 'in_proj_bias', 'gamma', 'linear_alpha', 'linear_gamma', 'out_proj_weight', 'out_proj_bias')}
    del _L2_attn_all

    def _L2_xattn_setup():
        import jax, jax.numpy as jnp
        import numpy as np
        import math
        NUM_HEAD = 16
        D_MODEL = 128
        BATCH = 2
        SEQ = 256

        def _split_heads(x):
            B, S, D = x.shape
            return x.reshape(B, S, NUM_HEAD, D // NUM_HEAD).transpose(0, 2, 1, 3)
        key = jax.random.key(seed)
        k1, k2, k3, k4 = jax.random.split(key, 4)
        scale = 1.0 / math.sqrt(D_MODEL)
        return {'query': jax.random.normal(k1, (BATCH, SEQ, D_MODEL), dtype=jnp.float32), 'key': jax.random.normal(k2, (BATCH, SEQ, D_MODEL), dtype=jnp.float32), 'value': jax.random.normal(k3, (BATCH, SEQ, D_MODEL), dtype=jnp.float32), 'w_concat': jax.random.normal(k4, (D_MODEL, D_MODEL), dtype=jnp.float32) * scale}
    _L2_xattn_all = _L2_xattn_setup()
    _L2_xattn_in = {k: v for k, v in _L2_xattn_all.items() if k in ('w_concat',)}
    del _L2_xattn_all

    def _L2_ffn_setup():
        import jax, jax.numpy as jnp
        import numpy as np
        BLOCK = 16
        _GRID = jnp.array([0.0, 0.5, 1.0, 1.5, 2.0, 3.0, 4.0, 6.0], dtype=jnp.float32)
        _MID = jnp.array([0.25, 0.75, 1.25, 1.75, 2.5, 3.5, 5.0], dtype=jnp.float32)

        def fp4_quant_dequant(x):
            shape = x.shape
            xb = x.reshape(shape[:-1] + (shape[-1] // BLOCK, BLOCK))
            scale = jnp.max(jnp.abs(xb), axis=-1, keepdims=True) / 6.0
            scale = jnp.maximum(scale, jnp.float32(1e-12))
            xn = xb / scale
            idx = jnp.searchsorted(_MID, jnp.abs(xn))
            q = _GRID[idx] * jnp.sign(xn) * scale
            return q.reshape(shape)

        def fp4_linear(x, w):
            xq = fp4_quant_dequant(x)
            wq = fp4_quant_dequant(w)
            return jnp.einsum('bsk,nk->bsn', xq, wq)
        key = jax.random.key(seed)
        k1, k2, k3, k4 = jax.random.split(key, 4)
        H, I = (128, 352)
        x = jax.random.normal(k1, (4, 512, H), dtype=jnp.float32)
        w_gate = jax.random.normal(k2, (I, H), dtype=jnp.float32) * 0.02
        w_up = jax.random.normal(k3, (I, H), dtype=jnp.float32) * 0.02
        w_down = jax.random.normal(k4, (H, I), dtype=jnp.float32) * 0.02
        return {'x': x, 'w_gate': w_gate, 'w_up': w_up, 'w_down': w_down}
    _L2_ffn_all = _L2_ffn_setup()
    _L2_ffn_in = {k: v for k, v in _L2_ffn_all.items() if k in ('w_gate', 'w_up', 'w_down')}
    del _L2_ffn_all

    def _L3_attn_setup():
        import jax, jax.numpy as jnp
        import numpy as np
        import math
        B, N, D = (2, 512, 128)
        NUM_LAYERS = 12
        INIT_RANGE = 0.02
        key = jax.random.key(seed)
        k1, k2 = jax.random.split(key)
        hidden_states = jax.random.normal(k1, (B, N, D), dtype=jnp.float32)
        std = INIT_RANGE / math.sqrt(2.0 * NUM_LAYERS * D)
        queries = jax.random.normal(k2, (D, D), dtype=jnp.float32) * std
        return {'hidden_states': hidden_states, 'queries': queries}
    _L3_attn_all = _L3_attn_setup()
    _L3_attn_in = {k: v for k, v in _L3_attn_all.items() if k in ('queries',)}
    del _L3_attn_all

    def _L3_xattn_setup():
        import jax, jax.numpy as jnp
        import numpy as np
        B, S, D, H = (2, 256, 128, 16)
        HD = D // H
        LN_EPS = 1e-05

        def _linear(x, w, b):
            return jnp.einsum('bsd,od->bso', x, w) + b

        def _split_heads(x):
            b, s, _ = x.shape
            return x.reshape(b, s, H, HD).transpose(0, 2, 1, 3)
        key = jax.random.key(seed)
        ks = jax.random.split(key, 14)
        w = 0.02
        return {'q': jax.random.normal(ks[0], (B, S, D), jnp.float32), 'k': jax.random.normal(ks[1], (B, S, D), jnp.float32), 'v': jax.random.normal(ks[2], (B, S, D), jnp.float32), 'mask': jnp.zeros((B, 1, S, S), dtype=bool), 'training': 0, 'wq_w': jax.random.normal(ks[3], (D, D), jnp.float32) * w, 'wq_b': jnp.zeros((D,), jnp.float32), 'wk_w': jax.random.normal(ks[4], (D, D), jnp.float32) * w, 'wk_b': jnp.zeros((D,), jnp.float32), 'wv_w': jax.random.normal(ks[5], (D, D), jnp.float32) * w, 'wv_b': jnp.zeros((D,), jnp.float32), 'wo_w': jax.random.normal(ks[6], (D, D), jnp.float32) * w, 'wo_b': jnp.zeros((D,), jnp.float32), 'ln_g': jnp.ones((D,), jnp.float32), 'ln_b': jnp.zeros((D,), jnp.float32)}
    _L3_xattn_all = _L3_xattn_setup()
    _L3_xattn_in = {k: v for k, v in _L3_xattn_all.items() if k in ('wq_w', 'wq_b', 'wk_w', 'wk_b', 'wv_w', 'wv_b', 'wo_w', 'wo_b', 'ln_g', 'ln_b')}
    del _L3_xattn_all

    def _L3_ffn_setup():
        import jax, jax.numpy as jnp
        import numpy as np
        N_EMBD = 128
        NUM_EXPERTS = 8
        TOP_K = 2

        def new_gelu(x):
            c = jnp.sqrt(2.0 / jnp.pi).astype(x.dtype)
            return 0.5 * x * (1.0 + jnp.tanh(c * (x + 0.044715 * x ** 3)))
        key = jax.random.key(seed)
        ks = jax.random.split(key, 6)
        C, E, H = (N_EMBD, NUM_EXPERTS, 4 * N_EMBD)
        x = jax.random.normal(ks[0], (4, 256, C), dtype=jnp.float32)
        router_w = 0.02 * jax.random.normal(ks[1], (E, C), dtype=jnp.float32)
        w1 = 0.02 * jax.random.normal(ks[2], (E, H, C), dtype=jnp.float32)
        b1 = jnp.zeros((E, H), dtype=jnp.float32)
        w2 = 0.02 * jax.random.normal(ks[3], (E, C, H), dtype=jnp.float32)
        b2 = jnp.zeros((E, C), dtype=jnp.float32)
        return {'x': x, 'router_w': router_w, 'w1': w1, 'b1': b1, 'w2': w2, 'b2': b2}
    _L3_ffn_all = _L3_ffn_setup()
    _L3_ffn_in = {k: v for k, v in _L3_ffn_all.items() if k in ('router_w', 'w1', 'b1', 'w2', 'b2')}
    del _L3_ffn_all
    return {'x': x, 'ctx_1024': ctx_1024, 'mask_Bx1xSxS2_ik1': mask_Bx1xSxS2_ik1, 'mask_BxS2_bf1': mask_BxS2_bf1, 'mask_Bx1xSxS2_bf0': mask_Bx1xSxS2_bf0, 'L0_attn_Wq': _L0_attn_in['Wq'], 'L0_attn_Wk': _L0_attn_in['Wk'], 'L0_attn_Wv': _L0_attn_in['Wv'], 'L0_attn_Wo': _L0_attn_in['Wo'], 'L0_attn_lambda_q1': _L0_attn_in['lambda_q1'], 'L0_attn_lambda_k1': _L0_attn_in['lambda_k1'], 'L0_attn_lambda_q2': _L0_attn_in['lambda_q2'], 'L0_attn_lambda_k2': _L0_attn_in['lambda_k2'], 'L0_xattn_W_fc': _L0_xattn_in['W_fc'], 'L0_xattn_b_fc': _L0_xattn_in['b_fc'], 'L0_ffn_w_router': _L0_ffn_in['w_router'], 'L0_ffn_W1': _L0_ffn_in['W1'], 'L0_ffn_b1': _L0_ffn_in['b1'], 'L0_ffn_W2': _L0_ffn_in['W2'], 'L0_ffn_b2': _L0_ffn_in['b2'], 'L0_ffn_Ws1': _L0_ffn_in['Ws1'], 'L0_ffn_bs1': _L0_ffn_in['bs1'], 'L0_ffn_Ws2': _L0_ffn_in['Ws2'], 'L0_ffn_bs2': _L0_ffn_in['bs2'], 'L1_attn_W_qkv': _L1_attn_in['W_qkv'], 'L1_attn_b_qkv': _L1_attn_in['b_qkv'], 'L1_attn_W_out': _L1_attn_in['W_out'], 'L1_attn_b_out': _L1_attn_in['b_out'], 'L1_attn_w_sur': _L1_attn_in['w_sur'], 'L1_attn_b_sur': _L1_attn_in['b_sur'], 'L1_attn_threshold': _L1_attn_in['threshold'], 'L1_xattn_Wq': _L1_xattn_in['Wq'], 'L1_xattn_bq': _L1_xattn_in['bq'], 'L1_xattn_Wk': _L1_xattn_in['Wk'], 'L1_xattn_bk': _L1_xattn_in['bk'], 'L1_xattn_Wv': _L1_xattn_in['Wv'], 'L1_xattn_bv': _L1_xattn_in['bv'], 'L1_xattn_Wo': _L1_xattn_in['Wo'], 'L1_xattn_bo': _L1_xattn_in['bo'], 'L1_ffn_Wr': _L1_ffn_in['Wr'], 'L1_ffn_Wg': _L1_ffn_in['Wg'], 'L1_ffn_Wu': _L1_ffn_in['Wu'], 'L1_ffn_Wd': _L1_ffn_in['Wd'], 'L1_ffn_Sg': _L1_ffn_in['Sg'], 'L1_ffn_Su': _L1_ffn_in['Su'], 'L1_ffn_Sd': _L1_ffn_in['Sd'], 'L2_attn_in_proj_weight': _L2_attn_in['in_proj_weight'], 'L2_attn_in_proj_bias': _L2_attn_in['in_proj_bias'], 'L2_attn_gamma': _L2_attn_in['gamma'], 'L2_attn_linear_alpha': _L2_attn_in['linear_alpha'], 'L2_attn_linear_gamma': _L2_attn_in['linear_gamma'], 'L2_attn_out_proj_weight': _L2_attn_in['out_proj_weight'], 'L2_attn_out_proj_bias': _L2_attn_in['out_proj_bias'], 'L2_xattn_w_concat': _L2_xattn_in['w_concat'], 'L2_ffn_w_gate': _L2_ffn_in['w_gate'], 'L2_ffn_w_up': _L2_ffn_in['w_up'], 'L2_ffn_w_down': _L2_ffn_in['w_down'], 'L3_attn_queries': _L3_attn_in['queries'], 'L3_xattn_wq_w': _L3_xattn_in['wq_w'], 'L3_xattn_wq_b': _L3_xattn_in['wq_b'], 'L3_xattn_wk_w': _L3_xattn_in['wk_w'], 'L3_xattn_wk_b': _L3_xattn_in['wk_b'], 'L3_xattn_wv_w': _L3_xattn_in['wv_w'], 'L3_xattn_wv_b': _L3_xattn_in['wv_b'], 'L3_xattn_wo_w': _L3_xattn_in['wo_w'], 'L3_xattn_wo_b': _L3_xattn_in['wo_b'], 'L3_xattn_ln_g': _L3_xattn_in['ln_g'], 'L3_xattn_ln_b': _L3_xattn_in['ln_b'], 'L3_ffn_router_w': _L3_ffn_in['router_w'], 'L3_ffn_w1': _L3_ffn_in['w1'], 'L3_ffn_b1': _L3_ffn_in['b1'], 'L3_ffn_w2': _L3_ffn_in['w2'], 'L3_ffn_b2': _L3_ffn_in['b2']}

def reference(x, ctx_1024, mask_Bx1xSxS2_ik1, mask_BxS2_bf1, mask_Bx1xSxS2_bf0, L0_attn_Wq, L0_attn_Wk, L0_attn_Wv, L0_attn_Wo, L0_attn_lambda_q1, L0_attn_lambda_k1, L0_attn_lambda_q2, L0_attn_lambda_k2, L0_xattn_W_fc, L0_xattn_b_fc, L0_ffn_w_router, L0_ffn_W1, L0_ffn_b1, L0_ffn_W2, L0_ffn_b2, L0_ffn_Ws1, L0_ffn_bs1, L0_ffn_Ws2, L0_ffn_bs2, L1_attn_W_qkv, L1_attn_b_qkv, L1_attn_W_out, L1_attn_b_out, L1_attn_w_sur, L1_attn_b_sur, L1_attn_threshold, L1_xattn_Wq, L1_xattn_bq, L1_xattn_Wk, L1_xattn_bk, L1_xattn_Wv, L1_xattn_bv, L1_xattn_Wo, L1_xattn_bo, L1_ffn_Wr, L1_ffn_Wg, L1_ffn_Wu, L1_ffn_Wd, L1_ffn_Sg, L1_ffn_Su, L1_ffn_Sd, L2_attn_in_proj_weight, L2_attn_in_proj_bias, L2_attn_gamma, L2_attn_linear_alpha, L2_attn_linear_gamma, L2_attn_out_proj_weight, L2_attn_out_proj_bias, L2_xattn_w_concat, L2_ffn_w_gate, L2_ffn_w_up, L2_ffn_w_down, L3_attn_queries, L3_xattn_wq_w, L3_xattn_wq_b, L3_xattn_wk_w, L3_xattn_wk_b, L3_xattn_wv_w, L3_xattn_wv_b, L3_xattn_wo_w, L3_xattn_wo_b, L3_xattn_ln_g, L3_xattn_ln_b, L3_ffn_router_w, L3_ffn_w1, L3_ffn_b1, L3_ffn_w2, L3_ffn_b2):
    import jax
    import jax.numpy as jnp

    def _L0_attn_ref(x, Wq, Wk, Wv, Wo, lambda_q1, lambda_k1, lambda_q2, lambda_k2):
        import jax, jax.numpy as jnp
        import numpy as np
        import math
        B, T, E = (1, 256, 128)
        H = 8
        D = E // H // 2
        LAMBDA_INIT = 0.8 - 0.6 * math.exp(-0.3 * 1)
        SCALE_BASE = 512.0
        THETA = 10000.0

        def _rope_tables(T, d):
            inv_freq = 1.0 / THETA ** (jnp.arange(0, d, 2, dtype=jnp.float32) / d)
            pos = jnp.arange(T, dtype=jnp.float32)
            freqs = pos[:, None] * inv_freq[None, :]
            freqs = jnp.repeat(freqs, 2, axis=-1)
            sv = (jnp.arange(0, d, 2, dtype=jnp.float32) + 0.4 * d) / (1.4 * d)
            power = (pos - T // 2) / SCALE_BASE
            scale = sv[None, :] ** power[:, None]
            scale = jnp.concatenate([scale, scale], axis=-1)
            return (freqs, scale)

        def _rotate_half(x):
            x1 = x[..., 0::2]
            x2 = x[..., 1::2]
            return jnp.stack([-x2, x1], axis=-1).reshape(x.shape)

        def _apply_rope(t, freqs, scale):
            f = freqs[None, :, None, :]
            s = scale[None, :, None, :]
            return t * jnp.cos(f) * s + _rotate_half(t) * jnp.sin(f) * s
        b, t, e = x.shape
        scaling = D ** (-0.5)
        q = (x @ Wq.T).reshape(b, t, 2 * H, D)
        k = (x @ Wk.T).reshape(b, t, 2 * H, D)
        v = (x @ Wv.T).reshape(b, t, H, 2 * D)
        freqs, scale = _rope_tables(t, D)
        q = _apply_rope(q, freqs, scale)
        k = _apply_rope(k, freqs, 1.0 / scale)
        q = jnp.transpose(q, (0, 2, 1, 3)) * scaling
        k = jnp.transpose(k, (0, 2, 1, 3))
        v = jnp.transpose(v, (0, 2, 1, 3))
        scores = jnp.einsum('bhtd,bhsd->bhts', q, k)
        probs = jax.nn.softmax(scores.astype(jnp.float32), axis=-1).astype(scores.dtype)
        lam1 = jnp.exp(jnp.sum(lambda_q1 * lambda_k1))
        lam2 = jnp.exp(jnp.sum(lambda_q2 * lambda_k2))
        lam = lam1 - lam2 + LAMBDA_INIT
        probs = probs.reshape(b, H, 2, t, t)
        diff = probs[:, :, 0] - lam * probs[:, :, 1]
        attn = jnp.einsum('bhts,bhsd->bhtd', diff, v)
        attn = attn * jax.lax.rsqrt(jnp.mean(attn * attn, axis=-1, keepdims=True) + 1e-05)
        attn = attn * (1.0 - LAMBDA_INIT)
        attn = jnp.transpose(attn, (0, 2, 1, 3)).reshape(b, t, e)
        return attn @ Wo.T

    def _L0_xattn_ref(value, key, query, mask, W_fc, b_fc):
        import jax, jax.numpy as jnp
        import numpy as np
        EMBED = 128
        HEADS = 16
        HEAD_DIM = EMBED // HEADS
        N, Sq, E = query.shape
        Sk = key.shape[1]
        Sv = value.shape[1]
        v = value.reshape(N, Sv, HEADS, HEAD_DIM)
        k = key.reshape(N, Sk, HEADS, HEAD_DIM)
        q = query.reshape(N, Sq, HEADS, HEAD_DIM)
        energy = jnp.einsum('nqhd,nkhd->nhqk', q, k)
        energy = jnp.where(mask == 0, jnp.float32(-1e+20), energy)
        attention = jax.nn.softmax(energy / jnp.sqrt(jnp.float32(E)), axis=3)
        out = jnp.einsum('nhql,nlhd->nqhd', attention, v).reshape(N, Sq, E)
        out = out @ W_fc.T + b_fc
        return out

    def _L0_ffn_ref(x, w_router, W1, b1, W2, b2, Ws1, bs1, Ws2, bs2):
        import jax, jax.numpy as jnp
        import numpy as np
        import math
        D_MODEL, D_FF, N_EXPERTS, TOP_K, N_SHARED = (128, 512, 8, 2, 1)
        B, T = (4, 128)
        SCALE = 1.0 / math.sqrt(N_SHARED + TOP_K / N_EXPERTS)
        logits = jnp.einsum('btd,ed->bte', x, w_router)
        probs = jax.nn.softmax(logits, axis=-1)
        vals, idx = jax.lax.top_k(probs, TOP_K)
        gates = jnp.sum(jax.nn.one_hot(idx, N_EXPERTS, dtype=x.dtype) * vals[..., None], axis=-2)
        hs = jax.nn.gelu(jnp.einsum('btd,fd->btf', x, Ws1) + bs1)
        acc = jnp.einsum('btf,df->btd', hs, Ws2) + bs2
        h = jax.nn.gelu(jnp.einsum('btd,efd->btef', x, W1) + b1)
        y = jnp.einsum('btef,edf->bted', h, W2) + b2
        acc = acc + jnp.einsum('bted,bte->btd', y, gates)
        return SCALE * acc

    def _L1_attn_ref(x, W_qkv, b_qkv, W_out, b_out, w_sur, b_sur, threshold):
        import jax, jax.numpy as jnp
        import numpy as np
        B, T, C, H = (4, 128, 128, 16)
        D = C // H

        def _expmap0_split(u):
            mink = -u[..., :1] ** 2 + jnp.sum(u[..., 1:] ** 2, axis=-1, keepdims=True)
            nomin = jnp.sqrt(jnp.maximum(mink, 1e-08))
            time = jnp.cosh(nomin)
            space = jnp.sinh(nomin) * u[..., 1:] / nomin
            return (time, space)
        Bx, Tx, Cx = x.shape
        importance = jax.nn.sigmoid(jnp.einsum('btc,c->bt', x, w_sur) + b_sur)
        spikes = (importance > threshold).astype(x.dtype)
        spike_mask = spikes[:, None, :, None]
        qkv = x @ W_qkv + b_qkv
        qkv = qkv.reshape(Bx, Tx, 3, H, D).transpose(2, 0, 3, 1, 4)
        q, k, v = (qkv[0], qkv[1], qkv[2])
        tq, sq = _expmap0_split(q)
        tk, sk = _expmap0_split(k)
        neg_inner = jnp.einsum('bhie,bhje->bhij', tq, tk) - jnp.einsum('bhid,bhjd->bhij', sq, sk)
        dist = jnp.arccosh(jnp.maximum(neg_inner, 1.0 + 1e-07))
        scores = -dist ** 2 / np.sqrt(D)
        causal = jnp.tril(jnp.ones((Tx, Tx), dtype=bool))
        scores = jnp.where(causal[None, None], scores, -jnp.inf)
        attn = jax.nn.softmax(scores, axis=-1) * spike_mask
        y = jnp.einsum('bhij,bhjd->bhid', attn, v)
        y = y.transpose(0, 2, 1, 3).reshape(Bx, Tx, Cx)
        return y @ W_out + b_out

    def _L1_xattn_ref(q, k, v, attention_mask, Wq, bq, Wk, bk, Wv, bv, Wo, bo):
        import jax, jax.numpy as jnp
        import numpy as np
        N_HEADS = 16
        D_MODEL = 128
        HEAD_DIM = D_MODEL // N_HEADS
        MASK_FILL = -100000000.0

        def _split_heads(x):
            B, S, _ = x.shape
            return x.reshape(B, S, N_HEADS, HEAD_DIM).transpose(0, 2, 1, 3)
        qm = _split_heads(q @ Wq.T + bq)
        km = _split_heads(k @ Wk.T + bk)
        vm = _split_heads(v @ Wv.T + bv)
        scores = jnp.einsum('bnlh,bnph->bnlp', qm, km) / np.sqrt(HEAD_DIM).astype(np.float32)
        mask = attention_mask[:, None, None, :]
        scores = jnp.where(mask, scores, MASK_FILL)
        attn = jax.nn.softmax(scores, axis=-1)
        out = jnp.einsum('bnlp,bnph->bnlh', attn, vm)
        B, _, L, _ = out.shape
        out = out.transpose(0, 2, 1, 3).reshape(B, L, D_MODEL)
        return out @ Wo.T + bo

    def _L1_ffn_ref(x, Wr, Wg, Wu, Wd, Sg, Su, Sd):
        import jax, jax.numpy as jnp
        import numpy as np
        TOP_K = 2
        EPS = 1e-20
        B, S, H = x.shape
        T = B * S
        xt = x.reshape(T, H)
        scores = jax.nn.softmax(xt @ Wr, axis=-1)
        topk_w, topk_idx = jax.lax.top_k(scores, TOP_K)
        topk_w = topk_w / (topk_w.sum(axis=-1, keepdims=True) + EPS)
        g = jax.nn.silu(jnp.einsum('th,ehd->etd', xt, Wg))
        u = jnp.einsum('th,ehd->etd', xt, Wu)
        out_all = jnp.einsum('etd,edh->eth', g * u, Wd)
        tok = jnp.arange(T)[:, None]
        gathered = out_all[topk_idx, tok, :]
        out = jnp.sum(gathered * topk_w[..., None], axis=1).reshape(B, S, H)
        shared = jax.nn.silu(x @ Sg) * (x @ Su) @ Sd
        return out + shared

    def _L2_attn_ref(x, in_proj_weight, in_proj_bias, gamma, linear_alpha, linear_gamma, out_proj_weight, out_proj_bias):
        import jax, jax.numpy as jnp
        import numpy as np
        S, B, E, H = (256, 2, 128, 16)
        D = E // H
        s, b, e = x.shape
        qkv = jnp.einsum('sbe,fe->sbf', x, in_proj_weight) + in_proj_bias
        qkv = qkv * gamma
        q, k, v = jnp.split(qkv, 3, axis=-1)

        def to_heads(t):
            return t.reshape(s, b * H, D).transpose(1, 0, 2)
        q, k, v = (to_heads(q), to_heads(k), to_heads(v))
        q = q / jnp.sqrt(jnp.asarray(D, dtype=q.dtype))
        scores = jnp.einsum('bsd,btd->bst', q, k)
        causal = jnp.tril(jnp.ones((s, s), dtype=bool))
        scores = jnp.where(causal[None], scores, jnp.asarray(-jnp.inf, scores.dtype))
        attn = jax.nn.softmax(scores, axis=-1)
        out = jnp.einsum('bst,btd->bsd', attn, v)
        out = out.transpose(1, 0, 2).reshape(s, b, e)
        out = out * linear_alpha
        out = jnp.einsum('sbe,fe->sbf', out, out_proj_weight) + out_proj_bias
        out = out * linear_gamma
        return out

    def _L2_xattn_ref(query, key, value, w_concat):
        import jax, jax.numpy as jnp
        import numpy as np
        import math
        NUM_HEAD = 16
        D_MODEL = 128
        BATCH = 2
        SEQ = 256

        def _split_heads(x):
            B, S, D = x.shape
            return x.reshape(B, S, NUM_HEAD, D // NUM_HEAD).transpose(0, 2, 1, 3)
        q = _split_heads(query)
        k = _split_heads(key)
        v = _split_heads(value)
        d_k = q.shape[-1]
        scores = jnp.einsum('bhqd,bhkd->bhqk', q, k) / math.sqrt(d_k)
        attn = jax.nn.softmax(scores, axis=-1)
        ctx = jnp.einsum('bhqk,bhkd->bhqd', attn, v)
        B, H, S, dk = ctx.shape
        x = ctx.transpose(0, 2, 1, 3).reshape(B, S, H * dk)
        return x @ w_concat.T

    def _L2_ffn_ref(x, w_gate, w_up, w_down):
        import jax, jax.numpy as jnp
        import numpy as np
        BLOCK = 16
        _GRID = jnp.array([0.0, 0.5, 1.0, 1.5, 2.0, 3.0, 4.0, 6.0], dtype=jnp.float32)
        _MID = jnp.array([0.25, 0.75, 1.25, 1.75, 2.5, 3.5, 5.0], dtype=jnp.float32)

        def fp4_quant_dequant(x):
            shape = x.shape
            xb = x.reshape(shape[:-1] + (shape[-1] // BLOCK, BLOCK))
            scale = jnp.max(jnp.abs(xb), axis=-1, keepdims=True) / 6.0
            scale = jnp.maximum(scale, jnp.float32(1e-12))
            xn = xb / scale
            idx = jnp.searchsorted(_MID, jnp.abs(xn))
            q = _GRID[idx] * jnp.sign(xn) * scale
            return q.reshape(shape)

        def fp4_linear(x, w):
            xq = fp4_quant_dequant(x)
            wq = fp4_quant_dequant(w)
            return jnp.einsum('bsk,nk->bsn', xq, wq)
        gate = fp4_linear(x, w_gate)
        y = fp4_linear(x, w_up)
        h = jax.nn.silu(gate) * y
        return fp4_linear(h, w_down)

    def _L3_attn_ref(hidden_states, queries):
        import jax, jax.numpy as jnp
        import numpy as np
        import math
        B, N, D = (2, 512, 128)
        NUM_LAYERS = 12
        INIT_RANGE = 0.02
        q = jnp.einsum('bnd,ed->bne', hidden_states, queries)
        pre_attn = jnp.einsum('bne,bme->bnm', q, hidden_states)
        attention = jnp.einsum('bnm,bmd->bnd', pre_attn, hidden_states)
        return attention

    def _L3_xattn_ref(q, k, v, mask, training, wq_w, wq_b, wk_w, wk_b, wv_w, wv_b, wo_w, wo_b, ln_g, ln_b):
        import jax, jax.numpy as jnp
        import numpy as np
        B, S, D, H = (2, 256, 128, 16)
        HD = D // H
        LN_EPS = 1e-05

        def _linear(x, w, b):
            return jnp.einsum('bsd,od->bso', x, w) + b

        def _split_heads(x):
            b, s, _ = x.shape
            return x.reshape(b, s, H, HD).transpose(0, 2, 1, 3)
        residual = q
        Q = _split_heads(_linear(q, wq_w, wq_b))
        K = _split_heads(_linear(k, wk_w, wk_b))
        V = _split_heads(_linear(v, wv_w, wv_b))
        dk = jnp.sqrt(jnp.asarray(HD, jnp.float16)).astype(jnp.float32) + 1e-08
        score = jnp.einsum('bhqd,bhkd->bhqk', Q, K) / dk
        attn = jnp.where(mask, -jnp.inf, score)
        ctx = jnp.einsum('bhqk,bhkd->bhqd', attn, V)
        b, _, s, _ = ctx.shape
        ctx = ctx.transpose(0, 2, 1, 3).reshape(b, s, D)
        o = _linear(ctx, wo_w, wo_b)
        x = residual + o
        mu = jnp.mean(x, axis=-1, keepdims=True)
        var = jnp.mean(jnp.square(x - mu), axis=-1, keepdims=True)
        return ln_g * (x - mu) * jax.lax.rsqrt(var + LN_EPS) + ln_b

    def _L3_ffn_ref(x, router_w, w1, b1, w2, b2):
        import jax, jax.numpy as jnp
        import numpy as np
        N_EMBD = 128
        NUM_EXPERTS = 8
        TOP_K = 2

        def new_gelu(x):
            c = jnp.sqrt(2.0 / jnp.pi).astype(x.dtype)
            return 0.5 * x * (1.0 + jnp.tanh(c * (x + 0.044715 * x ** 3)))
        B, T, C = x.shape
        E = router_w.shape[0]
        x_flat = x.reshape(B * T, C)
        router_logits = x_flat @ router_w.T
        router_probs = jax.nn.softmax(router_logits, axis=-1)
        top_k_probs, top_k_idx = jax.lax.top_k(router_probs, TOP_K)
        top_k_probs = top_k_probs / (top_k_probs.sum(axis=-1, keepdims=True) + 1e-08)
        cw = (jax.nn.one_hot(top_k_idx, E, dtype=x.dtype) * top_k_probs[..., None]).sum(axis=1)
        output = jnp.zeros_like(x_flat)
        for e in range(E):
            h = new_gelu(x_flat @ w1[e].T + b1[e])
            out_e = h @ w2[e].T + b2[e]
            output = output + cw[:, e:e + 1] * out_e
        return output.reshape(B, T, C)
    x = x + _L0_attn_ref(_layernorm(x, axis=-1), L0_attn_Wq, L0_attn_Wk, L0_attn_Wv, L0_attn_Wo, L0_attn_lambda_q1, L0_attn_lambda_k1, L0_attn_lambda_q2, L0_attn_lambda_k2)
    x = x + _L0_xattn_ref(ctx_1024, ctx_1024, _layernorm(x, axis=-1), mask_Bx1xSxS2_ik1, L0_xattn_W_fc, L0_xattn_b_fc)
    x = x + _L0_ffn_ref(_layernorm(x, axis=-1), L0_ffn_w_router, L0_ffn_W1, L0_ffn_b1, L0_ffn_W2, L0_ffn_b2, L0_ffn_Ws1, L0_ffn_bs1, L0_ffn_Ws2, L0_ffn_bs2)
    x = x + _L1_attn_ref(_layernorm(x, axis=-1), L1_attn_W_qkv, L1_attn_b_qkv, L1_attn_W_out, L1_attn_b_out, L1_attn_w_sur, L1_attn_b_sur, L1_attn_threshold)
    x = x + _L1_xattn_ref(_layernorm(x, axis=-1), ctx_1024, ctx_1024, mask_BxS2_bf1, L1_xattn_Wq, L1_xattn_bq, L1_xattn_Wk, L1_xattn_bk, L1_xattn_Wv, L1_xattn_bv, L1_xattn_Wo, L1_xattn_bo)
    x = x + _L1_ffn_ref(_layernorm(x, axis=-1), L1_ffn_Wr, L1_ffn_Wg, L1_ffn_Wu, L1_ffn_Wd, L1_ffn_Sg, L1_ffn_Su, L1_ffn_Sd)
    x = x + _L2_attn_ref(_layernorm(x, axis=-1), L2_attn_in_proj_weight, L2_attn_in_proj_bias, L2_attn_gamma, L2_attn_linear_alpha, L2_attn_linear_gamma, L2_attn_out_proj_weight, L2_attn_out_proj_bias)
    x = x + _L2_xattn_ref(_layernorm(x, axis=-1), ctx_1024, ctx_1024, L2_xattn_w_concat)
    x = x + _L2_ffn_ref(_layernorm(x, axis=-1), L2_ffn_w_gate, L2_ffn_w_up, L2_ffn_w_down)
    x = x + _L3_attn_ref(_layernorm(x, axis=-1), L3_attn_queries)
    x = x + _L3_xattn_ref(_layernorm(x, axis=-1), ctx_1024, ctx_1024, mask_Bx1xSxS2_bf0, 0, L3_xattn_wq_w, L3_xattn_wq_b, L3_xattn_wk_w, L3_xattn_wk_b, L3_xattn_wv_w, L3_xattn_wv_b, L3_xattn_wo_w, L3_xattn_wo_b, L3_xattn_ln_g, L3_xattn_ln_b)
    x = x + _L3_ffn_ref(_layernorm(x, axis=-1), L3_ffn_router_w, L3_ffn_w1, L3_ffn_b1, L3_ffn_w2, L3_ffn_b2)
    return x

_drawn_inputs = setup_inputs


def setup_inputs(seed=0):
    import zlib

    import numpy as np

    out = dict(_drawn_inputs(seed))
    spreads = {'L1_attn_b_qkv': (0.0, 0.1),
     'L1_attn_b_out': (0.0, 0.1),
     'L1_xattn_bq': (0.0, 0.301),
     'L1_xattn_bk': (0.0, 2.0),
     'L1_xattn_bv': (0.0, 0.1),
     'L1_xattn_bo': (0.0, 0.1),
     'L3_xattn_wq_b': (0.0, 0.8),
     'L3_xattn_wk_b': (0.0, 0.511),
     'L3_xattn_wv_b': (0.0, 0.594),
     'L3_xattn_wo_b': (0.0, 2.0),
     'L3_xattn_ln_g': (1.0, 0.6),
     'L3_xattn_ln_b': (0.0, 2.0),
     'L3_ffn_b1': (0.0, 0.8),
     'L3_ffn_b2': (0.0, 2.0)}
    factors = {'L0_attn_lambda_q1': 8.0,
     'L0_attn_lambda_k1': 8.0,
     'L0_attn_lambda_q2': 8.0,
     'L0_attn_lambda_k2': 8.0,
     'L0_ffn_b1': 7.187,
     'L0_ffn_b2': 3.752,
     'L1_ffn_Wr': 8.0,
     'L1_ffn_Wg': 8.0,
     'L1_ffn_Wu': 8.0,
     'L1_ffn_Wd': 8.0,
     'L1_ffn_Sg': 7.908,
     'L1_ffn_Su': 7.651,
     'L1_ffn_Sd': 7.592,
     'L2_attn_in_proj_bias': 7.118,
     'L2_attn_gamma': 8.0,
     'L2_attn_linear_alpha': 8.0,
     'L2_attn_linear_gamma': 8.0,
     'L2_ffn_w_gate': 6.523,
     'L2_ffn_w_up': 6.006,
     'L2_ffn_w_down': 5.767,
     'L3_ffn_router_w': 4.372,
     'L3_ffn_w1': 8.0,
     'L3_ffn_w2': 7.398,
     'L2_attn_out_proj_bias': 5.101,
     'L3_xattn_wq_w': 2.727,
     'L3_xattn_wk_w': 3.792,
     'L3_xattn_wv_w': 3.124,
     'L3_xattn_wo_w': 2.744}
    for name, (base, spread) in spreads.items():
        noise = np.random.default_rng([zlib.crc32(name.encode()), seed]).standard_normal(out[name].shape)
        drawn = base * np.exp(spread * noise) if base else spread * noise
        out[name] = jnp.asarray(drawn.astype(out[name].dtype))
    for name, factor in factors.items():
        out[name] = (out[name] * factor).astype(out[name].dtype)
    return out
```

```python
from contextlib import ExitStack

import numpy as np
import concourse.bass as bass
from concourse import mybir

ALU = mybir.AluOpType
ACT = mybir.ActivationFunctionType
AX = mybir.AxisListType.X
F32 = mybir.dt.float32
BF16 = mybir.dt.bfloat16
I32 = mybir.dt.int32
U8 = mybir.dt.uint8

P = 128
B, S, S2, E = 4, 256, 512, 128
H, D = 16, 8
TPB = S // P
NT = B * TPB
NC = B * S2 // P
TOK = B * S
CTX = B * S2
PAIRS = H // 2
SLOT = 64
PARTS = [(0, 0), (0, 1), (1, 0), (1, 1), (0, 2), (2, 0)]
ROW_MASK = len(PARTS) * D
ROW_MAX = ROW_MASK + 1
K_SCORE = ROW_MASK + 1
K_EXP = ROW_MAX + 3
BIG = float(2 ** 66)
LN_EPS = 1e-5
NE = 8
FH = 512
FJ = FH // P
F1 = 256
F1J = F1 // P
F2 = 352
F2J = (F2 + P - 1) // P
FP4_BLOCK = 16
DV0 = 16
H0 = 8
LAMBDA_INIT = 0.8 - 0.6 * float(np.exp(-0.3))
MOE_SCALE = 1.0 / float(np.sqrt(1 + 2 / NE))
RSQRT8 = 1.0 / float(np.sqrt(8.0))
RSQRT128 = 1.0 / float(np.sqrt(128.0))
DK3 = float(np.float32(np.sqrt(np.float16(8.0)))) + 1e-8


def columns(parts):
    at, n = {}, 0
    for name, width in parts:
        at[name] = (n, width)
        n += width
    return at, n


KEEP_AT, KEEP_N = columns([
    ("ident", P), ("blockdiag", P), ("rev", NE),
    ("L0x_fcT", E), ("L0f_router", NE), ("L1a_qkv", 3 * E + 1), ("L1a_out", E),
    ("L1x_qT", E), ("L1x_kT", E), ("L1x_vT", E), ("L1x_oT", E), ("L1f_router", NE),
    ("L2a_inT", 3 * E), ("L2a_outT", E), ("L2x_T", E), ("L3a_q", E),
    ("L3x_qT", E), ("L3x_kvT", 2 * E), ("L3x_oT", E), ("L3f_router", NE),
    ("L0f_b1", NE * FJ), ("L0f_bs1", FJ), ("L3f_b1", NE * FJ),
    ("L1x_bq", 1), ("L1x_bk", 1), ("L3x_bq", 1),
])
L0A_AT, L0A_N = columns([("qT", E), ("qpT", E), ("kT", E), ("kpT", E), ("vT", E), ("oT", E),
                         ("qcos", S), ("qsin", S), ("kcos", S), ("ksin", S)])
ROW_AT, ROW_N = columns([
    ("L0x_b", E), ("L1a_bqkv", 3 * E + 1), ("L1a_bout", E), ("L1x_bv", E), ("L1x_bo", E),
    ("L2a_bin", 3 * E), ("L2a_gamma", 3 * E), ("L2a_alpha", E), ("L2a_bout", E), ("L2a_lgamma", E),
    ("L3x_bkv", 2 * E), ("L3x_bo", E), ("L3x_g", E), ("L3x_b", E),
    ("lq1", D), ("lk1", D), ("lq2", D), ("lk2", D), ("thr", 1),
])
FFN_N = 9 * FH + 9 * FJ * E


class Lane:

    def __init__(self, engine, sem):
        self.engine, self.sem, self.count, self.seen = engine, sem, 0, {}

    def mark(self, instruction):
        instruction.then_inc(self.sem, 1)
        self.count += 1
        return (self.sem, self.count)

    def wait(self, *marks):
        for sem, value in marks:
            if self.seen.get(id(sem), 0) < value:
                self.engine.wait_ge(sem, value)
                self.seen[id(sem)] = value

    def step(self, instruction):
        m = self.mark(instruction)
        self.wait(m)
        return m


class Transfers:

    def __init__(self, sem):
        self.sem, self.count = sem, 0

    def start(self, lane, dst, src):
        lane.engine.dma_start(dst, src).then_inc(self.sem, 16)
        self.count += 16

    def done(self):
        return (self.sem, self.count)


class Slot:

    def __init__(self, ap):
        self.ap, self.freed = ap, ()


class Ring:
    def __init__(self, slots):
        self.slots, self.n = slots, 0

    def take(self, lane):
        slot = self.slots[self.n % len(self.slots)]
        self.n += 1
        lane.wait(*slot.freed)
        return slot


def decoder(nc, d, out, stop_after="L3f"):
    with ExitStack() as ctx:
        build(nc, d, out, ctx, stop_after)


def build(nc, d, out, ctx, stop_after):
    def sb(name, shape, dt=F32):
        return ctx.enter_context(nc.sbuf_tensor(name, shape, dt))

    every_transfer = []

    def transfers(name):
        t = Transfers(ctx.enter_context(nc.semaphore("dma_" + name)))
        every_transfer.append(t)
        return t

    def lane(engine, name):
        return Lane(engine, ctx.enter_context(nc.semaphore(name)))

    pe, dve, act, pool, sp = nc.tensor, nc.vector, nc.scalar, nc.gpsimd, nc.sync
    PE, V, A, G, Q = (lane(pe, "pe_done"), lane(dve, "dve_done"), lane(act, "act_done"),
                      lane(pool, "pool_done"), lane(sp, "sp_done"))

    x = sb("x", [P, NT, E])
    xn = sb("xn", [P, NT, E])
    xnT = sb("xnT", [P, TOK])
    qT = sb("qT", [P, TOK])
    q_stack = sb("q_stack", [P, B, PAIRS, S], BF16)
    self_stack = sb("self_stack", [P, PAIRS, TOK], BF16)
    ctx_stack = sb("ctx_stack", [P, PAIRS, CTX], BF16)
    parts = sb("parts", [P, 3, TOK], BF16)
    ffn_w = sb("ffn_w", [P, FFN_N])
    keep = sb("keep", [P, KEEP_N])
    rows = sb("rows", [P, ROW_N])
    vaug = sb("vaug", [P, NC, H * (D + 1)])
    work = sb("work", [P, 12288])
    kv3 = sb("kv3", [P, B, E])
    ident_b = sb("ident_b", [P, P], BF16)
    far_b = sb("far_b", [P, P], BF16)
    stats = sb("stats", [P, NT, 6])
    mv = sb("mv", [P, NT, 2])
    rstd = sb("rstd", [P, NT])
    mx = sb("mx", [P, B, 2, PAIRS, TPB])
    mparts = sb("mparts", [P, 3, 2 * TPB * PAIRS], BF16)
    mT = sb("mT", [96, B, P], BF16)
    rsum = sb("rsum", [P, TPB, H])
    gates = sb("gates", [P, NT, NE + 1])
    gatesT = parts[:].rearrange("p s t -> p (s t)").bitcast(F32)[0:NE + 1, 0:TOK]
    b2 = sb("b2", [NE + 1, 2, E])
    small = sb("small", [P, 4, 2 * TPB * PAIRS])
    lam = sb("lam", [P, 8])
    lam8 = sb("lam8", [P, 2, D])
    minus1 = sb("minus1", [P, 1])
    halves = sb("halves", [P, 2])
    maskrow = sb("maskrow", [NC, P], BF16)
    masku8 = sb("masku8", [NC, P], U8)
    spike = sb("spike", [P, NT])
    cm = sb("cm", [P, NT])

    def kp(name, lo=0, n=None):
        a, w = KEEP_AT[name]
        return keep[:, a + lo:a + lo + (w - lo if n is None else n)]

    def rw(name):
        a, w = ROW_AT[name]
        return rows[:, a:a + w]

    def l0w(name):
        a, w = L0A_AT[name]
        return ffn_w[:, a:a + w]

    def wk(lo, n):
        return work[:, lo:lo + n]

    ps_a = [ctx.enter_context(nc.psum_tensor(f"ps_a{i}", [P, 512], F32)) for i in range(2)]
    ps_t = [ctx.enter_context(nc.psum_tensor(f"ps_t{i}", [P, 2, 512], F32)) for i in range(2)]
    ps_o = ctx.enter_context(nc.psum_tensor("ps_o", [P, 2, 512], F32))
    one = Ring([Slot(t) for t in ps_a])
    slots_t = [Slot(t) for t in ps_t]
    slot_o = Slot(ps_o)
    two = Ring(slots_t)
    six = Ring(slots_t + [slot_o])
    outs = Ring([slot_o])

    q_scr = nc.dram_tensor("q_scr", (3, E, TOK), BF16)
    k_scr = nc.dram_tensor("k_scr", (3, E, TOK), BF16)
    c_scr = nc.dram_tensor("c_scr", (3, E, CTX), BF16)
    kx_scr = nc.dram_tensor("kx_scr", (3, E, CTX), BF16)
    m_scr = nc.dram_tensor("m_scr", (2, NC, P), BF16)
    v_scr = nc.dram_tensor("v_scr", (2, P, NC * H * (D + 1)), F32)

    t_x, t_keep, t_rows, t_l0a, t_ctx, t_mk = (transfers(n) for n in ("x", "keep", "rows", "l0a", "ctx", "mk"))
    t_b2, t_bf = transfers("b2"), transfers("bf")
    t_x.start(Q, x[:], d["x"].rearrange("b (j p) f -> p (b j) f", p=P))
    t_l0a.start(Q, ffn_w[:, 0:L0A_N], d["l0a"][:, :])
    t_keep.start(Q, keep[:], d["keep"][:, :])
    ctx_tok = wk(0, 2048).rearrange("p (t f) -> p t f", t=NC)
    ctxT = wk(2048, 2048)
    t_ctx.start(Q, ctx_tok, d["ctx_1024"].rearrange("b (j p) f -> p (b j) f", p=P))
    t_bf.start(Q, ident_b[:], d["const_bf16"][0])
    t_bf.start(Q, far_b[:], d["const_bf16"][1])
    t_rows.start(Q, rows[:], d["rows"][0:1, :].broadcast_to([P, ROW_N]))
    t_mk.start(Q, masku8[:], d["mask_keys"].rearrange("b (j p) -> (b j) p", p=P))
    t_b2.start(Q, b2[:, 0, :], d["b2_L0"][:, :])
    t_b2.start(Q, b2[0:NE, 1, :], d["b2_L3"][:, :])

    G.mark(pool.memset(halves[:, 0:1], -0.5))
    G.mark(pool.memset(halves[:, 1:2], 0.5))
    G.mark(pool.memset(q_stack[:], 1.0))
    G.mark(pool.memset(self_stack[:], 1.0))
    stacks_set = G.mark(pool.memset(ctx_stack[:], 1.0))
    V.mark(dve.memset(minus1[:], -1.0))
    V.mark(dve.memset(gates[:], MOE_SCALE))
    V.wait(t_keep.done())
    PE.wait(t_keep.done(), t_bf.done())
    A.wait(t_keep.done())
    ident = kp("ident")

    V.wait(t_rows.done())
    for i, (a, b_) in enumerate((("lq1", "lk1"), ("lq2", "lk2"))):
        V.step(dve.tensor_tensor(lam8[:, i, :], rw(a), rw(b_), ALU.mult))
        lam_sum = V.step(dve.tensor_reduce(lam[:, i:i + 1], lam8[:, i, :], AX, ALU.add))
    A.wait(lam_sum)
    lam_exp = A.mark(act.activation(lam[:, 2:4], lam[:, 0:2], ACT.Exp))
    V.wait(lam_exp)
    V.step(dve.tensor_tensor(lam[:, 4:5], lam[:, 3:4], lam[:, 2:3], ALU.subtract))
    V.step(dve.tensor_scalar(lam[:, 5:6], lam[:, 4:5], -LAMBDA_INIT, None, ALU.add))

    def evacuate(turn, dst, src, ready):
        if turn % 2:
            A.wait(ready)
            return A.mark(act.copy(dst, src))
        V.wait(ready)
        return V.mark(dve.tensor_copy(dst, src))

    def power(dst, src, exponent, ready):
        e = halves[:, 0:1] if exponent < 0 else halves[:, 1:2]
        G.wait(ready)
        return G.mark(pool.tensor_tensor(dst, src, e.broadcast_to(list(src.shape)), ALU.pow))

    def layer_norm(x_marks):
        for t in range(NT):
            V.wait(x_marks[t])
            m = V.mark(dve.bn_stats(stats[:, t, :], x[:, t, :]))
        V.wait(m)
        for t in range(NT):
            m = V.mark(dve.bn_aggr(mv[:, t, :], stats[:, t, :]))
        V.wait(m)
        m = V.step(dve.tensor_scalar(rstd[:], mv[:, :, 1], LN_EPS, None, ALU.add))
        V.wait(power(rstd[:], rstd[:], -0.5, m))
        marks = [V.mark(dve.tensor_scalar(xn[:, t, :], x[:, t, :], mv[:, t, 0:1], rstd[:, t:t + 1],
                                          ALU.subtract, ALU.mult)) for t in range(NT)]
        return marks, turn_tiles(xn, xnT, marks, NT)

    def turn_tiles(src, dst, marks, n):
        done = []
        for g in range(n // 4):
            slot = one.take(PE)
            for i in range(4):
                PE.wait(marks[4 * g + i])
                m = PE.mark(pe.transpose(slot.ap[:, i * P:(i + 1) * P], src[:, 4 * g + i, :], ident))
            m = evacuate(g, dst[:, g * 512:(g + 1) * 512], slot.ap[:], m)
            slot.freed = (m,)
            done.append(m)
        return done

    def feature_major(dst, w, srcT, ready, n, bias=None, scale=1.0):
        done = []
        for g in range(n // 512):
            slot = one.take(PE)
            PE.wait(ready[g])
            m = PE.mark(pe.matmul(slot.ap[:], w, srcT[:, g * 512:(g + 1) * 512], start=True, stop=True))
            A.wait(m)
            if bias is None:
                m = A.mark(act.activation(dst[:, g * 512:(g + 1) * 512], slot.ap[:], ACT.Copy, scale=scale))
            else:
                m = A.mark(act.activation(dst[:, g * 512:(g + 1) * 512], slot.ap[:], ACT.Identity,
                                          bias=bias, scale=1.0))
            slot.freed = (m,)
            done.append(m)
        return done

    def split(src, dst, n, ready, dst_free=()):
        V.wait(*ready)
        V.wait(*dst_free)
        V.step(dve.tensor_copy(dst[:, 0, :], src))
        V.step(dve.tensor_tensor(src, src, dst[:, 0, :], ALU.subtract))
        V.step(dve.tensor_copy(dst[:, 1, :], src))
        V.step(dve.tensor_tensor(src, src, dst[:, 1, :], ALU.subtract))
        return V.step(dve.tensor_copy(dst[:, 2, :], src))

    def to_scratch(name, scr, src, ready):
        t = transfers(name)
        Q.wait(ready)
        t.start(Q, scr[:, :, :].rearrange("s p t -> p s t"), src)
        return t

    def fill_stack(name, scr, stack, side, written, free=(), mask=None, batches=None):
        t = transfers(name)
        Q.wait(stacks_set, written.done(), *free)
        for parity in range(2):
            for r, pair in enumerate(PARTS):
                p0 = parity * SLOT + r * D
                src = scr[pair[side]].rearrange("(h two d) t -> two d h t", two=2, d=D)[parity]
                if batches:
                    for b in range(batches):
                        t.start(Q, stack[p0:p0 + D, b, :, :], src[:, :, b * S:(b + 1) * S])
                else:
                    t.start(Q, stack[p0:p0 + D, :, :], src)
            if mask is not None:
                n = stack.shape[-1]
                row = mask.rearrange("t p -> (t p)")[0:n]
                for h in range(PAIRS):
                    t.start(Q, stack[parity * SLOT + ROW_MASK:parity * SLOT + ROW_MASK + 1, h, :],
                            row.rearrange("(o n) -> o n", o=1))
        return t

    state = {"q_free": (), "self_free": (), "ctx_free": (), "parts_free": (), "x": [t_x.done()] * NT,
             "vaug_free": (), "ffn_free": ()}

    def queries(name, ready):
        m = split(qT[:], parts, TOK, ready, state["parts_free"])
        t = to_scratch(name + "_qw", q_scr, parts[:], m)
        state["parts_free"] = (t.done(),)
        return fill_stack(name + "_qf", q_scr, q_stack, 0, t, state["q_free"], batches=B)

    def head_slot(h):
        return h % 2 * SLOT, h // 2

    def max_to_stack(b, m, t):
        col = mx[:, b, :, :, :].rearrange("p a h q -> p (a h q)")
        V.wait(m)
        m = V.step(dve.tensor_copy(mparts[:, 0, :], col))
        V.step(dve.tensor_tensor(col, col, mparts[:, 0, :], ALU.subtract))
        V.step(dve.tensor_copy(mparts[:, 1, :], col))
        V.step(dve.tensor_tensor(col, col, mparts[:, 1, :], ALU.subtract))
        m = V.step(dve.tensor_copy(mparts[:, 2, :], col))
        slot = one.take(PE)
        PE.wait(m)
        ps = slot.ap[0:96, 0:64].bitcast(BF16)
        m = PE.mark(pe.transpose(ps, mparts[:].rearrange("p s c -> p (s c)"), ident_b[:]))
        V.wait(m)
        m = V.mark(dve.tensor_copy(mT[:, b, :], ps))
        slot.freed = (m,)
        Q.wait(m)
        for s in range(3):
            for parity in range(2):
                r = (s * 2 + parity) * TPB * PAIRS
                t.start(Q, q_stack[parity * SLOT + ROW_MAX + s:parity * SLOT + ROW_MAX + s + 1, b, :, :]
                        .rearrange("o h (q t) -> o (h q) t", q=TPB), mT[r:r + TPB * PAIRS, b, :])
        return t.done()

    def attention(name, k_stack, nk, values, dv, q_ready, k_ready, v_ready, finish, add_mask=None):
        nkt = nk // P
        PE.wait(q_ready, k_ready)
        pt_n = nkt * S
        pts = Ring([Slot(wk(9216 + i * pt_n, pt_n).rearrange("p (k q) -> p k q", k=nkt))
                    for i in range(3072 // pt_n)])
        t_max = [transfers(f"{name}_m{b}") for b in range(B)]
        max_ready = {}

        def max_head(b, h):
            p0, pair = head_slot(h)
            per = 512 // nk
            for g in range(TPB // per):
                slot = one.take(PE)
                for i in range(per):
                    q0 = (g * per + i) * P
                    m = PE.mark(pe.matmul(slot.ap[:, i * nk:(i + 1) * nk],
                                          q_stack[p0:p0 + K_SCORE, b, pair, q0:q0 + P],
                                          k_stack[p0:p0 + K_SCORE, pair, b * nk:(b + 1) * nk],
                                          start=True, stop=True))
                V.wait(m)
                if add_mask:
                    m = V.mark(dve.tensor_tensor_reduce(
                        slot.ap[:], slot.ap[:], add_mask[0][:, b * TPB + g, :], 1.0, -3e38,
                        ALU.add, ALU.max, mx[:, b, h % 2, pair, g:g + 1]))
                else:
                    m = V.mark(dve.tensor_reduce(mx[:, b, h % 2, pair, g * per:(g + 1) * per],
                                                 slot.ap[:].rearrange("p (i k) -> p i k", k=nk),
                                                 AX, ALU.max, negate=True))
                slot.freed = (m,)
            return m

        def close_max(b, m):
            if add_mask:
                V.wait(m)
                c = mx[:, b, :, :, :].rearrange("p a h q -> p (a h q)")
                m = V.mark(dve.tensor_scalar(c, c, -1.0, None, ALU.mult))
            max_ready[b] = max_to_stack(b, m, t_max[b])

        def exp_head(b, h):
            p0, pair = head_slot(h)
            slot = two.take(PE)
            ps = slot.ap[:].rearrange("p a n -> p (a n)")
            PE.wait(max_ready[b])
            for k in range(nkt):
                o = ps[:, k * S:(k + 1) * S]
                m = pe.matmul(o, k_stack[p0:p0 + K_EXP, pair, b * nk + k * P:b * nk + (k + 1) * P],
                              q_stack[p0:p0 + K_EXP, b, pair, :], start=True, stop=add_mask is None)
                if add_mask:
                    m = pe.matmul(o, ident_b[:], add_mask[1][:, b, k, :], start=False, stop=True)
            m = PE.mark(m)
            pt = pts.take(A)
            A.wait(m)
            m = A.mark(act.activation(pt.ap[:].rearrange("p k q -> p (k q)"), ps[:, 0:pt_n], ACT.Exp))
            slot.freed = (m,)
            return pt, m

        def values_head(b, h, pt, m, slot):
            PE.wait(m, v_ready)
            hv = h if dv == D else h // 2
            for q in range(TPB):
                for k in range(nkt):
                    m = PE_last[0] = pe.matmul(slot.ap[:, q, h * (dv + 1):(h + 1) * (dv + 1)],
                                               pt.ap[:, k, q * P:(q + 1) * P],
                                               values[:, b * nkt + k, hv * (dv + 1):(hv + 1) * (dv + 1)],
                                               start=(k == 0), stop=(k == nkt - 1))
            m = PE.mark(m)
            pt.freed = (m,)
            return m

        PE_last = [None]
        for h in range(H):
            m = max_head(0, h)
        close_max(0, m)
        for b in range(B):
            acc = outs.take(PE)
            held = None
            for h in range(H):
                now = exp_head(b, h)
                if b + 1 < B:
                    m = max_head(b + 1, h)
                if held:
                    values_head(b, h - 1, *held, acc)
                held = now
            last = values_head(b, H - 1, *held, acc)
            if b + 1 < B:
                close_max(b + 1, m)
            finish(b, acc, last)
        state["q_free"] = (last,)
        return last

    def normalise(b, acc, ready, scale=None):
        V.wait(ready)
        done = []
        for q in range(TPB):
            heads = acc.ap[:, q, 0:H * (D + 1)].rearrange("p (h e) -> p h e", h=H)
            V.step(dve.reciprocal(rsum[:, q, :], heads[:, :, D]))
            if scale is not None:
                V.step(dve.tensor_scalar(rsum[:, q, :], rsum[:, q, :], scale[:, b * TPB + q:b * TPB + q + 1],
                                         None, ALU.mult))
            done.append(V.mark(dve.tensor_tensor(
                xn[:, b * TPB + q, :].rearrange("p (h e) -> p h e", h=H), heads[:, :, 0:D],
                rsum[:, q, :].unsqueeze(2).broadcast_to([P, H, D]), ALU.mult)))
        acc.freed = (done[-1],)
        return done

    def project_out(b, w, marks, post=None):
        slot = one.take(PE)
        for q in range(TPB):
            PE.wait(marks[q])
            m = PE.mark(pe.transpose(slot.ap[:, q * P:(q + 1) * P], xn[:, b * TPB + q, :], ident))
        A.wait(m)
        m = A.mark(act.copy(qT[:, b * S:(b + 1) * S], slot.ap[:, 0:S]))
        slot.freed = (m,)
        slot = one.take(PE)
        PE.wait(m)
        for q in range(TPB):
            t = b * TPB + q
            m = PE.mark(pe.matmul(slot.ap[:, q * P:(q + 1) * P], qT[:, t * P:(t + 1) * P], w,
                                  start=True, stop=True))
        V.wait(m, *state["bias"])
        xb = x[:, b * TPB:(b + 1) * TPB, :]
        ps = slot.ap[:, 0:S].rearrange("p (q f) -> p q f", q=TPB)
        if post is not None:
            V.step(dve.tensor_tensor(ps, ps, post.unsqueeze(1).broadcast_to([P, TPB, E]), ALU.mult))
        m = V.mark(dve.tensor_tensor(xb, ps, xb, ALU.add))
        slot.freed = (m,)
        for q in range(TPB):
            state["x"][b * TPB + q] = m

    def add_rows(row, after):
        G.wait(t_rows.done(), *after)
        for t in range(NT):
            m = G.mark(pool.tensor_tensor(x[:, t, :], x[:, t, :], row, ALU.add))
        state["bias"] = (m,)

    def self_keys(name, kT, ready):
        m = split(kT, parts, TOK, ready, state["parts_free"])
        t = to_scratch(name + "_kw", k_scr, parts[:], m)
        state["parts_free"] = (t.done(),)
        return fill_stack(name + "_kf", k_scr, self_stack, 1, t, state["self_free"],
                          mask=m_scr[0] if name == "L0a" else None)

    def context():
        V.wait(t_mk.done())
        m = V.mark(dve.tensor_scalar(maskrow[:], masku8[:], -1.0, BIG, ALU.add, ALU.mult))
        Q.wait(m, stacks_set)
        t_mrow.start(Q, m_scr[0], d["const_bf16"][2, 0:NC, :])
        t_mrow.start(Q, m_scr[1], maskrow[:])

    t_mrow = transfers("mrow")
    context()
    Q.wait(t_mrow.done())

    def prepare_context():
        PE.wait(t_ctx.done())
        V.wait(t_ctx.done())
        ready = []
        for g in range(4):
            slot = one.take(PE)
            for i in range(4):
                m = PE.mark(pe.transpose(slot.ap[:, i * P:(i + 1) * P], ctx_tok[:, 4 * g + i, :], ident))
            m = evacuate(g, ctxT[:, g * 512:(g + 1) * 512], slot.ap[:], m)
            slot.freed = (m,)
            ready.append(m)
        ones_set = V.mark(dve.memset(vaug[:], 1.0))
        va = vaug[:].rearrange("p t (h e) -> p t h e", h=H)
        V.wait(ones_set)
        m_va = V.mark(dve.tensor_copy(va[:, :, :, 0:D].rearrange("p t h e -> p (t h) e"),
                                      ctx_tok.rearrange("p t (h e) -> p (t h) e", e=D)))
        state["va0"] = m_va
        t_v = transfers("v0w")
        Q.wait(m_va)
        t_v.start(Q, v_scr[0], vaug[:].rearrange("p t c -> p (t c)"))
        kx = wk(4096, 2048)
        kx_ready = feature_major(kx, kp("L1x_kT"), ctxT, ready, CTX, bias=kp("L1x_bk"))
        vx = wk(6144, NC * H * (D + 1)).rearrange("p (t c) -> p t c", t=NC)
        ones_set = V.mark(dve.memset(vx, 1.0))
        V.wait(ones_set, t_rows.done())
        for g in range(4):
            slot = one.take(PE)
            PE.wait(ready[g])
            for i in range(4):
                t = 4 * g + i
                m = PE.mark(pe.matmul(slot.ap[:, i * P:(i + 1) * P], ctxT[:, t * P:(t + 1) * P],
                                      kp("L1x_vT"), start=True, stop=True))
            V.wait(m)
            for i in range(4):
                t = 4 * g + i
                m = V.mark(dve.tensor_tensor(
                    vx[:, t, :].rearrange("p (h e) -> p h e", h=H)[:, :, 0:D],
                    slot.ap[:, i * P:(i + 1) * P].rearrange("p (h e) -> p h e", h=H),
                    rw("L1x_bv").rearrange("p (h e) -> p h e", h=H), ALU.add))
            slot.freed = (m,)
        t_vx = transfers("v1w")
        Q.wait(m)
        t_vx.start(Q, v_scr[1], vx.rearrange("p t c -> p (t c)"))
        kv = parts[:].rearrange("p s t -> p (s t)").bitcast(F32)[:, 0:4 * 2 * E].rearrange("p (t c) -> p t c", t=4)
        kv_free = ()
        for b in range(B):
            V.wait(*kv_free)
            for g in range(2):
                slot = one.take(PE)
                PE.wait(ready[b])
                for i in range(2):
                    t = 4 * b + 2 * g + i
                    m = PE.mark(pe.matmul(slot.ap[:, i * 256:(i + 1) * 256], ctxT[:, t * P:(t + 1) * P],
                                          kp("L3x_kvT"), start=True, stop=True))
                V.wait(m)
                m = V.mark(dve.tensor_tensor(
                    kv[:, 2 * g:2 * g + 2, :], slot.ap[:].rearrange("p (t c) -> p t c", t=2),
                    rw("L3x_bkv").unsqueeze(1).broadcast_to([P, 2, 2 * E]), ALU.add))
                slot.freed = (m,)
            slot = one.take(PE)
            PE.wait(m)
            for i in range(4):
                m = pe.matmul(slot.ap[:, 0:E], kv[:, i, 0:E], kv[:, i, E:2 * E], start=(i == 0), stop=(i == 3))
            m = PE.mark(m)
            kv_free = (m,)
            V.wait(m)
            m = V.mark(dve.scalar_tensor_tensor(kv3[:, b, :], slot.ap[:, 0:E], 1.0 / DK3, kp("blockdiag"),
                                                ALU.mult, ALU.mult))
            slot.freed = (m,)
        state["kv3"] = m
        room = [ctx_stack[:, 3 * i:3 * i + 3, :] for i in range(2)]
        V.wait(stacks_set)
        m = split(kx, room[0], CTX, kx_ready)
        t_kx = to_scratch("kx", kx_scr, room[0], m)
        m = split(ctxT, room[1], CTX, [state["kv3"]])
        t_c = to_scratch("c", c_scr, room[1], m)
        G.wait(t_kx.done(), t_c.done())
        again = G.mark(pool.memset(ctx_stack[:], 1.0))
        state["vx_w"], state["v0_w"] = t_vx, t_v
        return t_c, t_kx, again

    def load_ctx_stack(name, which, scr, written, mask):
        return fill_stack(name, scr, ctx_stack, 1, written, state["ctx_free"], mask=m_scr[mask])

    def load_values(name, which):
        t = transfers(name)
        Q.wait(state["vx_w"].done(), state["v0_w"].done(), *state["vaug_free"])
        t.start(Q, vaug[:].rearrange("p t c -> p (t c)"), v_scr[which])
        return t

    def finish_out():
        t_out = transfers("out")
        Q.wait(*state["x"])
        t_out.start(Q, out.rearrange("b (j p) f -> p (b j) f", p=P), x[:])
        for t in every_transfer:
            Q.wait(t.done())

    def l0_attention():
        _, ready = layer_norm(state["x"])
        PE.wait(t_l0a.done())
        V.wait(t_l0a.done())
        kT = xn[:].rearrange("p t f -> p (t f)")
        marks = {}
        for dst, w, wp, c, s_ in ((qT[:], "qT", "qpT", "qcos", "qsin"), (kT, "kT", "kpT", "kcos", "ksin")):
            done = []
            for g in range(2):
                s0 = one.take(PE)
                PE.wait(ready[g])
                m0 = PE.mark(pe.matmul(s0.ap[:], l0w(w), xnT[:, g * 512:(g + 1) * 512], start=True, stop=True))
                s1 = one.take(PE)
                m1 = PE.mark(pe.matmul(s1.ap[:], l0w(wp), xnT[:, g * 512:(g + 1) * 512], start=True, stop=True))
                o = dst[:, g * 512:(g + 1) * 512].rearrange("p (b t) -> p b t", b=2)
                tmp = wk(9216 + g * 512, 512).rearrange("p (b t) -> p b t", b=2)
                table = lambda n: l0w(n).unsqueeze(1).broadcast_to([P, 2, S])
                V.wait(m1)
                m = V.mark(dve.tensor_tensor(o, s0.ap[:].rearrange("p (b t) -> p b t", b=2), table(c), ALU.mult))
                s0.freed = (m,)
                m = V.step(dve.tensor_tensor(tmp, s1.ap[:].rearrange("p (b t) -> p b t", b=2), table(s_), ALU.mult))
                s1.freed = (m,)
                done.append(V.step(dve.tensor_tensor(o, o, tmp, ALU.add)))
            marks[w] = done
        tq = queries("L0a", marks["qT"])
        tk = self_keys("L0a", kT, marks["kT"])
        va = ffn_w[:, L0A_N:L0A_N + NT * H0 * (DV0 + 1)].rearrange("p (t h e) -> p t h e", t=NT, h=H0)
        V.wait(V.mark(dve.memset(va, 1.0)))
        for g in range(2):
            slot = one.take(PE)
            for i in range(4):
                t = 4 * g + i
                m = PE.mark(pe.matmul(slot.ap[:, i * P:(i + 1) * P], xnT[:, t * P:(t + 1) * P], l0w("vT"),
                                      start=True, stop=True))
            V.wait(m)
            for i in range(4):
                m = V.mark(dve.tensor_copy(va[:, 4 * g + i, :, 0:DV0],
                                           slot.ap[:, i * P:(i + 1) * P].rearrange("p (h e) -> p h e", h=H0)))
            slot.freed = (m,)
        state["bias"] = ()

        def finish(b, acc, ready):
            V.wait(ready)
            marks = []
            tmp = wk(8500, 640)
            for q in range(TPB):
                o = acc.ap[:, q, 0:H * (DV0 + 1)].rearrange("p (h two e) -> p h two e", two=2, e=DV0 + 1)
                r = rsum[:, q, :].rearrange("p (h two) -> p h two", two=2)
                V.step(dve.reciprocal(r, o[:, :, :, DV0]))
                V.step(dve.tensor_scalar(r[:, :, 1], r[:, :, 1], lam[:, 5:6], None, ALU.mult))
                t0 = tmp[:, 0:E].rearrange("p (h e) -> p h e", h=H0)
                t1 = tmp[:, E:2 * E].rearrange("p (h e) -> p h e", h=H0)
                V.mark(dve.tensor_tensor(t0, o[:, :, 0, 0:DV0], r[:, :, 0:1].broadcast_to([P, H0, DV0]), ALU.mult))
                V.step(dve.tensor_tensor(t1, o[:, :, 1, 0:DV0], r[:, :, 1:2].broadcast_to([P, H0, DV0]), ALU.mult))
                V.step(dve.tensor_tensor(t0, t0, t1, ALU.add))
                V.step(dve.tensor_tensor(t1, t0, t0, ALU.mult))
                ss = tmp[:, 256 + 16 * q:256 + 16 * q + H0]
                V.step(dve.tensor_reduce(ss, t1, AX, ALU.add))
                m = V.step(dve.tensor_scalar(ss, ss, 1.0 / DV0, 1e-5, ALU.mult, ALU.add))
                V.wait(power(ss, ss, -0.5, m))
                V.step(dve.tensor_scalar(ss, ss, 1.0 - LAMBDA_INIT, None, ALU.mult))
                marks.append(V.step(dve.tensor_tensor(xn[:, b * TPB + q, :].rearrange("p (h e) -> p h e", h=H0),
                                                      t0, ss.unsqueeze(2).broadcast_to([P, H0, DV0]), ALU.mult)))
            acc.freed = (marks[-1],)
            project_out(b, l0w("oT"), marks)

        last = attention("L0a", self_stack, S, va.rearrange("p t h e -> p t (h e)"), DV0,
                         tq.done(), tk.done(), m, finish)
        state["self_free"] = (last,)
        state["ffn_free"] = (PE_mark_now(), last)

    def PE_mark_now():
        return (PE.sem, PE.count)

    def load_ffn(name, pieces):
        t = transfers(name)
        Q.wait(*state["ffn_free"])
        n = 0
        for src in pieces:
            t.start(Q, ffn_w[:, n:n + src.shape[1]], src)
            n += src.shape[1]
        return t

    def cross(name, w_out, bias_row, t_stack, values_ready, scale, project=None, add_mask=None):
        norm, ready = layer_norm(state["x"])
        if bias_row is None:
            state["bias"] = ()
        else:
            add_rows(rw(bias_row), norm)
        if project is None:
            A.wait(*ready)
            m = A.mark(act.activation(qT[:], xnT[:], ACT.Copy, scale=scale))
            q_in = [m]
        else:
            q_in = feature_major(qT, kp(project), xnT, ready, TOK, bias=kp("L1x_bq"))
            A.wait(*q_in)
            q_in = [A.mark(act.activation(qT[:], qT[:], ACT.Copy, scale=scale))]
        tq = queries(name, q_in)

        def finish(b, acc, ready):
            project_out(b, w_out, normalise(b, acc, ready))

        last = attention(name, ctx_stack, S2, vaug, D, tq.done(), t_stack.done(), values_ready, finish, add_mask)
        state["ctx_free"] = state["vaug_free"] = (last,)

    def prepare_mask():
        t = transfers("mask")
        raw = wk(4096, 4096).bitcast(I32).rearrange("p (t k) -> p t k", t=NT)
        far_q = wk(0, 2048).bitcast(BF16).rearrange("p (t k) -> p t k", t=NT)
        far_k = wk(2048, 2048).bitcast(BF16).rearrange("p (b k q) -> p b k q", b=B, k=S2 // P)
        Q.wait(state["vx_w"].done(), state["c_done"], state["kx_done"])
        t.start(Q, raw, d["mask_L0"].rearrange("b o (j p) k -> p (b o j) k", p=P))
        V.wait(t.done(), state["c_done"])
        for i in range(NT):
            m = V.mark(dve.tensor_scalar(far_q[:, i, :], raw[:, i, :], 0, -BIG, ALU.is_equal, ALU.mult))
        for b in range(B):
            for k in range(S2 // P):
                slot = one.take(PE)
                PE.wait(m)
                ps = slot.ap[:, 0:P].bitcast(BF16)
                for q in range(TPB):
                    mm = PE.mark(pe.transpose(ps[:, q * P:(q + 1) * P],
                                              far_q[:, b * TPB + q, k * P:(k + 1) * P], ident_b[:]))
                mm = evacuate(k, far_k[:, b, k, :], ps, mm)
                slot.freed = (mm,)
                PE.wait(mm)
        return far_q, far_k

    def route(name, router, eps, ready):
        slot = one.take(PE)
        PE.wait(*ready)
        for t in range(NT):
            m = PE.mark(pe.matmul(slot.ap[:, t * NE:(t + 1) * NE], xnT[:, t * P:(t + 1) * P], router,
                                  start=True, stop=True))
        lg = slot.ap[:, 0:NT * NE].rearrange("p (t e) -> p t e", e=NE)
        V.wait(*state["parts_free"])
        flat = parts[:].rearrange("p s t -> p (s t)").bitcast(F32)
        sm = [flat[:, TOK + i * NT * NE:TOK + (i + 1) * NT * NE].rearrange("p (t e) -> p t e", e=NE) for i in range(8)]
        p_, eq, o1, o2, c = sm[0:5]
        r = [sm[5][:, :, i] for i in range(8)] + [sm[6][:, :, i] for i in range(2)]
        wide = lambda a: a.unsqueeze(2).broadcast_to([P, NT, NE])
        rev = kp("rev").unsqueeze(1).broadcast_to([P, NT, NE])
        V.wait(m)
        V.step(dve.tensor_reduce(r[0], lg, AX, ALU.max))
        m = V.step(dve.tensor_tensor(p_, lg, wide(r[0]), ALU.subtract))
        slot.freed = (m,)
        A.wait(m)
        V.wait(A.mark(act.activation(p_, p_, ACT.Exp)))
        V.step(dve.tensor_reduce(r[1], p_, AX, ALU.add))
        V.step(dve.reciprocal(r[1], r[1]))
        V.step(dve.tensor_tensor(p_, p_, wide(r[1]), ALU.mult))
        for o, top in ((o1, r[2]), (o2, r[3])):
            V.step(dve.tensor_reduce(top, p_, AX, ALU.max))
            V.step(dve.tensor_tensor(eq, p_, wide(top), ALU.is_equal))
            V.step(dve.tensor_tensor(eq, eq, rev, ALU.mult))
            V.step(dve.tensor_reduce(r[4], eq, AX, ALU.max))
            V.step(dve.tensor_tensor(o, rev, wide(r[4]), ALU.is_equal))
            if o is o1:
                V.step(dve.scalar_tensor_tensor(c, o, -2.0, p_, ALU.mult, ALU.add))
                p_ = c
        if eps is None:
            for top in (r[2], r[3]):
                V.step(dve.tensor_scalar(top, top, MOE_SCALE, None, ALU.mult))
        else:
            V.step(dve.tensor_tensor(r[5], r[2], r[3], ALU.add))
            V.step(dve.tensor_scalar(r[5], r[5], eps, None, ALU.add))
            V.step(dve.reciprocal(r[5], r[5]))
            for top in (r[2], r[3]):
                V.step(dve.tensor_tensor(top, top, r[5], ALU.mult))
        V.mark(dve.tensor_tensor(o1, o1, wide(r[2]), ALU.mult))
        V.step(dve.tensor_tensor(o2, o2, wide(r[3]), ALU.mult))
        return V.step(dve.tensor_tensor(gates[:, :, 0:NE], o1, o2, ALU.add))

    def add_gated_bias(which, n, gated):
        PE.wait(t_b2.done())
        V.wait(*state["parts_free"])
        for g in range(2):
            slot = one.take(PE)
            PE.wait(gated)
            for i in range(4):
                m = PE.mark(pe.transpose(slot.ap[0:n, i * P:(i + 1) * P], gates[:, 4 * g + i, 0:n], ident))
            V.wait(m)
            m = V.mark(dve.tensor_copy(gatesT[0:n, g * 512:(g + 1) * 512], slot.ap[0:n, :]))
            slot.freed = (m,)
            slot = one.take(PE)
            PE.wait(m)
            for i in range(4):
                t = 4 * g + i
                m = PE.mark(pe.matmul(slot.ap[:, i * P:(i + 1) * P], gatesT[0:n, t * P:(t + 1) * P],
                                      b2[0:n, which, :], start=True, stop=True))
            V.wait(m)
            xs = x[:, 4 * g:4 * g + 4, :]
            m = V.mark(dve.tensor_tensor(xs, slot.ap[:].rearrange("p (t f) -> p t f", t=4), xs, ALU.add))
            slot.freed = (m,)
            for i in range(4):
                state["x"][4 * g + i] = m

    def down(hidden, blocks, w2, scalar_of, ready):
        for g in range(2):
            slot = one.take(PE)
            PE.wait(ready)
            for i in range(4):
                t = 4 * g + i
                for j in range(blocks):
                    m = pe.matmul(slot.ap[:, i * P:(i + 1) * P], hidden[:, j, t * P:(t + 1) * P], w2(j),
                                  start=(j == 0), stop=(j == blocks - 1))
            last = PE.mark(m)
            V.wait(last)
            for i in range(4):
                t = 4 * g + i
                V.wait(state["x"][t])
                state["x"][t] = V.mark(dve.scalar_tensor_tensor(
                    x[:, t, :], slot.ap[:, i * P:(i + 1) * P], scalar_of(t), x[:, t, :], ALU.mult, ALU.add))
            slot.freed = (state["x"][4 * g + 3],)
        return last

    def gelu_experts(name, router, eps, n_exp, w_off2, b1, t_w, bias_which, bias_rows, weights):
        _, ready = layer_norm(state["x"])
        gated = route(name, router, eps, ready)
        add_gated_bias(bias_which, bias_rows, gated)
        hid = Ring([Slot(wk(i * FJ * TOK, FJ * TOK).rearrange("p (j t) -> p j t", j=FJ)) for i in range(2)])

        def up(e):
            h = hid.take(A)
            PE.wait(t_w.done())
            for j in range(FJ):
                slot = six.take(PE)
                for g in range(2):
                    m = PE.mark(pe.matmul(slot.ap[:, g, :],
                                          weights[:, (e * FJ + j) * P:(e * FJ + j + 1) * P],
                                          xnT[:, g * 512:(g + 1) * 512], start=True, stop=True))
                A.wait(m)
                m = A.mark(act.activation(h.ap[:, j, :], slot.ap[:].rearrange("p a n -> p (a n)"),
                                          ACT.Gelu_apprx_tanh, bias=b1(e, j)))
                slot.freed = (m,)
            return h, m

        held = up(0)
        for e in range(n_exp):
            nxt = up(e + 1) if e + 1 < n_exp else None
            h, m = held
            w2 = lambda j: weights[:, w_off2 + (e * FJ + j) * E:w_off2 + (e * FJ + j + 1) * E]
            scalar = (lambda t: gates[:, t, e:e + 1]) if e < NE else (lambda t: MOE_SCALE)
            h.freed = (down(h.ap, FJ, w2, scalar, m),)
            held = nxt
        state["ffn_free"] = h.freed

    def swiglu_experts(t_w):
        _, ready = layer_norm(state["x"])
        route("L1f", kp("L1f_router"), 1e-20, ready)
        hid = Ring([Slot(wk(i * F1J * TOK, F1J * TOK).rearrange("p (j t) -> p j t", j=F1J)) for i in range(2)])
        PE.wait(t_w.done())

        def up(e):
            h = hid.take(A)
            for j in range(F1J):
                pair = []
                for part in range(2):
                    slot = six.take(PE)
                    for g in range(2):
                        m = PE.mark(pe.matmul(slot.ap[:, g, :],
                                              ffn_w[:, ((part * 9 + e) * F1J + j) * P:((part * 9 + e) * F1J + j + 1) * P],
                                              xnT[:, g * 512:(g + 1) * 512], start=True, stop=True))
                    pair.append((slot, m))
                (sg, mg), (su, mu) = pair
                A.wait(mg)
                m = A.mark(act.activation(h.ap[:, j, :], sg.ap[:].rearrange("p a n -> p (a n)"), ACT.Silu))
                sg.freed = (m,)
                V.wait(m, mu)
                m = V.mark(dve.tensor_tensor(h.ap[:, j, :], h.ap[:, j, :],
                                             su.ap[:].rearrange("p a n -> p (a n)"), ALU.mult))
                su.freed = (m,)
            return h, m

        held = up(0)
        for e in range(NE + 1):
            nxt = up(e + 1) if e < NE else None
            h, m = held
            w2 = lambda j: ffn_w[:, (18 * F1J + e * F1J + j) * P:(18 * F1J + e * F1J + j + 1) * P]
            scalar = (lambda t: gates[:, t, e:e + 1]) if e < NE else (lambda t: 1.0)
            h.freed = (down(h.ap, F1J, w2, scalar, m),)
            held = nxt
        state["ffn_free"] = h.freed

    def l1_attention():
        norm, ready = layer_norm(state["x"])
        add_rows(rw("L1a_bout"), norm)
        W = 3 * E + 1
        qkv = wk(0, NT * W).rearrange("p (t c) -> p t c", t=NT)
        for t in range(NT):
            slot = one.take(PE)
            PE.wait(*ready)
            m = PE.mark(pe.matmul(slot.ap[:, 0:W], xnT[:, t * P:(t + 1) * P], kp("L1a_qkv"), start=True, stop=True))
            V.wait(m)
            m = V.step(dve.tensor_tensor(qkv[:, t, :], slot.ap[:, 0:W], rw("L1a_bqkv"), ALU.add))
            slot.freed = (m,)
        n2 = NT * 2 * H
        u2 = wk(3200, NT * 2 * E)
        u = qkv[:, :, 0:2 * E]
        V.step(dve.tensor_tensor(u2.rearrange("p (t c) -> p t c", t=NT), u, u, ALU.mult))
        aux = [wk(5300 + i * n2, n2) for i in range(8)]
        w, n, e, ei, f, poly, wc, less = aux
        by8 = u2.rearrange("p (g e) -> p g e", e=D)
        V.step(dve.tensor_reduce(w, by8, AX, ALU.add))
        V.step(dve.scalar_tensor_tensor(w, by8[:, :, 0], -2.0, w, ALU.mult, ALU.add))
        m = V.step(dve.tensor_scalar(w, w, 1e-8, None, ALU.max))
        m = power(n, w, 0.5, m)
        A.wait(m)
        m = A.mark(act.activation(e, n, ACT.Exp))
        V.step(dve.tensor_scalar(wc, w, 1.0, None, ALU.min))
        V.step(dve.tensor_scalar(less, w, 1.0, None, ALU.is_lt))
        V.step(dve.tensor_scalar(poly, wc, 1.0 / 39916800, None, ALU.mult))
        for c in (1.0 / 362880, 1.0 / 5040, 1.0 / 120, 1.0 / 6):
            V.step(dve.scalar_tensor_tensor(poly, poly, c, wc, ALU.add, ALU.mult))
        V.step(dve.tensor_scalar(poly, poly, 1.0, None, ALU.add))
        V.wait(m)
        V.step(dve.reciprocal(ei, e))
        V.step(dve.reciprocal(n, n))
        V.step(dve.tensor_tensor(f, e, ei, ALU.subtract))
        V.step(dve.scalar_tensor_tensor(f, f, 0.5, n, ALU.mult, ALU.mult))
        V.step(dve.tensor_tensor(poly, poly, f, ALU.subtract))
        V.step(dve.tensor_tensor(poly, poly, less, ALU.mult))
        V.step(dve.tensor_tensor(f, f, poly, ALU.add))
        V.step(dve.tensor_tensor(e, e, ei, ALU.add))
        V.step(dve.tensor_scalar(e, e, 0.5, None, ALU.mult))
        fq = f.rearrange("p (t g h) -> p t g h", t=NT, g=2)[:, :, 0, :]
        V.step(dve.tensor_scalar(fq, fq, -1.0, None, ALU.mult))
        by8u = u.rearrange("p t (g e) -> p t g e", e=D)
        for t in range(NT):
            m = V.mark(dve.tensor_tensor(by8u[:, t, :, :], by8u[:, t, :, :],
                                         f.rearrange("p (t g) -> p t g", t=NT)[:, t, :].unsqueeze(2)
                                         .broadcast_to([P, 2 * H, D]), ALU.mult))
        V.wait(m)
        m = V.step(dve.tensor_copy(by8u[:, :, :, 0], e.rearrange("p (t g) -> p t g", t=NT)))
        va = ffn_w[:, 27 * 256:27 * 256 + NT * H * (D + 1)].rearrange("p (t h e) -> p t h e", t=NT, h=H)
        V.wait(*state["ffn_free"])
        V.step(dve.memset(va, 1.0))
        for t in range(NT):
            mv_ = V.mark(dve.tensor_copy(va[:, t, :, 0:D], qkv[:, t, 2 * E:3 * E].rearrange("p (h e) -> p h e", h=H)))
        A.wait(mv_)
        ms = A.mark(act.activation(spike[:], qkv[:, :, 3 * E], ACT.Exp, scale=-1.0))
        V.wait(ms)
        V.step(dve.tensor_scalar(spike[:], spike[:], 1.0, None, ALU.add))
        V.step(dve.reciprocal(spike[:], spike[:]))
        V.step(dve.tensor_scalar(spike[:], spike[:], rw("thr"), None, ALU.is_gt))
        kT = xn[:].rearrange("p t f -> p (t f)")
        done = {}
        for name, dst, off in (("q", qT[:], 0), ("k", kT, E)):
            done[name] = turn_tiles(qkv[:, :, off:off + E], dst, [m] * NT, NT)
        tq = queries("L1a", done["q"])
        tk = self_keys("L1a", kT, done["k"])
        PE.wait(tq.done(), tk.done())

        WIDE = S + P
        c_buf = Ring([Slot(wk(i * H * WIDE, H * WIDE).rearrange("p (h c) -> p h c", h=H)) for i in range(1)])
        s_buf = Ring([Slot(wk(H * WIDE, H * WIDE).rearrange("p (h c) -> p h c", h=H))])
        m1 = small

        def nearest(b):
            for h in range(H):
                p0, pair = head_slot(h)
                slot = one.take(PE)
                blocks = ((0, 0, P), (P, P, S))
                for q in range(TPB):
                    c0, k_n = (0, P) if q == 0 else (P, S)
                    pe.matmul(slot.ap[:, c0:c0 + k_n], q_stack[p0:p0 + K_SCORE - 1, b, pair, q * P:(q + 1) * P],
                              self_stack[p0:p0 + K_SCORE - 1, pair, b * S:b * S + k_n], start=True, stop=False,
                              skip_group_check=True)
                    m = PE.mark(pe.matmul(slot.ap[:, c0 + k_n - P:c0 + k_n], ident_b[:], far_b[:],
                                          start=False, stop=True, skip_group_check=True))
                V.wait(m)
                V.mark(dve.tensor_reduce(mx[:, b, h % 2, pair, 0:1], slot.ap[:, 0:P], AX, ALU.min))
                m = V.mark(dve.tensor_reduce(mx[:, b, h % 2, pair, 1:2], slot.ap[:, P:P + S], AX, ALU.min))
                slot.freed = (m,)
            c = mx[:, b, :, :, :].rearrange("p a h q -> p (a h q)")
            V.wait(m)
            m = V.step(dve.tensor_scalar(c, c, 1.0 + 1e-7, None, ALU.max))
            V.step(dve.tensor_tensor(m1[:, 0, :], c, c, ALU.mult))
            m = V.step(dve.tensor_scalar(m1[:, 0, :], m1[:, 0, :], -1.0, None, ALU.add))
            m = power(m1[:, 1, :], m1[:, 0, :], 0.5, m)
            V.wait(m)
            m = V.step(dve.tensor_tensor(m1[:, 2, :], c, m1[:, 1, :], ALU.add))
            A.wait(m)
            m = A.mark(act.activation(m1[:, 3, :], m1[:, 2, :], ACT.Ln))
            V.wait(m)
            V.step(dve.tensor_tensor(m1[:, 3, :], m1[:, 3, :], m1[:, 3, :], ALU.mult))
            return V.step(dve.tensor_scalar(c, m1[:, 3, :], RSQRT8, None, ALU.mult))

        for b in range(B):
            far = nearest(b)
            c, s_ = c_buf.take(V), s_buf.take(A)
            marks = []
            for h in range(H):
                p0, pair = head_slot(h)
                slot = one.take(PE)
                for k in range(TPB):
                    o = slot.ap[:, 0:S] if k == 0 else slot.ap[:, S:WIDE]
                    m = pe.matmul(o, self_stack[p0:p0 + ROW_MASK, pair, b * S + k * P:b * S + (k + 1) * P],
                                  q_stack[p0:p0 + ROW_MASK, b, pair, k * P:S], start=True, stop=True)
                m = PE.mark(m)
                V.wait(m)
                m = V.mark(dve.tensor_scalar(c.ap[:, h, :], slot.ap[:, 0:WIDE], 1.0 + 1e-7, None, ALU.max))
                slot.freed = (m,)
                marks.append(m)
            GR = 4
            groups = [slice(g, g + GR) for g in range(0, H, GR)]
            squared = []
            for gi, g in enumerate(groups):
                A.wait(marks[g.stop - 1])
                squared.append(A.mark(act.activation(s_.ap[:, g, :], c.ap[:, g, :], ACT.Square)))
            rooted = []
            for gi, g in enumerate(groups):
                A.wait(squared[gi])
                rooted.append(A.mark(act.activation(s_.ap[:, g, :], s_.ap[:, g, :], ACT.Sqrt, bias=minus1[:])))
            summed = []
            for gi, g in enumerate(groups):
                V.wait(rooted[gi])
                summed.append(V.mark(dve.tensor_tensor(c.ap[:, g, :], c.ap[:, g, :], s_.ap[:, g, :], ALU.add)))
            logs = []
            for gi, g in enumerate(groups):
                A.wait(summed[gi])
                logs.append(A.mark(act.activation(c.ap[:, g, :], c.ap[:, g, :], ACT.Ln)))
            dist = []
            for gi, g in enumerate(groups):
                A.wait(logs[gi])
                dist.append(A.mark(act.activation(s_.ap[:, g, :], c.ap[:, g, :], ACT.Square)))
            shifted = []
            for h in range(H):
                slot = one.take(PE)
                PE.wait(far)
                for q in range(TPB):
                    m = PE.mark(pe.transpose(slot.ap[:, q * P:(q + 1) * P],
                                             mx[:, b, h % 2, h // 2, q:q + 1].broadcast_to([P, P]), ident))
                V.wait(m, dist[h // GR])
                V.mark(dve.scalar_tensor_tensor(c.ap[:, h, 0:S], s_.ap[:, h, 0:S], -RSQRT8, slot.ap[:, 0:S],
                                                ALU.mult, ALU.add))
                m = V.mark(dve.scalar_tensor_tensor(c.ap[:, h, S:WIDE], s_.ap[:, h, S:WIDE], -RSQRT8,
                                                    slot.ap[:, P:S], ALU.mult, ALU.add))
                slot.freed = (m,)
                shifted.append(m)
            ready = []
            for gi, g in enumerate(groups):
                A.wait(shifted[g.stop - 1])
                m = A.mark(act.activation(c.ap[:, g, :], c.ap[:, g, :], ACT.Exp))
                G.wait(m)
                for lo in (0, S):
                    blk = c.ap[:, g, lo:lo + P]
                    m = G.mark(pool.affine_select(out=blk, in_=blk, compare_op=ALU.is_ge, fill=0.0, base=0,
                                                  pattern=[[0, GR], [1, P]], channel_multiplier=-1))
                ready.append(m)
            s_.freed = (shifted[-1],)
            acc = outs.take(PE)
            PE.wait(mv_)
            for h in range(H):
                PE.wait(ready[h // GR])
                cols = slice(h * (D + 1), (h + 1) * (D + 1))
                pe.matmul(acc.ap[:, 0, cols], c.ap[:, h, 0:P], va[:, b * TPB, h, :], start=True, stop=True)
                pe.matmul(acc.ap[:, 1, cols], c.ap[:, h, P:S], va[:, b * TPB, h, :], start=True, stop=False)
                m = pe.matmul(acc.ap[:, 1, cols], c.ap[:, h, S:WIDE], va[:, b * TPB + 1, h, :],
                              start=False, stop=True)
            last = PE.mark(m)
            c.freed = (last,)
            project_out(b, kp("L1a_out"), normalise(b, acc, last, spike))
        state["q_free"] = state["self_free"] = (last,)
        state["va1_free"] = (last,)

    def l2_attention():
        norm, ready = layer_norm(state["x"])
        W = 3 * E
        qkv = wk(0, NT * W).rearrange("p (t c) -> p t c", t=NT)
        G.wait(t_rows.done(), *norm)
        row = wk(12000, E)
        bg = G.mark(pool.tensor_tensor(row, rw("L2a_bout"), rw("L2a_lgamma"), ALU.mult))
        G.wait(bg)
        add_rows(row, norm)
        for t in range(NT):
            slot = one.take(PE)
            PE.wait(*ready)
            m = PE.mark(pe.matmul(slot.ap[:, 0:W], xnT[:, t * P:(t + 1) * P], kp("L2a_inT"), start=True, stop=True))
            V.wait(m)
            m = V.step(dve.tensor_tensor(qkv[:, t, :], slot.ap[:, 0:W], rw("L2a_bin"), ALU.add))
            slot.freed = (m,)
            qkv_ready = V.mark(dve.tensor_tensor(qkv[:, t, :], qkv[:, t, :], rw("L2a_gamma"), ALU.mult))
        V.wait(qkv_ready)
        for s in range(B):
            n = s + 1
            prod = wk(3200, n * TPB * E)
            sc = wk(3200 + 1024 + s * 128, n * TPB * H)
            q = qkv[:, s * TPB:(s + 1) * TPB, 0:E].unsqueeze(1).broadcast_to([P, n, TPB, E])
            k = qkv[:, 0:n * TPB, E:2 * E].rearrange("p (n q) f -> p n q f", q=TPB)
            V.step(dve.tensor_tensor(prod.rearrange("p (n q f) -> p n q f", n=n, q=TPB), q, k, ALU.mult))
            V.step(dve.tensor_reduce(sc, prod.rearrange("p (g e) -> p g e", e=D), AX, ALU.add))
            scn = sc.rearrange("p (n g) -> p n g", n=n)
            top = wk(6000 + s * 64, TPB * H)
            V.step(dve.tensor_reduce(top, sc.rearrange("p (n g) -> p g n", n=n), AX, ALU.max))
            m = V.step(dve.tensor_tensor(scn, scn, top.unsqueeze(1).broadcast_to([P, n, TPB * H]), ALU.subtract))
            A.wait(m)
            m = A.mark(act.activation(sc, sc, ACT.Exp, scale=RSQRT8))
            V.wait(m)
            V.step(dve.tensor_reduce(top, sc.rearrange("p (n g) -> p g n", n=n), AX, ALU.add))
            V.step(dve.reciprocal(top, top))
            v = qkv[:, 0:n * TPB, 2 * E:3 * E].rearrange("p t (h e) -> p t h e", e=D)
            for j in range(n * TPB):
                m = V.mark(dve.tensor_tensor(
                    prod[:, j * E:(j + 1) * E].rearrange("p (h e) -> p h e", e=D), v[:, j, :, :],
                    sc[:, j * H:(j + 1) * H].unsqueeze(2).broadcast_to([P, H, D]), ALU.mult))
            V.wait(m)
            o = wk(6400, TPB * E)
            V.step(dve.tensor_reduce(o, prod.rearrange("p (n g) -> p g n", n=n), AX, ALU.add))
            og = o.rearrange("p (g e) -> p g e", e=D)
            V.step(dve.tensor_tensor(og, og, top.unsqueeze(2).broadcast_to([P, TPB * H, D]), ALU.mult))
            m = V.step(dve.tensor_tensor(xn[:, s * TPB:(s + 1) * TPB, :], o.rearrange("p (q f) -> p q f", q=TPB),
                                         rw("L2a_alpha").unsqueeze(1).broadcast_to([P, TPB, E]), ALU.mult))
            project_out(s, kp("L2a_outT"), [m] * TPB, post=rw("L2a_lgamma"))

    def fp4(src, dst, n, ready, buf):
        nb = n // FP4_BLOCK
        a, mag, sgn, sc, rs = buf
        blk = lambda t: t.rearrange("p (b e) -> p b e", e=FP4_BLOCK)
        wide = lambda t: t.unsqueeze(2).broadcast_to([P, nb, FP4_BLOCK])
        V.wait(*ready)
        V.step(dve.tensor_reduce(sc, blk(src), AX, ALU.max, apply_absolute_value=True))
        V.step(dve.tensor_scalar(sc, sc, 1.0 / 6.0, 1e-12, ALU.mult, ALU.max))
        V.step(dve.reciprocal(rs, sc))
        m = V.step(dve.tensor_tensor(blk(mag), blk(src), wide(rs), ALU.mult))
        A.wait(m)
        m = A.mark(act.activation(sgn, mag, ACT.Sign))
        A.wait(m)
        m = A.mark(act.activation(mag, mag, ACT.Abs))
        V.wait(m)
        V.step(dve.tensor_scalar(a, mag, 5.0, 2.0, ALU.is_gt, ALU.mult))
        for mid in (3.5, 2.5):
            V.step(dve.scalar_tensor_tensor(a, mag, mid, a, ALU.is_gt, ALU.add))
        V.step(dve.tensor_scalar(a, a, 2.0, None, ALU.mult))
        for mid in (1.75, 1.25, 0.75, 0.25):
            V.step(dve.scalar_tensor_tensor(a, mag, mid, a, ALU.is_gt, ALU.add))
        V.step(dve.scalar_tensor_tensor(a, a, 0.5, sgn, ALU.mult, ALU.mult))
        return V.step(dve.tensor_tensor(blk(dst), blk(a), wide(sc), ALU.mult))

    def l2_ffn(t_w):
        NW = 2 * F2J * P + F2
        _, __ = layer_norm_only(state["x"])
        raw = ffn_w[:, 0:NW]
        gT, uT, dT = (ffn_w[:, NW + i * F2J * P:NW + (i + 1) * F2J * P] for i in range(3))
        N4 = 4 * F2
        bufs = lambda n: [wk(i * N4, n) for i in range(3)] + [wk(3 * N4, n // 16), wk(3 * N4 + 128, n // 16)]
        hbuf = wk(3 * N4 + 256, N4)
        m = fp4(raw, raw, NW, [t_w.done()], bufs(NW))
        for dst, off, rows_n in ((gT, 0, P), (uT, F2J * P, P), (dT, 2 * F2J * P, P)):
            slot = one.take(PE)
            PE.wait(m)
            for j in range(F2J):
                n = P if off < 2 * F2J * P else min(P, F2 - j * P)
                mm = PE.mark(pe.transpose(slot.ap[0:n, j * P:(j + 1) * P], raw[:, off + j * P:off + j * P + n], ident))
            V.wait(mm)
            if off < 2 * F2J * P:
                mm = V.mark(dve.tensor_copy(dst, slot.ap[:, 0:F2J * P]))
            else:
                V.mark(dve.tensor_copy(dst[:, 0:2 * P], slot.ap[:, 0:2 * P]))
                mm = V.mark(dve.tensor_copy(dst[0:F2 - 2 * P, 2 * P:3 * P], slot.ap[0:F2 - 2 * P, 2 * P:3 * P]))
            slot.freed = (mm,)
        PE.wait(mm)
        flat = xn[:].rearrange("p t f -> p (t f)")
        m = fp4(flat, flat, TOK, [], bufs(TOK))
        ready = turn_tiles(xn, xnT, [m] * NT, NT)
        for g in range(2):
            marks = []
            for i in range(4):
                t = 4 * g + i
                slot = six.take(PE)
                PE.wait(ready[g])
                pe.matmul(slot.ap[:, 0, 0:F2], xnT[:, t * P:(t + 1) * P], gT[:, 0:F2], start=True, stop=True)
                m = PE.mark(pe.matmul(slot.ap[:, 1, 0:F2], xnT[:, t * P:(t + 1) * P], uT[:, 0:F2],
                                      start=True, stop=True))
                h = hbuf[:, i * F2:(i + 1) * F2]
                A.wait(m, *state.get("hbuf", ()))
                m = A.mark(act.activation(h, slot.ap[:, 0, 0:F2], ACT.Silu))
                V.wait(m)
                m = V.mark(dve.tensor_tensor(h, h, slot.ap[:, 1, 0:F2], ALU.mult))
                slot.freed = (m,)
                marks.append(m)
            m = fp4(hbuf, hbuf, N4, marks, bufs(N4))
            for i in range(4):
                t = 4 * g + i
                slot = one.take(PE)
                PE.wait(m)
                for j in range(F2J):
                    n = min(P, F2 - j * P)
                    mm = PE.mark(pe.transpose(slot.ap[0:n, j * P:(j + 1) * P],
                                              hbuf[:, i * F2 + j * P:i * F2 + j * P + n], ident))
                hT = qT[:, (t % 2) * 512:(t % 2) * 512 + 384]
                A.wait(mm)
                A.mark(act.copy(hT[:, 0:2 * P], slot.ap[:, 0:2 * P]))
                mm = A.mark(act.copy(hT[0:F2 - 2 * P, 2 * P:3 * P], slot.ap[0:F2 - 2 * P, 2 * P:3 * P]))
                slot.freed = (mm,)
                slot = one.take(PE)
                PE.wait(mm)
                for j in range(F2J):
                    n = min(P, F2 - j * P)
                    mm = pe.matmul(slot.ap[:, 0:E], hT[0:n, j * P:(j + 1) * P], dT[0:n, j * P:(j + 1) * P],
                                   start=(j == 0), stop=(j == F2J - 1))
                mm = PE.mark(mm)
                V.wait(mm)
                mm = V.mark(dve.tensor_tensor(x[:, t, :], slot.ap[:, 0:E], x[:, t, :], ALU.add))
                slot.freed = (mm,)
                state["x"][t] = mm
            state["hbuf"] = (mm,)

    def layer_norm_only(x_marks):
        for t in range(NT):
            V.wait(x_marks[t])
            m = V.mark(dve.bn_stats(stats[:, t, :], x[:, t, :]))
        V.wait(m)
        for t in range(NT):
            m = V.mark(dve.bn_aggr(mv[:, t, :], stats[:, t, :]))
        V.wait(m)
        m = V.step(dve.tensor_scalar(rstd[:], mv[:, :, 1], LN_EPS, None, ALU.add))
        V.wait(power(rstd[:], rstd[:], -0.5, m))
        marks = [V.mark(dve.tensor_scalar(xn[:, t, :], x[:, t, :], mv[:, t, 0:1], rstd[:, t:t + 1],
                                          ALU.subtract, ALU.mult)) for t in range(NT)]
        V.wait(*marks)
        return marks, None

    def l3_attention():
        _, ready = layer_norm(state["x"])
        gram = wk(0, B * E).rearrange("p (b f) -> p b f", b=B)
        mix = wk(B * E, B * E).rearrange("p (b f) -> p b f", b=B)
        slot = one.take(PE)
        PE.wait(*ready)
        for b in range(B):
            for q in range(TPB):
                t = b * TPB + q
                m = pe.matmul(slot.ap[:, b * E:(b + 1) * E], xn[:, t, :], xn[:, t, :], start=(q == 0), stop=(q == TPB - 1))
        m = PE.mark(m)
        V.wait(m)
        m = V.mark(dve.tensor_copy(gram, slot.ap[:].rearrange("p (b f) -> p b f", b=B)))
        slot.freed = (m,)
        slot = one.take(PE)
        PE.wait(m)
        for b in range(B):
            m = PE.mark(pe.matmul(slot.ap[:, b * E:(b + 1) * E], kp("L3a_q"), gram[:, b, :], start=True, stop=True))
        V.wait(m)
        m = V.mark(dve.tensor_copy(mix, slot.ap[:].rearrange("p (b f) -> p b f", b=B)))
        slot.freed = (m,)
        for g in range(2):
            slot = one.take(PE)
            PE.wait(m)
            for i in range(4):
                t = 4 * g + i
                mm = PE.mark(pe.matmul(slot.ap[:, i * P:(i + 1) * P], xnT[:, t * P:(t + 1) * P], mix[:, t // TPB, :],
                                       start=True, stop=True))
            V.wait(mm)
            xs = x[:, 4 * g:4 * g + 4, :]
            mm = V.mark(dve.tensor_tensor(xs, slot.ap[:].rearrange("p (t f) -> p t f", t=4), xs, ALU.add))
            slot.freed = (mm,)
            for i in range(4):
                state["x"][4 * g + i] = mm

    def l3_cross(t_mask):
        norm, ready = layer_norm(state["x"])
        raw = self_stack[:].rearrange("p h t -> p (h t)").bitcast(I32)[:, 0:NT * S2 // 4].rearrange("p (t k) -> p t k", t=NT)
        V.wait(t_mask.done())
        V.step(dve.tensor_reduce(cm[:], raw, AX, ALU.max))
        V.step(dve.tensor_scalar(cm[:], cm[:], 3e38, 3e38, ALU.mult, ALU.mult))
        V.wait(*norm, *ready)
        for t in range(NT):
            m_res = V.mark(dve.scalar_tensor_tensor(xn[:, t, :], xn[:, t, :], cm[:, t:t + 1], rw("L3x_bo"),
                                                    ALU.add, ALU.add))
        q_in = feature_major(qT, kp("L3x_qT"), xnT, ready, TOK, bias=kp("L3x_bq"))
        PE.wait(state["kv3"])
        marks = []
        for g in range(2):
            slot = one.take(PE)
            PE.wait(q_in[g], m_res)
            for i in range(2):
                b = 2 * g + i
                m = PE.mark(pe.matmul(slot.ap[:, i * S:(i + 1) * S], kv3[:, b, :], qT[:, b * S:(b + 1) * S],
                                      start=True, stop=True))
            m = evacuate(1, xnT[:, g * 512:(g + 1) * 512], slot.ap[:], m)
            slot.freed = (m,)
            slot = one.take(PE)
            PE.wait(m)
            for i in range(4):
                t = 4 * g + i
                m = PE.mark(pe.matmul(slot.ap[:, i * P:(i + 1) * P], xnT[:, t * P:(t + 1) * P], kp("L3x_oT"),
                                      start=True, stop=True))
            V.wait(m, m_res)
            xs = xn[:, 4 * g:4 * g + 4, :]
            m = V.mark(dve.tensor_tensor(xs, slot.ap[:].rearrange("p (t f) -> p t f", t=4), xs, ALU.add))
            slot.freed = (m,)
            marks += [m] * 4
        for t in range(NT):
            V.wait(marks[t])
            m = V.mark(dve.bn_stats(stats[:, t, :], xn[:, t, :]))
        V.wait(m)
        for t in range(NT):
            m = V.mark(dve.bn_aggr(mv[:, t, :], stats[:, t, :]))
        V.wait(m)
        m = V.step(dve.tensor_scalar(rstd[:], mv[:, :, 1], LN_EPS, None, ALU.add))
        V.wait(power(rstd[:], rstd[:], -0.5, m))
        for t in range(NT):
            V.step(dve.tensor_scalar(xn[:, t, :], xn[:, t, :], mv[:, t, 0:1], rstd[:, t:t + 1], ALU.subtract, ALU.mult))
        wide = lambda n: rw(n).unsqueeze(1).broadcast_to([P, NT, E])
        V.step(dve.tensor_tensor(xn[:], xn[:], wide("L3x_g"), ALU.mult))
        V.step(dve.tensor_tensor(xn[:], xn[:], wide("L3x_b"), ALU.add))
        m = V.step(dve.tensor_tensor(x[:], x[:], xn[:], ALU.add))
        state["x"] = [m] * NT

    def b1_of(name, e, j):
        return kp(name, e * FJ + j, 1) if e < NE else kp("L0f_bs1", j, 1)

    def run():
        t_c, t_kx, again = prepare_context()
        state["c_done"], state["kx_done"] = t_c.done(), t_kx.done()
        state["ctx_free"] = (again,)
        l0_attention()
        if stop_after == "L0a":
            return
        t_w0 = load_ffn("w0", [d["L0f_w"][:, :]])
        t_cs = load_ctx_stack("c0", 0, c_scr, t_c, 0)
        add_mask = prepare_mask()
        cross("L0x", kp("L0x_fcT"), "L0x_b", t_cs, state["va0"], RSQRT128, add_mask=add_mask)
        t_cs = load_ctx_stack("c1", 1, kx_scr, t_kx, 1)
        t_va = load_values("v1", 1)
        if stop_after == "L0x":
            return
        gelu_experts("L0f", kp("L0f_router"), None, NE + 1, 9 * FH, lambda e, j: b1_of("L0f_b1", e, j), t_w0, 0,
                     NE + 1, ffn_w)
        t_w1 = load_ffn("w1", [d["L1f_w"][:, :]])
        if stop_after == "L0f":
            return
        l1_attention()
        if stop_after == "L1a":
            return
        cross("L1x", kp("L1x_oT"), "L1x_bo", t_cs, t_va.done(), RSQRT8, project="L1x_qT")
        t_cs = load_ctx_stack("c2", 0, c_scr, t_c, 0)
        t_va = load_values("v2", 0)
        t_mask = transfers("mask3")
        Q.wait(*state["self_free"])
        t_mask.start(Q, self_stack[:].rearrange("p h t -> p (h t)").bitcast(I32)[:, 0:NT * S2 // 4]
                     .rearrange("p (t k) -> p t k", t=NT), d["mask_L3"].rearrange("b o (j p) k -> p (b o j) k", p=P))
        if stop_after == "L1x":
            return
        swiglu_experts(t_w1)
        t_w2 = load_ffn("w2", [d["L2f_w"][:, :]])
        if stop_after == "L1f":
            return
        l2_attention()
        if stop_after == "L2a":
            return
        cross("L2x", kp("L2x_T"), None, t_cs, t_va.done(), RSQRT8)
        w3 = ctx_stack[:].rearrange("p h t -> p (h t)").bitcast(F32)
        t_w3 = transfers("w3")
        Q.wait(*state["ctx_free"])
        t_w3.start(Q, w3, d["L3f_w"][:, :])
        if stop_after == "L2x":
            return
        l2_ffn(t_w2)
        if stop_after == "L2f":
            return
        l3_attention()
        if stop_after == "L3a":
            return
        l3_cross(t_mask)
        if stop_after == "L3x":
            return
        gelu_experts("L3f", kp("L3f_router"), 1e-8, NE, NE * FH, lambda e, j: b1_of("L3f_b1", e, j), t_w3, 1, NE, w3)

    run()
    finish_out()


def shape_constants():
    k = np.arange(P)
    ident = np.eye(P, dtype=np.float32)
    blockdiag = (k[:, None] // D == k[None, :] // D).astype(np.float32)
    far = np.where(k[None, :] > k[:, None], np.float32(BIG), np.float32(0))
    rev = np.broadcast_to(np.arange(NE, 0, -1, dtype=np.float32), (P, NE))
    f32 = np.float32
    inv = f32(1.0) / f32(10000.0) ** (np.arange(0, D, 2, dtype=np.float32) / f32(D))
    pos = np.arange(S, dtype=np.float32)
    freqs = np.repeat(pos[:, None] * inv[None, :], 2, axis=-1)
    sv = (np.arange(0, D, 2, dtype=np.float32) + f32(0.4 * D)) / f32(1.4 * D)
    scale = sv[None, :] ** ((pos - S // 2) / f32(512.0))[:, None]
    scale = np.concatenate([scale, scale], axis=-1)
    sign = np.where(np.arange(D) % 2 == 0, f32(-1), f32(1))
    cos, sin = np.cos(freqs), np.sin(freqs) * sign
    tables = [cos * scale * D ** -0.5, sin * scale * D ** -0.5, cos / scale, sin / scale]
    tables = [np.tile(t.T.astype(np.float32), (H, 1)) for t in tables]
    return ident, blockdiag, far, rev, tables


def lay_out(inp):
    g = lambda n: np.asarray(inp[n])
    ident, blockdiag, far, rev, tables = shape_constants()

    def fill(at, n, parts):
        out = np.zeros((P, n), np.float32)
        assert set(parts) == set(at)
        for name, a in parts.items():
            lo, w = at[name]
            assert a.shape == (P, w), (name, a.shape, w)
            out[:, lo:lo + w] = a
        return out

    col = lambda a: a.reshape(-1, P).T
    keep = fill(KEEP_AT, KEEP_N, {
        "ident": ident, "blockdiag": blockdiag, "rev": rev,
        "L0x_fcT": g("L0_xattn_W_fc").T, "L0f_router": g("L0_ffn_w_router").T,
        "L1a_qkv": np.concatenate([g("L1_attn_W_qkv"), g("L1_attn_w_sur")[:, None]], 1),
        "L1a_out": g("L1_attn_W_out"), "L1x_qT": g("L1_xattn_Wq").T, "L1x_kT": g("L1_xattn_Wk").T,
        "L1x_vT": g("L1_xattn_Wv").T, "L1x_oT": g("L1_xattn_Wo").T, "L1f_router": g("L1_ffn_Wr"),
        "L2a_inT": g("L2_attn_in_proj_weight").T, "L2a_outT": g("L2_attn_out_proj_weight").T,
        "L2x_T": g("L2_xattn_w_concat").T, "L3a_q": g("L3_attn_queries"),
        "L3x_qT": g("L3_xattn_wq_w").T,
        "L3x_kvT": np.concatenate([g("L3_xattn_wk_w").T, g("L3_xattn_wv_w").T], 1),
        "L3x_oT": g("L3_xattn_wo_w").T, "L3f_router": g("L3_ffn_router_w").T,
        "L0f_b1": col(g("L0_ffn_b1")), "L0f_bs1": col(g("L0_ffn_bs1")), "L3f_b1": col(g("L3_ffn_b1")),
        "L1x_bq": g("L1_xattn_bq")[:, None], "L1x_bk": g("L1_xattn_bk")[:, None], "L3x_bq": g("L3_xattn_wq_b")[:, None],
    })
    swap = np.arange(E) ^ 1
    wq, wk_ = g("L0_attn_Wq").T, g("L0_attn_Wk").T
    l0a = fill(L0A_AT, L0A_N, {
        "qT": wq, "qpT": wq[:, swap], "kT": wk_, "kpT": wk_[:, swap], "vT": g("L0_attn_Wv").T,
        "oT": g("L0_attn_Wo").T, "qcos": tables[0], "qsin": tables[1], "kcos": tables[2], "ksin": tables[3]})
    r = {
        "L0x_b": g("L0_xattn_b_fc"), "L1a_bqkv": np.concatenate([g("L1_attn_b_qkv"), g("L1_attn_b_sur")[None]]),
        "L1a_bout": g("L1_attn_b_out"), "L1x_bv": g("L1_xattn_bv"), "L1x_bo": g("L1_xattn_bo"),
        "L2a_bin": g("L2_attn_in_proj_bias"), "L2a_gamma": g("L2_attn_gamma")[0, 0],
        "L2a_alpha": g("L2_attn_linear_alpha")[0, 0], "L2a_bout": g("L2_attn_out_proj_bias"),
        "L2a_lgamma": g("L2_attn_linear_gamma")[0, 0],
        "L3x_bkv": np.concatenate([g("L3_xattn_wk_b"), g("L3_xattn_wv_b")]), "L3x_bo": g("L3_xattn_wo_b"),
        "L3x_g": g("L3_xattn_ln_g"), "L3x_b": g("L3_xattn_ln_b"),
        "lq1": g("L0_attn_lambda_q1"), "lk1": g("L0_attn_lambda_k1"), "lq2": g("L0_attn_lambda_q2"),
        "lk2": g("L0_attn_lambda_k2"), "thr": g("L1_attn_threshold")[None],
    }
    rows = np.zeros((1, ROW_N), np.float32)
    for name, a in r.items():
        lo, w = ROW_AT[name]
        rows[0, lo:lo + w] = a

    def up(w):
        return w.transpose(2, 0, 1).reshape(E, -1)

    def dn(w):
        e, dd, f = w.shape
        return w.transpose(0, 2, 1).reshape(e, f // P, P, dd).transpose(2, 0, 1, 3).reshape(P, -1)

    def pad(w):
        a = np.zeros((F2J * P, E), np.float32)
        a[:F2] = w
        return a.reshape(F2J, P, E).transpose(1, 0, 2).reshape(P, -1)

    all0 = np.concatenate([g("L0_ffn_W1"), g("L0_ffn_Ws1")[None]]), np.concatenate([g("L0_ffn_W2"), g("L0_ffn_Ws2")[None]])
    l1 = [np.concatenate([g("L1_ffn_" + a), g("L1_ffn_" + b)[None]]) for a, b in (("Wg", "Sg"), ("Wu", "Su"), ("Wd", "Sd"))]
    arrays = {
        "const_bf16": np.stack([ident, far, np.zeros_like(ident)]).astype(mybir.dt.np(BF16)),
        "x": g("x"), "ctx_1024": g("ctx_1024"), "keep": keep, "l0a": l0a, "rows": rows,
        "mask_L0": g("mask_Bx1xSxS2_ik1"), "mask_keys": g("mask_BxS2_bf1").view(np.uint8),
        "mask_L3": g("mask_Bx1xSxS2_bf0").view(np.int32),
        "b2_L0": np.concatenate([g("L0_ffn_b2"), g("L0_ffn_bs2")[None]]), "b2_L3": g("L3_ffn_b2"),
        "L0f_w": np.concatenate([up(all0[0]), dn(all0[1])], 1),
        "L1f_w": np.concatenate([up(l1[0].transpose(0, 2, 1)), up(l1[1].transpose(0, 2, 1)),
                                 dn(l1[2].transpose(0, 2, 1))], 1),
        "L2f_w": np.concatenate([pad(g("L2_ffn_w_gate")), pad(g("L2_ffn_w_up")), g("L2_ffn_w_down")], 1),
        "L3f_w": np.concatenate([up(g("L3_ffn_w1")), dn(g("L3_ffn_w2"))], 1),
    }
    return {n: np.ascontiguousarray(a) for n, a in arrays.items()}


STOP_AFTER = "L3f"


def kernel(**inputs):
    import concourse.bacc as bacc
    from concourse.bass_utils import run_bass_kernel_spmd

    nc = bacc.Bacc("TRN2", target_bir_lowering=False, num_devices=1)
    arrays = lay_out(inputs)
    d = {n: nc.dram_tensor("in_" + n, a.shape, mybir.dt.from_np(a.dtype), kind="ExternalInput").ap()
         for n, a in arrays.items()}
    out = nc.dram_tensor("out_x", (B, S, E), F32, kind="ExternalOutput").ap()
    decoder(nc, d, out, STOP_AFTER)
    r = run_bass_kernel_spmd(nc, [{"in_" + n: a for n, a in arrays.items()}], core_ids=[0])
    return r.results[0]["out_x"]
```

```python
from collections import deque
from contextlib import ExitStack

import numpy as np
import concourse.bass as bass
from concourse import mybir

ALU = mybir.AluOpType
ACT = mybir.ActivationFunctionType
AX = mybir.AxisListType.X
F32 = mybir.dt.float32
BF16 = mybir.dt.bfloat16
I32 = mybir.dt.int32
U8 = mybir.dt.uint8

P = 128
B, S, S2, E = 4, 256, 512, 128
H, D = 16, 8
TPB = S // P
NT = B * TPB
NC = B * S2 // P
TOK = B * S
CTX = B * S2
PAIRS = H // 2
SLOT = 64
COLS = 32
GROUP = P // COLS
PARTS = [(0, 0), (1, 0), (2, 0), (0, 1), (1, 1), (0, 2)]
QUERY_RUNS = [(0, 3), (3, 2), (5, 1)]
ROW_MASK = len(PARTS) * D
ROW_MAX = ROW_MASK + 1
K_SCORE = ROW_MASK + 1
K_EXP = ROW_MAX + 3
TWO_ONES = float(np.array([0x3F803F80], np.uint32).view(np.float32)[0])
BIG = float(2 ** 66)
LN_EPS = 1e-5
NE = 8
FH = 512
FJ = FH // P
F1 = 256
F1J = F1 // P
F2 = 352
F2J = (F2 + P - 1) // P
FP4_BLOCK = 16
VA = H * (D + 1)
WARM = 16
SLOW = 3
LEAD = 2
DV0 = 16
H0 = 8
LAMBDA_INIT = 0.8 - 0.6 * float(np.exp(-0.3))
MOE_SCALE = 1.0 / float(np.sqrt(1 + 2 / NE))
RSQRT8 = 1.0 / float(np.sqrt(8.0))
RSQRT128 = 1.0 / float(np.sqrt(128.0))
DK3 = float(np.float32(np.sqrt(np.float16(8.0)))) + 1e-8


def columns(parts):
    at, n = {}, 0
    for name, width in parts:
        at[name] = (n, width)
        n += width
    return at, n


KEEP_AT, KEEP_N = columns([
    ("ident", P), ("blockdiag", P), ("rev", NE),
    ("L0x_fcT", E), ("L0f_router", NE), ("L1a_qkv", 3 * E + 1), ("L1a_out", E),
    ("L1x_qT", E), ("L1x_kT", E), ("L1x_vT", E), ("L1x_oT", E), ("L1f_router", NE),
    ("L2a_inT", 3 * E), ("L2a_outT", E), ("L2x_T", E), ("L3a_q", E),
    ("L3x_qT", E), ("L3x_kvT", 2 * E), ("L3x_oT", E), ("L3f_router", NE),
    ("L0f_b1", NE * FJ), ("L0f_bs1", FJ), ("L3f_b1", NE * FJ),
    ("L1x_bq", 1), ("L1x_bk", 1), ("L3x_bq", 1),
])
L0A_AT, L0A_N = columns([("qT", E), ("qpT", E), ("kT", E), ("kpT", E), ("vT", E), ("oT", E),
                         ("qcos", S), ("qsin", S), ("kcos", S), ("ksin", S)])
ROW_AT, ROW_N = columns([
    ("L0x_b", E), ("L1a_bqkv", 3 * E + 1), ("L1a_bout", E), ("L1x_bv", E), ("L1x_bo", E),
    ("L2a_bin", 3 * E), ("L2a_gamma", 3 * E), ("L2a_alpha", E), ("L2a_bout", E), ("L2a_lgamma", E),
    ("L3x_bkv", 2 * E), ("L3x_bo", E), ("L3x_g", E), ("L3x_b", E),
    ("lq1", D), ("lk1", D), ("lq2", D), ("lk2", D), ("thr", 1),
])
FFN_N = 9 * FH + 9 * FJ * E


class Lane:

    def __init__(self, engine, sem):
        self.engine, self.sem, self.count, self.seen = engine, sem, 0, {}

    def mark(self, instruction):
        instruction.then_inc(self.sem, 1)
        self.count += 1
        return (self.sem, self.count)

    def wait(self, *marks):
        for sem, value in marks:
            if self.seen.get(id(sem), 0) < value:
                self.engine.wait_ge(sem, value)
                self.seen[id(sem)] = value

    def step(self, instruction):
        m = self.mark(instruction)
        self.wait(m)
        return m


class Transfers:

    def __init__(self, sem):
        self.sem, self.count = sem, 0

    def start(self, lane, dst, src):
        lane.engine.dma_start(dst, src).then_inc(self.sem, 16)
        self.count += 16

    def done(self):
        return (self.sem, self.count)


class Slot:

    def __init__(self, ap):
        self.ap, self.freed = ap, ()


class Ring:
    def __init__(self, slots):
        self.slots, self.n = slots, 0

    def held(self):
        return self.slots[self.n % len(self.slots)].freed is None

    def take(self, lane):
        slot = self.slots[self.n % len(self.slots)]
        self.n += 1
        lane.wait(*slot.freed)
        slot.freed = None
        return slot


def decoder(nc, d, out):
    with ExitStack() as ctx:
        build(nc, d, out, ctx)


def build(nc, d, out, ctx):
    def sb(name, shape, dt=F32):
        return ctx.enter_context(nc.sbuf_tensor(name, shape, dt))

    every_transfer = []

    def transfers(name):
        t = Transfers(ctx.enter_context(nc.semaphore("dma_" + name)))
        every_transfer.append(t)
        return t

    def lane(engine, name):
        return Lane(engine, ctx.enter_context(nc.semaphore(name)))

    pe, dve, act, pool, sp = nc.tensor, nc.vector, nc.scalar, nc.gpsimd, nc.sync
    PE, V, A, G, Q = (lane(pe, "pe_done"), lane(dve, "dve_done"), lane(act, "act_done"),
                      lane(pool, "pool_done"), lane(sp, "sp_done"))

    x = sb("x", [P, NT, E])
    xn = sb("xn", [P, NT, E])
    xnT = sb("xnT", [P, TOK])
    qT = sb("qT", [P, TOK])
    q_stack = sb("q_stack", [P, B, PAIRS, S], BF16)
    self_stack = sb("self_stack", [P, PAIRS, TOK], BF16)
    ctx_stack = sb("ctx_stack", [P, PAIRS, CTX], BF16)
    parts = sb("parts", [P, 3, TOK], BF16)
    ffn_w = sb("ffn_w", [P, FFN_N])
    keep = sb("keep", [P, KEEP_N])
    rows = sb("rows", [P, ROW_N])
    vaug_pad = sb("vaug", [P, NC * VA + COLS])
    vaug = vaug_pad[:, 0:NC * VA].rearrange("p (t c) -> p t c", t=NC)
    work = sb("work", [P, 12288])
    kv3 = sb("kv3", [P, B, E])
    ident_b = sb("ident_b", [P, P], BF16)
    far_b = sb("far_b", [P, P], BF16)
    stats = sb("stats", [P, NT, 6])
    mv = sb("mv", [P, NT, 2])
    rstd = sb("rstd", [P, NT])
    mx = sb("mx", [P, B, 2, PAIRS, TPB])
    mparts = sb("mparts", [P, 3, 2 * TPB * PAIRS], BF16)
    mT = sb("mT", [96, B, P], BF16)
    rsum = sb("rsum", [P, 2, TPB, GROUP])
    gates = sb("gates", [P, NT, NE + 1])
    gatesT = parts[:].rearrange("p s t -> p (s t)").bitcast(F32)[0:NE + 1, 0:TOK]
    b2 = sb("b2", [NE + 1, 2, E])
    small = sb("small", [P, 4, 2 * TPB * PAIRS])
    lam = sb("lam", [P, 8])
    lam8 = sb("lam8", [P, 2, D])
    l0a_ss = sb("l0a_ss", [P, TPB * H0])
    bq_scaled = sb("bq_scaled", [P, 1])
    minus1 = sb("minus1", [P, 1])
    halves = sb("halves", [P, 2])
    maskrow = sb("maskrow", [NC, P], BF16)
    masku8 = sb("masku8", [NC, P], U8)
    spike = sb("spike", [P, NT])
    cm = sb("cm", [P, NT])

    def kp(name, lo=0, n=None):
        a, w = KEEP_AT[name]
        return keep[:, a + lo:a + lo + (w - lo if n is None else n)]

    def rw(name):
        a, w = ROW_AT[name]
        return rows[:, a:a + w]

    def l0w(name):
        a, w = L0A_AT[name]
        return ffn_w[:, a:a + w]

    def wk(lo, n):
        return work[:, lo:lo + n]

    outT = wk(12288 - 2 * S, 2 * S).rearrange("p (g t) -> p g t", g=2)

    ps_a = [ctx.enter_context(nc.psum_tensor(f"ps_a{i}", [P, 512], F32)) for i in range(2)]
    ps_t = [ctx.enter_context(nc.psum_tensor(f"ps_t{i}", [P, 2, 512], F32)) for i in range(2)]
    ps_v = ctx.enter_context(nc.psum_tensor("ps_v", [P, 512], F32))
    ps_m = ctx.enter_context(nc.psum_tensor("ps_m", [P, 2, S], F32))
    one = Ring([Slot(t[:]) for t in ps_a])
    two = Ring([Slot(t[:]) for t in ps_t])
    outs = Ring([Slot(ps_v[:, 0:S])])
    misc = Ring([Slot(ps_m[:, 0, :])])

    q_scr = nc.dram_tensor("q_scr", (H, 3, D, TOK), BF16)
    k_scr = nc.dram_tensor("k_scr", (H, 3, D, TOK), BF16)
    c_scr = nc.dram_tensor("c_scr", (H, 3, D, CTX), BF16)
    kx_scr = nc.dram_tensor("kx_scr", (H, 3, D, CTX), BF16)
    m_scr = nc.dram_tensor("m_scr", (2, NC, P), BF16)
    v_scr = nc.dram_tensor("v_scr", (2, P, NC * H * (D + 1)), F32)

    t_x, t_keep, t_rows, t_l0a, t_ctx, t_mk = (transfers(n) for n in ("x", "keep", "rows", "l0a", "ctx", "mk"))
    t_b2, t_bf = transfers("b2"), transfers("bf")
    t_x.start(Q, x[:], d["x"].rearrange("b (j p) f -> p (b j) f", p=P))
    t_l0a.start(Q, ffn_w[:, 0:L0A_N], d["l0a"][:, :])
    t_keep.start(Q, keep[:], d["keep"][:, :])
    t_ctx.start(Q, wk(0, 2048).rearrange("p (t f) -> p t f", t=NC), d["ctx_1024"].rearrange("b (j p) f -> p (b j) f", p=P))
    t_bf.start(Q, ident_b[:], d["const_bf16"][0])
    t_bf.start(Q, far_b[:], d["const_bf16"][1])
    t_rows.start(Q, rows[:], d["rows"][0:1, :].broadcast_to([P, ROW_N]))
    t_mk.start(Q, masku8[:], d["mask_keys"].rearrange("b (j p) -> (b j) p", p=P))
    t_b2.start(Q, b2[:, 0, :], d["b2_L0"][:, :])
    t_b2.start(Q, b2[0:NE, 1, :], d["b2_L3"][:, :])

    G.mark(pool.memset(halves[:, 0:1], -0.5))
    G.mark(pool.memset(halves[:, 1:2], 0.5))
    q_set = V.mark(dve.memset(q_stack[:].bitcast(F32), TWO_ONES))
    self_set = V.mark(dve.memset(self_stack[:].bitcast(F32), TWO_ONES))
    va0_set = V.mark(dve.memset(ffn_w[:, L0A_N:L0A_N + NT * H0 * (DV0 + 1) + COLS], 1.0))
    vaug_set = G.mark(pool.memset(vaug_pad[:], 1.0))
    vx_set = G.mark(pool.memset(wk(6144, 8 * VA), 1.0))
    V.mark(dve.memset(minus1[:], -1.0))
    V.mark(dve.memset(gates[:], MOE_SCALE))
    V.wait(t_keep.done())
    PE.wait(t_keep.done(), t_bf.done())
    A.wait(t_keep.done())
    ident = kp("ident")

    V.mark(dve.tensor_scalar(bq_scaled[:], kp("L1x_bq"), RSQRT8, None, ALU.mult))
    A.wait((V.sem, V.count))
    V.wait(t_mk.done())
    m_mask = V.mark(dve.tensor_scalar(maskrow[:], masku8[:], -1.0, BIG, ALU.add, ALU.mult))

    V.wait(t_rows.done())
    for i, (a, b_) in enumerate((("lq1", "lk1"), ("lq2", "lk2"))):
        V.step(dve.tensor_tensor(lam8[:, i, :], rw(a), rw(b_), ALU.mult))
        lam_sum = V.step(dve.tensor_reduce(lam[:, i:i + 1], lam8[:, i, :], AX, ALU.add))
    A.wait(lam_sum)
    lam_exp = A.mark(act.activation(lam[:, 2:4], lam[:, 0:2], ACT.Exp))
    V.wait(lam_exp)
    V.step(dve.tensor_tensor(lam[:, 4:5], lam[:, 3:4], lam[:, 2:3], ALU.subtract))
    V.step(dve.tensor_scalar(lam[:, 5:6], lam[:, 4:5], -LAMBDA_INIT, None, ALU.add))

    background = deque()

    def spawn(task):
        background.append(task)
        return task

    slow, turns = [], [0]

    def tick(urgent=False):
        turns[0] += 1
        for task in list(background):
            if task in slow and turns[0] % (8 if urgent else SLOW):
                continue
            if next(task, "end") == "end":
                background.remove(task)

    def claim(ring, lane_):
        while ring.held():
            yield
        return ring.take(lane_)

    def warm(n):
        slot = take(outs, PE)
        for _ in range(n):
            m = pe.matmul(ps_v[:], ident_b[:], far_b[:].unsqueeze(1).broadcast_to([P, 4, P]),
                          start=True, stop=True)
        slot.freed = (PE.mark(m),)

    def take(ring, lane_):
        while ring.held():
            tick(urgent=True)
        return ring.take(lane_)

    room_held = set()

    def hold(room):
        while room in room_held:
            yield
        room_held.add(room)

    release = room_held.remove

    def finish(task):
        while task in background:
            tick(urgent=task not in slow)

    def await_prologue(b):
        while b not in prologue_done:
            tick(urgent=True)
        finish(prologue_done.pop(b))

    def evacuate(turn, dst, src, ready):
        if turn % 2:
            A.wait(ready)
            return A.mark(act.copy(dst, src))
        V.wait(ready)
        return V.mark(dve.tensor_copy(dst, src))

    lifter = [A]

    def lift(dst, src, ready, scale=1.0):
        lifter[0].wait(*ready)
        if lifter[0] is A:
            return A.mark(act.activation(dst, src, ACT.Copy, scale=scale))
        return V.mark(dve.tensor_scalar(dst, src, scale, None, ALU.mult))

    def power(dst, src, exponent, ready):
        e = halves[:, 0:1] if exponent < 0 else halves[:, 1:2]
        G.wait(ready)
        return G.mark(pool.tensor_tensor(dst, src, e.broadcast_to(list(src.shape)), ALU.pow))

    def tiles(b):
        return range(b * TPB, (b + 1) * TPB)

    def cols(b):
        return slice(b * S, (b + 1) * S)

    xn_ready, xnT_ready, prologue_done = {}, {}, {}

    def statistics(src, b):
        for t in tiles(b):
            m = V.mark(dve.bn_stats(stats[:, t, :], src[:, t, :]))
        V.wait(m)
        for t in tiles(b):
            m = V.mark(dve.bn_aggr(mv[:, t, :], stats[:, t, :]))
        V.wait(m)
        r = rstd[:, b * TPB:(b + 1) * TPB]
        m = V.mark(dve.tensor_scalar(r, mv[:, b * TPB:(b + 1) * TPB, 1], LN_EPS, None, ALU.add))
        return power(r, r, -0.5, m)

    def normalised(src, b, rooted):
        V.wait(rooted)
        for t in tiles(b):
            m = V.mark(dve.tensor_scalar(xn[:, t, :], src[:, t, :], mv[:, t, 0:1], rstd[:, t:t + 1],
                                         ALU.subtract, ALU.mult))
        return m

    def norm(b, bias_row=None, turn=True, dst=None, scale=1.0):
        V.wait(state["x"][b])
        m = statistics(x, b)
        yield
        xn_ready[b] = m = normalised(x, b, m)
        bias_added[b] = ()
        if bias_row is not None:
            G.wait(m)
            for t in tiles(b):
                g = G.mark(pool.tensor_tensor(x[:, t, :], x[:, t, :], bias_row, ALU.add))
            bias_added[b] = (g,)
        if turn:
            yield
            yield from turn_batch(b, xn, xnT if dst is None else dst, m, scale)

    def turn_batch(b, src, dst, ready, scale=1.0):
        slot = yield from claim(misc, PE)
        PE.wait(ready)
        for i, t in enumerate(tiles(b)):
            m = PE.mark(pe.transpose(slot.ap[:, i * P:(i + 1) * P], src[:, t, :], ident))
        yield
        xnT_ready[b] = m = lift(dst[:, cols(b)], slot.ap, [m], scale)
        slot.freed = (m,)

    def project_batch(b, dst, w, bias, scale, ready):
        slot = yield from claim(misc, PE)
        PE.wait(ready)
        m = PE.mark(pe.matmul(slot.ap, w, xnT[:, cols(b)], start=True, stop=True))
        yield
        A.wait(m)
        m = A.mark(act.activation(dst[:, cols(b)], slot.ap, ACT.Identity, bias=bias, scale=scale))
        slot.freed = (m,)
        projected[b] = m

    bias_added, projected = {}, {}

    def split(src, dst, ready, dst_free=()):
        V.wait(*ready)
        V.wait(*dst_free)
        V.step(dve.tensor_copy(dst[:, 0, :], src))
        V.step(dve.tensor_tensor(src, src, dst[:, 0, :], ALU.subtract))
        V.step(dve.tensor_copy(dst[:, 1, :], src))
        V.step(dve.tensor_tensor(src, src, dst[:, 1, :], ALU.subtract))
        return V.mark(dve.tensor_copy(dst[:, 2, :], src))

    def write_parts(t, scr, src, lo, n, ready):
        Q.wait(ready)
        for s in range(3):
            t.start(Q, scr[:, s, :, lo:lo + n], src[:, s, :])
        return t.done()

    def fill_queries(t, b, written, free):
        Q.wait(written, *free)
        for parity in range(2):
            heads = q_scr[:, :, :, cols(b)].rearrange("(h two) s d t -> two (s d) h t", two=2)[parity]
            for block, n in QUERY_RUNS:
                p0 = parity * SLOT + block * D
                t.start(Q, q_stack[p0:p0 + n * D, b, :, :], heads[0:n * D])
        return t.done()

    def fill_keys(t, scr, stack, lo, n, written, free):
        Q.wait(written, *free)
        for parity in range(2):
            heads = scr[:, :, :, lo:lo + n].rearrange("(h two) s d t -> two (s d) h t", two=2)[parity]
            for block, (_, part) in enumerate(PARTS):
                p0 = parity * SLOT + block * D
                t.start(Q, stack[p0:p0 + D, :, lo:lo + n], heads[part * D:(part + 1) * D])
        return t.done()

    def fill_mask_row(t, stack, row):
        for parity in range(2):
            p0 = parity * SLOT + ROW_MASK
            n = stack.shape[-1]
            src = row.rearrange("t p -> (t p)")[0:n].rearrange("(o h n) -> o h n", o=1, h=1)
            t.start(Q, stack[p0:p0 + 1, :, :], src.broadcast_to([1, PAIRS, n]))

    state = {"q_free": [(q_set,)] * B, "self_free": (self_set,), "ctx_free": (), "parts_free": [()] * B,
             "x": [t_x.done()] * B, "vaug_free": (), "ffn_free": ()}
    t_write = [transfers(f"write{b}") for b in range(B)]
    t_fill = [transfers(f"fill{b}") for b in range(B)]
    t_kwrite = [transfers(f"kwrite{b}") for b in range(B)]
    t_kfill = [transfers(f"kfill{b}") for b in range(B)]
    t_maxrow = [transfers(f"maxrow{b}") for b in range(B)]

    def queries(b, ready):
        m = split(qT[:, cols(b)], parts[:, :, cols(b)], ready, state["parts_free"][b])
        yield
        written = write_parts(t_write[b], q_scr, parts[:, :, cols(b)], b * S, S, m)
        state["parts_free"][b] = (written,)
        q_filled[b] = fill_queries(t_fill[b], b, written, state["q_free"][b])

    def self_keys(b, kT, ready):
        m = split(kT[:, cols(b)], parts[:, :, cols(b)], ready, state["parts_free"][b])
        yield
        written = write_parts(t_kwrite[b], k_scr, parts[:, :, cols(b)], b * S, S, m)
        state["parts_free"][b] = (written,)
        k_filled[b] = fill_keys(t_kfill[b], k_scr, self_stack, b * S, S, written, state["self_free"])

    q_filled, k_filled = {}, {}

    def head_slot(h):
        return h % 2 * SLOT, h // 2

    def max_to_stack(b, m, max_ready):
        col = mx[:, b, :, :, :].rearrange("p a h q -> p (a h q)")
        V.wait(m)
        V.step(dve.tensor_copy(mparts[:, 0, :], col))
        V.step(dve.tensor_tensor(col, col, mparts[:, 0, :], ALU.subtract))
        V.step(dve.tensor_copy(mparts[:, 1, :], col))
        V.step(dve.tensor_tensor(col, col, mparts[:, 1, :], ALU.subtract))
        m = V.mark(dve.tensor_copy(mparts[:, 2, :], col))
        yield
        slot = yield from claim(misc, PE)
        PE.wait(m)
        ps = slot.ap[0:96, 0:64].bitcast(BF16)
        m = PE.mark(pe.transpose(ps, mparts[:].rearrange("p s c -> p (s c)"), ident_b[:]))
        yield
        V.wait(m, t_maxrow[b].done())
        m = V.mark(dve.tensor_copy(mT[:, b, :], ps))
        slot.freed = (m,)
        Q.wait(m)
        for s in range(3):
            for parity in range(2):
                r = (s * 2 + parity) * TPB * PAIRS
                p0 = parity * SLOT + ROW_MAX + s
                t_maxrow[b].start(Q, q_stack[p0:p0 + 1, b, :, :].rearrange("o h (q t) -> o (h q) t", q=TPB),
                                  mT[r:r + TPB * PAIRS, b, :])
        max_ready[b] = t_maxrow[b].done()

    def turn_group(b, g, slot, ready, weigh, close, following):
        o = outT[:, g % 2, :]
        m = lift(o, slot.ap, [ready, *outT_free[g % 2]])
        slot.freed = (m,)
        yield
        slot = yield from claim(misc, PE)
        PE.wait(m)
        for q in range(TPB):
            m = PE.mark(pe.transpose(slot.ap[:, q * P:(q + 1) * P], o[:, q * P:(q + 1) * P], ident))
        outT_free[g % 2] = (m,)
        yield
        V.wait(m)
        m = weigh(b, g, slot.ap.rearrange("p (q j e) -> p q j e", q=TPB, e=COLS), rsum[:, g % 2, :, :])
        slot.freed = (m,)
        if g == H // GROUP - 1:
            yield
            yield from close(b, m)
            if following:
                prologue_done[b] = spawn(following(b))

    def attention(k_stack, nk, values, dv, k_ready, v_ready, weigh, close, following, add_mask=None,
                  pt_at=(4096, 7)):
        nkt = nk // P
        units = nkt // 2
        pts = Ring([Slot(wk(pt_at[0] + i * 1024, 1024).rearrange("p (a k q) -> p a k q", a=2, k=2))
                    for i in range(pt_at[1])])
        max_ready, held = {}, {}

        def maxima(step, part):
            b, pair = divmod(step, PAIRS)
            if pair == 0 and part == 0:
                await_prologue(b)
                if b == 0:
                    warm(WARM)
                PE.wait(q_filled[b], k_ready(b))
            slots = []
            for i in range(2 if nk == S2 else 1):
                slot = take(one, PE)
                parity = i if nk == S2 else part
                p0 = parity * SLOT
                for q in ([part] if nk == S2 else range(TPB)):
                    lo = 0 if nk == S2 else q * nk
                    m = PE.mark(pe.matmul(slot.ap[:, lo:lo + nk], q_stack[p0:p0 + K_SCORE, b, pair, q * P:(q + 1) * P],
                                          k_stack[p0:p0 + K_SCORE, pair, b * nk:(b + 1) * nk],
                                          start=True, stop=True))
                slots.append((slot, parity, m))
            for slot, parity, m in slots:
                V.wait(m)
                if add_mask:
                    m = V.mark(dve.tensor_tensor_reduce(
                        slot.ap, slot.ap, add_mask[0][:, b * TPB + part, :], 1.0, -3e38,
                        ALU.add, ALU.max, mx[:, b, parity, pair, part:part + 1]))
                elif nk == S2:
                    m = V.mark(dve.tensor_reduce(mx[:, b, parity, pair, part:part + 1], slot.ap,
                                                 AX, ALU.max, negate=True))
                else:
                    m = V.mark(dve.tensor_reduce(mx[:, b, parity, pair, :],
                                                 slot.ap.rearrange("p (i k) -> p i k", k=nk),
                                                 AX, ALU.max, negate=True))
                slot.freed = (m,)
            if pair == PAIRS - 1 and part == 1:
                if add_mask:
                    V.wait(m)
                    c = mx[:, b, :, :, :].rearrange("p a h q -> p (a h q)")
                    m = V.mark(dve.tensor_scalar(c, c, -1.0, None, ALU.mult))
                spawn(max_to_stack(b, m, max_ready))

        def exps(step, unit):
            b, pair = divmod(step, PAIRS)
            while b not in max_ready:
                tick(urgent=True)
            slot = take(two, PE)
            PE.wait(max_ready[b])
            for i in range(2):
                k = 2 * unit + i
                for parity in range(2):
                    p0 = parity * SLOT
                    m = pe.matmul(slot.ap[:, parity, i * S:(i + 1) * S],
                                  k_stack[p0:p0 + K_EXP, pair, b * nk + k * P:b * nk + (k + 1) * P],
                                  q_stack[p0:p0 + K_EXP, b, pair, :], start=True, stop=add_mask is None,
                                  skip_group_check=add_mask is not None)
                    if add_mask:
                        m = pe.matmul(slot.ap[:, parity, i * S:(i + 1) * S], ident_b[:], add_mask[1][:, b, k, :],
                                      start=False, stop=True, skip_group_check=True)
            m = PE.mark(m)
            if pair == PAIRS - 1 and unit == units - 1:
                state["q_free"][b] = (m,)
            pt = pts.take(A)
            A.wait(m)
            m = A.mark(act.activation(pt.ap.rearrange("p a k q -> p (a k q)"),
                                      slot.ap.rearrange("p a n -> p (a n)"), ACT.Exp))
            slot.freed = (m,)
            held[step, unit] = (pt, m)

        def sums(b, g):
            slot = take(outs, PE)
            for k in range(nkt):
                for j in range(GROUP):
                    pt, ready = held[b * PAIRS + 2 * g + j // 2, k // 2]
                    PE.wait(ready, v_ready(b))
                    m = pe.matmul(slot.ap[j * COLS:(j + 1) * COLS, :], values(b * nkt + k, g * GROUP + j),
                                  pt.ap[:, j % 2, k % 2, :], start=(k == 0), stop=(k == nkt - 1),
                                  tile_position=(0, j * COLS))
            m = PE.mark(m)
            for key in [key for key in held if key[0] // 2 == (b * PAIRS + 2 * g) // 2]:
                held.pop(key)[0].freed = (m,)
            spawn(turn_group(b, g, slot, m, weigh, close, following))
            return m

        n_steps = B * PAIRS
        ahead = PAIRS + LEAD
        for i in range(ahead):
            maxima(i, 0)
            maxima(i, 1)
            tick()
        for i in range(n_steps):
            if i == 0:
                warm(WARM)
            exps(i, 0)
            tick()
            if i + ahead < n_steps:
                maxima(i + ahead, 0)
            tick()
            if units == 2:
                exps(i, 1)
            if i and i % 2 == 0:
                sums((i - 1) // PAIRS, (i - 1) % PAIRS // 2)
            tick()
            if i + ahead < n_steps:
                maxima(i + ahead, 1)
            tick()
        last = sums(B - 1, H // GROUP - 1)
        return last

    outT_free = [(), ()]

    def normalise(b, g, heads, rs, scale=None):
        V.step(dve.reciprocal(rs, heads[:, :, :, D]))
        if scale is not None:
            V.step(dve.tensor_tensor(rs, rs, scale[:, b * TPB:(b + 1) * TPB].unsqueeze(2)
                                     .broadcast_to([P, TPB, GROUP]), ALU.mult))
        o = xn[:, b * TPB:(b + 1) * TPB, g * GROUP * D:(g + 1) * GROUP * D].rearrange("p q (j e) -> p q j e", e=D)
        return V.mark(dve.tensor_tensor(o, heads[:, :, :, 0:D],
                                        rs.unsqueeze(3).broadcast_to([P, TPB, GROUP, D]), ALU.mult))

    def project_out(b, w, ready, post=None):
        slot = yield from claim(misc, PE)
        PE.wait(ready)
        for i, t in enumerate(tiles(b)):
            m = PE.mark(pe.transpose(slot.ap[:, i * P:(i + 1) * P], xn[:, t, :], ident))
        yield
        m = lift(qT[:, cols(b)], slot.ap, [m])
        slot.freed = (m,)
        yield
        slot = yield from claim(misc, PE)
        PE.wait(m)
        for i, t in enumerate(tiles(b)):
            m = PE.mark(pe.matmul(slot.ap[:, i * P:(i + 1) * P], qT[:, t * P:(t + 1) * P], w, start=True, stop=True))
        yield
        V.wait(m, *bias_added[b])
        xb = x[:, b * TPB:(b + 1) * TPB, :]
        ps = slot.ap.rearrange("p (q f) -> p q f", q=TPB)
        if post is not None:
            V.step(dve.tensor_tensor(ps, ps, post.unsqueeze(1).broadcast_to([P, TPB, E]), ALU.mult))
        m = V.mark(dve.tensor_tensor(xb, ps, xb, ALU.add))
        slot.freed = (m,)
        state["x"][b] = m

    ctx_tok = wk(0, 2048).rearrange("p (t f) -> p t f", t=NC)
    ctxT = wk(2048, 2048)
    t_cwrite, t_kxwrite, t_vwrite, t_mrow = (transfers(n) for n in ("cwrite", "kxwrite", "vwrite", "mrow"))
    t_cfill, t_vload, t_mask3 = (transfers(n) for n in ("cfill", "vload", "mask3"))
    t_w0, t_w1, t_w2, t_w3 = (transfers(f"w{i}") for i in range(4))

    def turn_context():
        PE.wait(t_ctx.done())
        V.wait(t_ctx.done())
        for g in range(4):
            slot = yield from claim(one, PE)
            for i in range(4):
                m = PE.mark(pe.transpose(slot.ap[:, i * P:(i + 1) * P], ctx_tok[:, 4 * g + i, :], ident))
            ctxT_ready.append(evacuate(g, ctxT[:, g * 512:(g + 1) * 512], slot.ap, m))
            slot.freed = (ctxT_ready[-1],)
            yield
        va = vaug.rearrange("p t (h e) -> p t h e", h=H)
        V.wait(vaug_set)
        for g in range(4):
            m = V.mark(dve.tensor_copy(va[:, 4 * g:4 * g + 4, :, 0:D].rearrange("p t h e -> p (t h) e"),
                                       ctx_tok[:, 4 * g:4 * g + 4, :].rearrange("p t (h e) -> p (t h) e", e=D)))
            yield
        state["va0"] = m
        Q.wait(m)
        t_vwrite.start(Q, v_scr[0], vaug_pad[:, 0:NC * VA])

    def context_keys_l3():
        kv_free = ()
        for b in range(B):
            V.wait(*kv_free)
            for g in range(2):
                slot = yield from claim(one, PE)
                PE.wait(ctxT_ready[b])
                for i in range(2):
                    t = 4 * b + 2 * g + i
                    m = PE.mark(pe.matmul(slot.ap[:, i * 256:(i + 1) * 256], ctxT[:, t * P:(t + 1) * P],
                                          kp("L3x_kvT"), start=True, stop=True))
                yield
                V.wait(m)
                m = V.mark(dve.tensor_tensor(
                    kv[:, 2 * g:2 * g + 2, :], slot.ap.rearrange("p (t c) -> p t c", t=2),
                    rw("L3x_bkv").unsqueeze(1).broadcast_to([P, 2, 2 * E]), ALU.add))
                slot.freed = (m,)
            yield
            slot = yield from claim(one, PE)
            PE.wait(m)
            for i in range(4):
                m = pe.matmul(slot.ap[:, 0:E], kv[:, i, 0:E], kv[:, i, E:2 * E], start=(i == 0), stop=(i == 3))
            m = PE.mark(m)
            kv_free = (m,)
            V.wait(m)
            m = V.mark(dve.scalar_tensor_tensor(kv3[:, b, :], slot.ap[:, 0:E], 1.0 / DK3, kp("blockdiag"),
                                                ALU.mult, ALU.mult))
            slot.freed = (m,)
            yield
        state["kv3"] = m

    def context_values_l1():
        V.wait(t_rows.done())
        for g in range(4):
            slot = yield from claim(one, PE)
            PE.wait(ctxT_ready[g])
            for i in range(4):
                t = 4 * g + i
                m = PE.mark(pe.matmul(slot.ap[:, i * P:(i + 1) * P], ctxT[:, t * P:(t + 1) * P],
                                      kp("L1x_vT"), start=True, stop=True))
            yield
            vx = vx_buf[:, g % 2, :].rearrange("p (t c) -> p t c", t=4)
            V.wait(m, vx_set, *([vx_sent[g - 2]] if g >= 2 else []))
            for i in range(4):
                m = V.mark(dve.tensor_tensor(
                    vx[:, i, :].rearrange("p (h e) -> p h e", h=H)[:, :, 0:D],
                    slot.ap[:, i * P:(i + 1) * P].rearrange("p (h e) -> p h e", h=H),
                    rw("L1x_bv").rearrange("p (h e) -> p h e", h=H), ALU.add))
            slot.freed = (m,)
            Q.wait(m)
            t_vx[g % 2].start(Q, v_scr[1][:, g * 4 * VA:(g + 1) * 4 * VA], vx_buf[:, g % 2, :])
            vx_sent.append(t_vx[g % 2].done())
            yield

    def context_keys():
        kx = wk(4096, 2048)
        for g in range(4):
            slot = yield from claim(one, PE)
            PE.wait(ctxT_ready[g])
            m = PE.mark(pe.matmul(slot.ap, kp("L1x_kT"), ctxT[:, g * 512:(g + 1) * 512], start=True, stop=True))
            yield
            A.wait(m)
            m = A.mark(act.activation(kx[:, g * 512:(g + 1) * 512], slot.ap, ACT.Identity, bias=kp("L1x_bk")))
            slot.freed = (m,)
            kx_ready.append(m)
            yield
        PE_done = (PE.sem, PE.count)
        for src, room, t, scr in ((ctxT, 0, t_cwrite, c_scr), (kx, 1, t_kxwrite, kx_scr)):
            for g in range(4):
                lo = g * 512
                half = ffn_w[:, ROOM_AT + room * 3072:ROOM_AT + (room + 1) * 3072].bitcast(BF16) \
                    .rearrange("p (s t) -> p s t", s=3)[:, :, lo:lo + 512]
                m = split(src[:, lo:lo + 512], half, [kx_ready[g], ctxT_ready[g], PE_done])
                write_parts(t, scr, half, lo, 512, m)
                yield
            Q.wait(t.done(), m)
            t_mask[room].start(Q, mask_raw[room], d["mask_L0"].rearrange("b o (j p) k -> p (b o j) k", p=P)
                               [:, 4 * room:4 * room + 4, :])

    def prepare_mask():
        for half in range(2):
            raw = mask_raw[half]
            V.wait(t_mask[half].done(), t_vwrite.done(), (PE.sem, PE.count))
            for i in range(4):
                m = V.mark(dve.tensor_scalar(far_q[:, 4 * half + i, :], raw[:, i, :], 0, -BIG,
                                             ALU.is_equal, ALU.mult))
                yield
            for b in range(2 * half, 2 * half + 2):
                slot = yield from claim(misc, PE)
                PE.wait(m)
                ps = ps_m[:].rearrange("p i n -> p (i n)").bitcast(BF16)
                for k in range(S2 // P):
                    for q in range(TPB):
                        mm = PE.mark(pe.transpose(ps[:, (k * TPB + q) * P:(k * TPB + q + 1) * P],
                                                  far_q[:, b * TPB + q, k * P:(k + 1) * P], ident_b[:]))
                A.wait(mm)
                mm = A.mark(act.copy(far_k[:, b, :, :].rearrange("p k q -> p (k q)"), ps))
                slot.freed = (mm,)
                yield
        state["mask_ready"] = mm

    ROOM_AT = L0A_N + NT * H0 * (DV0 + 1) + COLS
    mask_raw = [a.bitcast(I32).rearrange("p (t k) -> p t k", t=4)
                for a in (ffn_w[:, ROOM_AT:ROOM_AT + 2048], wk(4096, 2048))]
    t_mask = [transfers(f"mask{i}") for i in range(2)]
    far_q = wk(0, 2048).bitcast(BF16).rearrange("p (t k) -> p t k", t=NT)
    far_k = wk(2048, 2048).bitcast(BF16).rearrange("p (b k q) -> p b k q", b=B, k=S2 // P)
    ctxT_ready, kx_ready, vx_sent = [], [], []
    t_vx = [transfers(f"vx{i}") for i in range(2)]
    vx_buf = wk(6144, 8 * VA).rearrange("p (g c) -> p g c", g=2)
    kv = ffn_w[:, ROOM_AT:ROOM_AT + 8 * E].rearrange("p (t c) -> p t c", t=4)

    def set_ctx_stack():
        for pair in range(PAIRS):
            m = G.mark(pool.memset(ctx_stack[:, pair, :].bitcast(F32), TWO_ONES))
            yield
        state["ctx_free"] = (m,)

    def prepare_context():
        yield from turn_context()
        yield from context_keys_l3()
        yield from context_values_l1()
        yield from context_keys()
        assert state["ctx_free"]
        load_ctx_stack(c_scr, 0, t_cwrite.done())
        yield from prepare_mask()

    def load_ctx_stack(scr, mask, written):
        Q.wait(t_mrow.done())
        fill_keys(t_cfill, scr, ctx_stack, 0, CTX, written, state["ctx_free"])
        fill_mask_row(t_cfill, ctx_stack, m_scr[mask])

    def load_values(which):
        Q.wait(t_vwrite.done(), vx_sent[-1], vx_sent[-2], *state["vaug_free"])
        t_vload.start(Q, vaug_pad[:, 0:NC * VA], v_scr[which])

    def finish_out():
        t_out = transfers("out")
        Q.wait(*state["x"], *(m for b in range(B) for m in bias_added[b]))
        t_out.start(Q, out.rearrange("b (j p) f -> p (b j) f", p=P), x[:])
        for t in every_transfer:
            Q.wait(t.done())

    va0 = ffn_w[:, L0A_N:L0A_N + NT * H0 * (DV0 + 1) + COLS]
    va0_tiles = va0[:, 0:NT * H0 * (DV0 + 1)].rearrange("p (t h e) -> p t h e", t=NT, h=H0)
    rope_tmp = wk(7400, S)
    kT = xn[:].rearrange("p t f -> p (t f)")

    def l0a_prologue(b):
        yield from norm(b)
        PE.wait(t_l0a.done())
        V.wait(t_l0a.done())
        for dst, w, wp, c, s_, after in ((qT, "qT", "qpT", "qcos", "qsin", queries),
                                         (kT, "kT", "kpT", "kcos", "ksin", self_keys)):
            s0 = yield from claim(misc, PE)
            other = ps_m[:, 1, :]
            PE.wait(xnT_ready[b])
            PE.mark(pe.matmul(s0.ap, l0w(w), xnT[:, cols(b)], start=True, stop=True))
            m1 = PE.mark(pe.matmul(other, l0w(wp), xnT[:, cols(b)], start=True, stop=True))
            o = dst[:, cols(b)]
            V.wait(m1)
            V.mark(dve.tensor_tensor(o, s0.ap, l0w(c), ALU.mult))
            m = V.step(dve.tensor_tensor(rope_tmp, other, l0w(s_), ALU.mult))
            s0.freed = (m,)
            m = V.mark(dve.tensor_tensor(o, o, rope_tmp, ALU.add))
            if after is queries:
                yield from queries(b, [m])
            else:
                yield from self_keys(b, dst, [m])
            yield
        slot = yield from claim(misc, PE)
        for i, t in enumerate(tiles(b)):
            m = PE.mark(pe.matmul(slot.ap[:, i * P:(i + 1) * P], xnT[:, t * P:(t + 1) * P], l0w("vT"),
                                  start=True, stop=True))
        V.wait(m, va0_set)
        for i, t in enumerate(tiles(b)):
            m = V.mark(dve.tensor_copy(va0_tiles[:, t, :, 0:DV0],
                                       slot.ap[:, i * P:(i + 1) * P].rearrange("p (h e) -> p h e", h=H0)))
        slot.freed = (m,)
        va_ready[b] = m

    va_ready = {}

    def l0a_weigh(b, g, heads, rs):
        V.step(dve.reciprocal(rs, heads[:, :, :, DV0]))
        r2 = rs.rearrange("p q (j two) -> p q j two", two=2)
        V.step(dve.tensor_scalar(r2[:, :, :, 1], r2[:, :, :, 1], lam[:, 5:6], None, ALU.mult))
        tmp = l0a_tmp[:, g % 2, :].rearrange("p (q j e) -> p q j e", q=TPB, e=DV0)
        V.step(dve.tensor_tensor(tmp, heads[:, :, :, 0:DV0], rs.unsqueeze(3).broadcast_to([P, TPB, GROUP, DV0]),
                                 ALU.mult))
        for q in range(TPB):
            two = tmp[:, q, :, :].rearrange("p (j two) e -> p j two e", two=2)
            o = xn[:, b * TPB + q, g * 2 * DV0:(g + 1) * 2 * DV0].rearrange("p (j e) -> p j e", e=DV0)
            m = V.mark(dve.tensor_tensor(o, two[:, :, 0, :], two[:, :, 1, :], ALU.add))
        return m

    def l0a_close(b, m):
        V.wait(m)
        heads = xn[:, b * TPB:(b + 1) * TPB, :].rearrange("p q (h e) -> p (q h) e", e=DV0)
        sq = rope_sq.rearrange("p (g e) -> p g e", e=DV0)
        V.step(dve.tensor_tensor(sq, heads, heads, ALU.mult))
        ss = l0a_ss[:]
        V.step(dve.tensor_reduce(ss, sq, AX, ALU.add))
        m = V.mark(dve.tensor_scalar(ss, ss, 1.0 / DV0, 1e-5, ALU.mult, ALU.add))
        m = power(ss, ss, -0.5, m)
        yield
        V.wait(m)
        V.step(dve.tensor_scalar(ss, ss, 1.0 - LAMBDA_INIT, None, ALU.mult))
        m = V.mark(dve.tensor_tensor(heads, heads, ss.unsqueeze(2).broadcast_to([P, TPB * H0, DV0]), ALU.mult))
        yield from project_out(b, l0w("oT"), m)

    rope_sq = wk(7656, TPB * E)
    l0a_tmp = wk(7912, 2 * TPB * GROUP * DV0).rearrange("p (g c) -> p g c", g=2)

    def cross_prologue(bias_row, scale, project=None):
        def prologue(b):
            row = None if bias_row is None else rw(bias_row)
            if project is None:
                yield from norm(b, row, dst=qT, scale=scale)
                m = xnT_ready[b]
            else:
                yield from norm(b, row)
                yield from project_batch(b, qT, kp(project), bq_scaled[:], scale, xnT_ready[b])
                m = projected[b]
            yield
            yield from queries(b, [m])
        return prologue

    def cross(w_out, v_ready, following, add_mask=None):
        values = lambda tile, h: vaug_pad[:, tile * VA + h * (D + 1):tile * VA + h * (D + 1) + COLS]
        if add_mask:
            PE.wait(state["mask_ready"])
            V.wait(state["mask_ready"])
        last = attention(ctx_stack, S2, values, D, lambda b: t_cfill.done(), lambda b: v_ready, normalise,
                         lambda b, m: project_out(b, w_out, m), following, add_mask)
        state["ctx_free"] = state["vaug_free"] = (last,)

    def ffn_prologue(b):
        yield from norm(b)

    def l0f_prologue(b):
        if b == 0:
            Q.wait((PE.sem, PE.count), (V.sem, V.count), t_cwrite.done(), t_kxwrite.done())
            t_w0.start(Q, ffn_w[:, 0:FFN_N], d["L0f_w"][:, :])
        yield from norm(b)

    def route(router, eps):
        for b in range(B):
            await_prologue(b)
        slot = take(one, PE)
        for b in range(B):
            PE.wait(xnT_ready[b])
            for t in tiles(b):
                m = PE.mark(pe.matmul(slot.ap[:, t * NE:(t + 1) * NE], xnT[:, t * P:(t + 1) * P], router,
                                      start=True, stop=True))
        lg = slot.ap[:, 0:NT * NE].rearrange("p (t e) -> p t e", e=NE)
        V.wait(*(m for b in range(B) for m in state["parts_free"][b]))
        flat = parts[:].rearrange("p s t -> p (s t)").bitcast(F32)
        sm = [flat[:, TOK + i * NT * NE:TOK + (i + 1) * NT * NE].rearrange("p (t e) -> p t e", e=NE) for i in range(8)]
        p_, eq, o1, o2, c = sm[0:5]
        r = [sm[5][:, :, i] for i in range(8)] + [sm[6][:, :, i] for i in range(2)]
        wide = lambda a: a.unsqueeze(2).broadcast_to([P, NT, NE])
        rev = kp("rev").unsqueeze(1).broadcast_to([P, NT, NE])
        V.wait(m)
        V.step(dve.tensor_reduce(r[0], lg, AX, ALU.max))
        m = V.step(dve.tensor_tensor(p_, lg, wide(r[0]), ALU.subtract))
        slot.freed = (m,)
        A.wait(m)
        V.wait(A.mark(act.activation(p_, p_, ACT.Exp)))
        V.step(dve.tensor_reduce(r[1], p_, AX, ALU.add))
        V.step(dve.reciprocal(r[1], r[1]))
        V.step(dve.tensor_tensor(p_, p_, wide(r[1]), ALU.mult))
        for o, top in ((o1, r[2]), (o2, r[3])):
            V.step(dve.tensor_reduce(top, p_, AX, ALU.max))
            V.step(dve.tensor_tensor(eq, p_, wide(top), ALU.is_equal))
            V.step(dve.tensor_tensor(eq, eq, rev, ALU.mult))
            V.step(dve.tensor_reduce(r[4], eq, AX, ALU.max))
            V.step(dve.tensor_tensor(o, rev, wide(r[4]), ALU.is_equal))
            if o is o1:
                V.step(dve.scalar_tensor_tensor(c, o, -2.0, p_, ALU.mult, ALU.add))
                p_ = c
        if eps is None:
            for top in (r[2], r[3]):
                V.step(dve.tensor_scalar(top, top, MOE_SCALE, None, ALU.mult))
        else:
            V.step(dve.tensor_tensor(r[5], r[2], r[3], ALU.add))
            V.step(dve.tensor_scalar(r[5], r[5], eps, None, ALU.add))
            V.step(dve.reciprocal(r[5], r[5]))
            for top in (r[2], r[3]):
                V.step(dve.tensor_tensor(top, top, r[5], ALU.mult))
        V.mark(dve.tensor_tensor(o1, o1, wide(r[2]), ALU.mult))
        V.step(dve.tensor_tensor(o2, o2, wide(r[3]), ALU.mult))
        return V.step(dve.tensor_tensor(gates[:, :, 0:NE], o1, o2, ALU.add))

    def add_gated_bias(which, n, gated):
        PE.wait(t_b2.done())
        for g in range(2):
            slot = take(one, PE)
            PE.wait(gated)
            for i in range(4):
                m = PE.mark(pe.transpose(slot.ap[0:n, i * P:(i + 1) * P], gates[:, 4 * g + i, 0:n], ident))
            V.wait(m)
            m = V.mark(dve.tensor_copy(gatesT[0:n, g * 512:(g + 1) * 512], slot.ap[0:n, :]))
            slot.freed = (m,)
            slot = take(one, PE)
            PE.wait(m)
            for i in range(4):
                t = 4 * g + i
                m = PE.mark(pe.matmul(slot.ap[:, i * P:(i + 1) * P], gatesT[0:n, t * P:(t + 1) * P],
                                      b2[0:n, which, :], start=True, stop=True))
            V.wait(m)
            xs = x[:, 4 * g:4 * g + 4, :]
            m = V.mark(dve.tensor_tensor(xs, slot.ap.rearrange("p (t f) -> p t f", t=4), xs, ALU.add))
            slot.freed = (m,)
            state["x"][2 * g] = state["x"][2 * g + 1] = m

    def down(parts_of, blocks, following=None):
        for b in range(B):
            for hidden, w2, scalar_of, ready in parts_of:
                slot = take(one, PE)
                PE.wait(ready)
                for i, t in enumerate(tiles(b)):
                    for j in range(blocks):
                        m = pe.matmul(slot.ap[:, i * P:(i + 1) * P], hidden.ap[:, j, t * P:(t + 1) * P], w2(j),
                                      start=(j == 0), stop=(j == blocks - 1))
                last = PE.mark(m)
                hidden.freed = (last,)
                V.wait(last, state["x"][b])
                for i, t in enumerate(tiles(b)):
                    m = V.mark(dve.scalar_tensor_tensor(x[:, t, :], slot.ap[:, i * P:(i + 1) * P], scalar_of(t),
                                                        x[:, t, :], ALU.mult, ALU.add))
                slot.freed = (m,)
                state["x"][b] = m
            if following:
                prologue_done[b] = spawn(following(b))
            tick()

    def experts(n, up, blocks, w2_of, scalar_of, following):
        each = lambda e, held: (held[0], lambda j: w2_of(e, j), lambda t: scalar_of(e, t), held[1])
        held = up(0)
        for e in range(n - 2):
            nxt = up(e + 1)
            down([each(e, held)], blocks)
            held = nxt
        nxt = up(n - 1)
        down([each(n - 2, held), each(n - 1, nxt)], blocks, following)
        state["ffn_free"] = held[0].freed + nxt[0].freed

    def gelu_experts(router, eps, n_exp, w_off2, b1, t_w, bias_which, bias_rows, weights, following):
        gated = route(router, eps)
        hid = Ring([Slot(wk(i * FJ * TOK, FJ * TOK).rearrange("p (j t) -> p j t", j=FJ)) for i in range(2)])

        def up(e):
            h = hid.take(A)
            PE.wait(t_w.done())
            for j in range(FJ):
                slot = take(two, PE)
                for g in range(2):
                    m = PE.mark(pe.matmul(slot.ap[:, g, :],
                                          weights[:, (e * FJ + j) * P:(e * FJ + j + 1) * P],
                                          xnT[:, g * 512:(g + 1) * 512], start=True, stop=True))
                A.wait(m)
                m = A.mark(act.activation(h.ap[:, j, :], slot.ap.rearrange("p a n -> p (a n)"),
                                          ACT.Gelu_apprx_tanh, bias=b1(e, j)))
                slot.freed = (m,)
                tick()
            return h, m

        def w2_of(e, j):
            return weights[:, w_off2 + (e * FJ + j) * E:w_off2 + (e * FJ + j + 1) * E]

        def scalar_of(e, t):
            return gates[:, t, e:e + 1] if e < NE else MOE_SCALE

        def up_and_bias(e):
            h = up(e)
            if e == 1:
                add_gated_bias(bias_which, bias_rows, gated)
            return h

        experts(n_exp, up_and_bias, FJ, w2_of, scalar_of, following)

    def swiglu_experts(t_w, following):
        route(kp("L1f_router"), 1e-20)
        hid = Ring([Slot(wk(i * F1J * TOK, F1J * TOK).rearrange("p (j t) -> p j t", j=F1J)) for i in range(2)])
        PE.wait(t_w.done())

        def up(e):
            h = hid.take(A)
            for j in range(F1J):
                pair = []
                for part in range(2):
                    slot = take(two, PE)
                    for g in range(2):
                        at = ((part * 9 + e) * F1J + j) * P
                        m = PE.mark(pe.matmul(slot.ap[:, g, :], ffn_w[:, at:at + P],
                                              xnT[:, g * 512:(g + 1) * 512], start=True, stop=True))
                    pair.append((slot, m))
                (sg, mg), (su, mu) = pair
                A.wait(mg)
                m = A.mark(act.activation(h.ap[:, j, :], sg.ap.rearrange("p a n -> p (a n)"), ACT.Silu))
                sg.freed = (m,)
                V.wait(m, mu)
                m = V.mark(dve.tensor_tensor(h.ap[:, j, :], h.ap[:, j, :],
                                             su.ap.rearrange("p a n -> p (a n)"), ALU.mult))
                su.freed = (m,)
                tick()
            return h, m

        def w2_of(e, j):
            return ffn_w[:, (18 * F1J + e * F1J + j) * P:(18 * F1J + e * F1J + j + 1) * P]

        experts(NE + 1, up, F1J, w2_of, lambda e, t: gates[:, t, e:e + 1] if e < NE else 1.0, following)

    QKV_N = 3 * E + 1
    l1_qkv = wk(9216, TPB * QKV_N).rearrange("p (t c) -> p t c", t=TPB)
    l1_sq = wk(9988, TPB * 2 * E)
    l1_aux = [wk(10500 + i * TPB * 2 * H, TPB * 2 * H) for i in range(8)]
    va1 = vaug_pad[:, 0:NT * VA].rearrange("p (t h e) -> p t h e", t=NT, h=H)
    qkv_free = [()]

    def l1a_prologue(b):
        yield from norm(b, rw("L1a_bout"))
        yield from hold("l1_qkv")
        V.wait(*qkv_free[0])
        for i, t in enumerate(tiles(b)):
            slot = yield from claim(one, PE)
            PE.wait(xnT_ready[b])
            m = PE.mark(pe.matmul(slot.ap[:, 0:QKV_N], xnT[:, t * P:(t + 1) * P], kp("L1a_qkv"),
                                  start=True, stop=True))
            V.wait(m)
            m = V.mark(dve.tensor_tensor(l1_qkv[:, i, :], slot.ap[:, 0:QKV_N], rw("L1a_bqkv"), ALU.add))
            slot.freed = (m,)
        V.wait(m)
        yield
        u = l1_qkv[:, :, 0:2 * E]
        w, n, e, ei, f, poly, wc, less = l1_aux
        V.step(dve.tensor_tensor(l1_sq.rearrange("p (t c) -> p t c", t=TPB), u, u, ALU.mult))
        by8 = l1_sq.rearrange("p (g e) -> p g e", e=D)
        V.step(dve.tensor_reduce(w, by8, AX, ALU.add))
        V.step(dve.scalar_tensor_tensor(w, by8[:, :, 0], -2.0, w, ALU.mult, ALU.add))
        m = V.step(dve.tensor_scalar(w, w, 1e-8, None, ALU.max))
        A.wait(m)
        A.step(act.activation(n, w, ACT.Sqrt))
        m = A.mark(act.activation(e, n, ACT.Exp))
        yield
        V.step(dve.tensor_scalar(wc, w, 1.0, None, ALU.min))
        V.mark(dve.tensor_scalar(less, w, 1.0, None, ALU.is_lt))
        V.step(dve.tensor_scalar(poly, wc, 1.0 / 39916800, None, ALU.mult))
        for c in (1.0 / 362880, 1.0 / 5040, 1.0 / 120, 1.0 / 6):
            V.step(dve.scalar_tensor_tensor(poly, poly, c, wc, ALU.add, ALU.mult))
        V.step(dve.tensor_scalar(poly, poly, 1.0, None, ALU.add))
        yield
        V.wait(m)
        V.step(dve.reciprocal(ei, e))
        V.step(dve.reciprocal(n, n))
        V.step(dve.tensor_tensor(f, e, ei, ALU.subtract))
        V.step(dve.scalar_tensor_tensor(f, f, 0.5, n, ALU.mult, ALU.mult))
        V.step(dve.tensor_tensor(poly, poly, f, ALU.subtract))
        V.step(dve.tensor_tensor(poly, poly, less, ALU.mult))
        V.step(dve.tensor_tensor(f, f, poly, ALU.add))
        V.step(dve.tensor_tensor(e, e, ei, ALU.add))
        V.step(dve.tensor_scalar(e, e, 0.5, None, ALU.mult))
        fq = f.rearrange("p (t g h) -> p t g h", t=TPB, g=2)[:, :, 0, :]
        V.step(dve.tensor_scalar(fq, fq, -1.0, None, ALU.mult))
        yield
        by8u = u.rearrange("p t (g e) -> p t g e", e=D)
        for i in range(TPB):
            m = V.mark(dve.tensor_tensor(by8u[:, i, :, :], by8u[:, i, :, :],
                                         f.rearrange("p (t g) -> p t g", t=TPB)[:, i, :].unsqueeze(2)
                                         .broadcast_to([P, 2 * H, D]), ALU.mult))
        V.wait(m)
        m = V.mark(dve.tensor_copy(by8u[:, :, :, 0], e.rearrange("p (t g) -> p t g", t=TPB)))
        for dst, off, after in ((qT, 0, queries), (kT, E, self_keys)):
            slot = yield from claim(misc, PE)
            PE.wait(m)
            for i in range(TPB):
                mm = PE.mark(pe.transpose(slot.ap[:, i * P:(i + 1) * P], l1_qkv[:, i, off:off + E], ident))
            yield
            mm = lift(dst[:, cols(b)], slot.ap, [mm])
            slot.freed = (mm,)
            yield
            if after is queries:
                yield from queries(b, [mm])
            else:
                yield from self_keys(b, dst, [mm])
        for i, t in enumerate(tiles(b)):
            m = V.mark(dve.tensor_copy(va1[:, t, :, 0:D], l1_qkv[:, i, 2 * E:3 * E].rearrange("p (h e) -> p h e", h=H)))
        va_ready[b] = m
        sp_b = spike[:, b * TPB:(b + 1) * TPB]
        A.wait(m)
        ms = A.mark(act.activation(sp_b, l1_qkv[:, :, 3 * E], ACT.Exp, scale=-1.0))
        qkv_free[0] = (ms,)
        release("l1_qkv")
        yield
        V.wait(ms)
        V.step(dve.tensor_scalar(sp_b, sp_b, 1.0, None, ALU.add))
        V.step(dve.reciprocal(sp_b, sp_b))
        V.step(dve.tensor_scalar(sp_b, sp_b, rw("thr"), None, ALU.is_gt))

    def l1_attention(following):
        WIDE = S + P
        UH = 8
        c_buf = Ring([Slot(wk(i * UH * WIDE, UH * WIDE).rearrange("p (h c) -> p h c", h=UH)) for i in range(2)])
        s_buf = Ring([Slot(wk(2 * UH * WIDE, UH * WIDE).rearrange("p (h c) -> p h c", h=UH))])
        halves_of = [slice(0, 4), slice(4, 8)]
        held = {}
        small_free = [()]
        banks = [[Slot(t[:, j, :]) for j in range(2)] for t in ps_t]
        for pair_, whole in zip(banks, two.slots):
            for slot in pair_:
                slot.freed = whole.freed
        single = Ring(banks[0] + banks[1])

        def nearest(u):
            b, half = divmod(u, 2)
            if half == 0:
                await_prologue(b)
                PE.wait(q_filled[b], k_filled[b])
            for h in range(half * UH, half * UH + UH):
                p0, pair = head_slot(h)
                slot = take(single, PE)
                for q in range(TPB):
                    c0, k_n = (0, P) if q == 0 else (P, S)
                    pe.matmul(slot.ap[:, c0:c0 + k_n], q_stack[p0:p0 + ROW_MASK, b, pair, q * P:(q + 1) * P],
                              self_stack[p0:p0 + ROW_MASK, pair, b * S:b * S + k_n], start=True, stop=False,
                              skip_group_check=True)
                    m = pe.matmul(slot.ap[:, c0 + k_n - P:c0 + k_n], ident_b[:], far_b[:],
                                  start=False, stop=True, skip_group_check=True)
                m = PE.mark(m)
                V.wait(m)
                V.mark(dve.tensor_reduce(mx[:, b, h % 2, pair, 0:1], slot.ap[:, 0:P], AX, ALU.min))
                m = V.mark(dve.tensor_reduce(mx[:, b, h % 2, pair, 1:2], slot.ap[:, P:P + S], AX, ALU.min))
                slot.freed = (m,)
                if h % 4 == 3:
                    tick()
            return m

        def roots(u, reduced):
            b, half = divmod(u, 2)
            c, s_ = c_buf.take(V), s_buf.take(V)
            squared = []
            for g in halves_of:
                for i in range(g.start, g.stop):
                    h = half * UH + i
                    p0, pair = head_slot(h)
                    slot = take(single, PE)
                    for k in range(TPB):
                        o = slot.ap[:, 0:S] if k == 0 else slot.ap[:, S:WIDE]
                        m = pe.matmul(o, self_stack[p0:p0 + ROW_MASK, pair, b * S + k * P:b * S + (k + 1) * P],
                                      q_stack[p0:p0 + ROW_MASK, b, pair, k * P:S], start=True, stop=True)
                    m = PE.mark(m)
                    V.wait(m)
                    m = V.mark(dve.tensor_scalar(c.ap[:, i, :], slot.ap[:, 0:WIDE], 1.0 + 1e-7, None, ALU.max))
                    slot.freed = (m,)
                V.wait(m)
                squared.append(V.mark(dve.tensor_tensor(s_.ap[:, g, :], c.ap[:, g, :], c.ap[:, g, :], ALU.mult)))
                tick()
            if half:
                state["q_free"][b] = ((PE.sem, PE.count),)
            least = mx[:, b, :, half * 4:half * 4 + 4, :]
            sq_s, root_s, sum_s = (small[:, i, 0:16] for i in range(3))
            four = lambda t: t.rearrange("p (a h q) -> p a h q", a=2, q=TPB)
            V.wait(reduced, *small_free[0])
            V.step(dve.tensor_scalar(least, least, 1.0 + 1e-7, None, ALU.max))
            m_s = V.mark(dve.tensor_tensor(four(sq_s), least, least, ALU.mult))
            rooted, summed = [], []
            for n, g in enumerate(halves_of):
                A.wait(squared[n])
                rooted.append(A.mark(act.activation(s_.ap[:, g, :], s_.ap[:, g, :], ACT.Sqrt, bias=minus1[:])))
            A.wait(m_s)
            rooted_s = A.mark(act.activation(root_s, sq_s, ACT.Sqrt, bias=minus1[:]))
            for n, g in enumerate(halves_of):
                G.wait(rooted[n])
                summed.append(G.mark(pool.tensor_tensor(c.ap[:, g, :], c.ap[:, g, :], s_.ap[:, g, :], ALU.add)))
            s_.freed = (summed[-1],)
            G.wait(rooted_s)
            summed_s = G.mark(pool.tensor_tensor(four(sum_s), four(root_s), least, ALU.add))
            return c, summed, summed_s, least

        def logs(c, summed, summed_s, least):
            sum_s, log_s = (small[:, i, 0:16] for i in range(2, 4))
            dist = []
            for n, g in enumerate(halves_of):
                A.wait(summed[n])
                A.step(act.activation(c.ap[:, g, :], c.ap[:, g, :], ACT.Ln))
                if n:
                    A.wait(summed_s)
                    logged = A.mark(act.activation(log_s, sum_s, ACT.Ln))
                dist.append(A.mark(act.activation(c.ap[:, g, :], c.ap[:, g, :], ACT.Square)))
            A.wait(logged)
            far = A.mark(act.activation(least, log_s.rearrange("p (a h q) -> p a h q", a=2, q=TPB), ACT.Square, scale=float(np.sqrt(RSQRT8))))
            small_free[0] = (far,)
            return c, dist, far

        def weights(u, c, dist, far):
            b, half = divmod(u, 2)
            for n, g in enumerate(halves_of):
                for i in range(g.start, g.stop):
                    h = half * UH + i
                    slot = take(single, PE)
                    PE.wait(far)
                    for j, q in enumerate((0, 1, 1)):
                        m = PE.mark(pe.transpose(slot.ap[:, j * P:(j + 1) * P],
                                                 mx[:, b, h % 2, h // 2, q:q + 1].broadcast_to([P, P]), ident))
                    V.wait(m, dist[n])
                    m = V.mark(dve.scalar_tensor_tensor(c.ap[:, i, :], c.ap[:, i, :], -RSQRT8, slot.ap[:, 0:WIDE],
                                                        ALU.mult, ALU.add))
                    slot.freed = (m,)
                A.wait(m)
                m = A.mark(act.activation(c.ap[:, g, :], c.ap[:, g, :], ACT.Exp))
                G.wait(m)
                for lo in (0, S):
                    blk = c.ap[:, g, lo:lo + P]
                    m = G.mark(pool.affine_select(out=blk, in_=blk, compare_op=ALU.is_ge, fill=0.0, base=0,
                                                  pattern=[[0, 4], [1, P]], channel_multiplier=-1))
                held[u, n] = m
                tick()

        def group_sums(u, c):
            b, half = divmod(u, 2)
            for n, g in enumerate(halves_of):
                slot = take(outs, PE)
                PE.wait(held[u, n], va_ready[b])
                for k in range(TPB):
                    for j in range(GROUP):
                        h = half * UH + n * 4 + j
                        at = (b * TPB + k) * VA + h * (D + 1)
                        q0, blk = (0, slice(0, S)) if k == 0 else (P, slice(S, WIDE))
                        m = pe.matmul(slot.ap[j * COLS:(j + 1) * COLS, q0:S], vaug_pad[:, at:at + COLS],
                                      c.ap[:, n * 4 + j, blk], start=(k == 0), stop=(k == 1),
                                      tile_position=(0, j * COLS), skip_group_check=True)
                m = PE.mark(m)
                spawn(turn_group(b, half * 2 + n, slot, m, lambda b, g, hd, rs: normalise(b, g, hd, rs, spike),
                                 lambda b, m: project_out(b, kp("L1a_out"), m), following))
            c.freed = (m,)
            return m

        n_units = 2 * B
        reduced = {u: nearest(u) for u in range(2)}
        unit = logs(*roots(0, reduced[0]))
        for u in range(n_units):
            if u + 1 < n_units:
                rooted_next = roots(u + 1, reduced[u + 1])
            weights(u, *unit)
            c = unit[0]
            if u + 1 < n_units:
                unit = logs(*rooted_next)
            if u + 2 < n_units:
                reduced[u + 2] = nearest(u + 2)
            last = group_sums(u, c)
            tick()
        for pair_, whole in zip(banks, two.slots):
            whole.freed = pair_[0].freed + pair_[1].freed
        state["self_free"] = (last,)
        state["vaug_free"] = (last,)

    l2_qkv = wk(8192, NT * 3 * E).rearrange("p (t c) -> p t c", t=NT)

    def l2a_prologue(b):
        yield from norm(b, rw("L2a_bout"))
        yield
        for t in tiles(b):
            slot = yield from claim(one, PE)
            PE.wait(xnT_ready[b])
            m = PE.mark(pe.matmul(slot.ap[:, 0:3 * E], xnT[:, t * P:(t + 1) * P], kp("L2a_inT"),
                                  start=True, stop=True))
            V.wait(m)
            m = V.mark(dve.tensor_tensor(l2_qkv[:, t, :], slot.ap[:, 0:3 * E], rw("L2a_bin"), ALU.add))
            slot.freed = (m,)
            G.wait(m)
            m = G.mark(pool.tensor_tensor(l2_qkv[:, t, :], l2_qkv[:, t, :], rw("L2a_gamma"), ALU.mult))
            yield
        qkv_ready[b] = m

    qkv_ready = {}

    def l2_attention(following):
        for s in range(B):
            await_prologue(s)
            V.wait(qkv_ready[s])
            n = s + 1
            prod = wk(0, n * TPB * E)
            sc = wk(1024 + s * 128, n * TPB * H)
            q = l2_qkv[:, s * TPB:(s + 1) * TPB, 0:E].unsqueeze(1).broadcast_to([P, n, TPB, E])
            k = l2_qkv[:, 0:n * TPB, E:2 * E].rearrange("p (n q) f -> p n q f", q=TPB)
            V.step(dve.tensor_tensor(prod.rearrange("p (n q f) -> p n q f", n=n, q=TPB), q, k, ALU.mult))
            V.step(dve.tensor_reduce(sc, prod.rearrange("p (g e) -> p g e", e=D), AX, ALU.add))
            scn = sc.rearrange("p (n g) -> p n g", n=n)
            top = wk(1600 + s * 64, TPB * H)
            V.step(dve.tensor_reduce(top, sc.rearrange("p (n g) -> p g n", n=n), AX, ALU.max))
            m = V.mark(dve.tensor_tensor(scn, scn, top.unsqueeze(1).broadcast_to([P, n, TPB * H]), ALU.subtract))
            A.wait(m)
            m = A.mark(act.activation(sc, sc, ACT.Exp, scale=RSQRT8))
            tick()
            V.wait(m)
            V.step(dve.tensor_reduce(top, sc.rearrange("p (n g) -> p g n", n=n), AX, ALU.add))
            V.step(dve.reciprocal(top, top))
            v = l2_qkv[:, 0:n * TPB, 2 * E:3 * E].rearrange("p t (h e) -> p t h e", e=D)
            V.step(dve.tensor_tensor(
                prod.rearrange("p (t h e) -> p t h e", h=H, e=D), v,
                sc.rearrange("p (t h) -> p t h", h=H).unsqueeze(3).broadcast_to([P, n * TPB, H, D]), ALU.mult))
            o = wk(2000, TPB * E)
            V.step(dve.tensor_reduce(o, prod.rearrange("p (n g) -> p g n", n=n), AX, ALU.add))
            og = o.rearrange("p (g e) -> p g e", e=D)
            V.step(dve.tensor_tensor(og, og, top.unsqueeze(2).broadcast_to([P, TPB * H, D]), ALU.mult))
            m = V.mark(dve.tensor_tensor(xn[:, s * TPB:(s + 1) * TPB, :], o.rearrange("p (q f) -> p q f", q=TPB),
                                         rw("L2a_alpha").unsqueeze(1).broadcast_to([P, TPB, E]), ALU.mult))
            spawn(l2a_close(s, m, following))
            tick()

    def l2a_close(b, m, following):
        yield from project_out(b, kp("L2a_outT"), m, post=rw("L2a_lgamma"))
        prologue_done[b] = spawn(following(b))

    def fp4(src, n, ready, at):
        nb = n // FP4_BLOCK
        a, mag, sgn = (wk(at + i * n, n) for i in range(3))
        sc, rs = (wk(at + 3 * n + i * nb, nb) for i in range(2))
        blk = lambda t: t.rearrange("p (b e) -> p b e", e=FP4_BLOCK)
        wide = lambda t: t.unsqueeze(2).broadcast_to([P, nb, FP4_BLOCK])
        V.wait(*ready)
        V.step(dve.tensor_reduce(sc, blk(src), AX, ALU.max, apply_absolute_value=True))
        V.step(dve.tensor_scalar(sc, sc, 1.0 / 6.0, 1e-12, ALU.mult, ALU.max))
        V.step(dve.reciprocal(rs, sc))
        m = V.mark(dve.tensor_tensor(blk(mag), blk(src), wide(rs), ALU.mult))
        A.wait(m)
        m = A.mark(act.activation(sgn, mag, ACT.Sign, scale=0.5))
        A.wait(m)
        m = A.mark(act.activation(mag, mag, ACT.Abs))
        yield
        V.wait(m)
        V.step(dve.tensor_scalar(a, mag, 5.0, 2.0, ALU.is_gt, ALU.mult))
        for mid in (3.5, 2.5):
            V.step(dve.scalar_tensor_tensor(a, mag, mid, a, ALU.is_gt, ALU.add))
        V.step(dve.tensor_scalar(a, a, 2.0, None, ALU.mult))
        yield
        for mid in (1.75, 1.25, 0.75, 0.25):
            V.step(dve.scalar_tensor_tensor(a, mag, mid, a, ALU.is_gt, ALU.add))
        V.step(dve.scalar_tensor_tensor(a, a, 0.5, sgn, ALU.mult, ALU.mult))
        restored[at] = V.mark(dve.tensor_tensor(blk(src), blk(a), wide(sc), ALU.mult))

    restored = {}
    F2_N = 2 * F2J * P + F2
    F2_AT = 27 * 2 * P
    f2_raw = ffn_w[:, F2_AT:F2_AT + F2_N]
    gT, uT, dT = (ffn_w[:, F2_AT + F2_N + i * F2J * P:F2_AT + F2_N + (i + 1) * F2J * P] for i in range(3))

    def l2f_weights():
        at = 4096
        yield from fp4(f2_raw, F2_N, [t_w2.done()], at)
        m = restored[at]
        for dst, off in ((gT, 0), (uT, F2J * P), (dT, 2 * F2J * P)):
            yield
            slot = yield from claim(one, PE)
            PE.wait(m)
            down_ = off == 2 * F2J * P
            for j in range(F2J):
                n = min(P, F2 - j * P) if down_ else P
                mm = PE.mark(pe.transpose(slot.ap[0:n, j * P:(j + 1) * P], f2_raw[:, off + j * P:off + j * P + n],
                                          ident))
            V.wait(mm)
            if down_:
                V.mark(dve.tensor_copy(dst[:, 0:2 * P], slot.ap[:, 0:2 * P]))
                mm = V.mark(dve.tensor_copy(dst[0:F2 - 2 * P, 2 * P:3 * P], slot.ap[0:F2 - 2 * P, 2 * P:3 * P]))
            else:
                mm = V.mark(dve.tensor_copy(dst, slot.ap[:, 0:F2J * P]))
            slot.freed = (mm,)
        state["w2_ready"] = mm

    N2 = TPB * F2

    def l2f_at(b):
        return b % 2 * (4 * N2 + 96)

    def l2f_prologue(b):
        yield from norm(b, turn=False)
        flat = kT[:, cols(b)]
        at = l2f_at(b)
        yield from hold(at)
        yield from fp4(flat, S, [xn_ready[b], *l2f_free[b % 2]], at)
        release(at)
        yield from turn_batch(b, xn, xnT, restored[at])

    l2f_free = {0: (), 1: ()}

    def l2f_batch(b, following):
        PE.wait(state["w2_ready"])
        at = l2f_at(b)
        hbuf = wk(at + 3 * N2 + 96, N2)
        yield from hold(at)
        for i, t in enumerate(tiles(b)):
            slot = yield from claim(two, PE)
            PE.wait(xnT_ready[b])
            pe.matmul(slot.ap[:, 0, 0:F2], xnT[:, t * P:(t + 1) * P], gT[:, 0:F2], start=True, stop=True)
            m = PE.mark(pe.matmul(slot.ap[:, 1, 0:F2], xnT[:, t * P:(t + 1) * P], uT[:, 0:F2], start=True, stop=True))
            h = hbuf[:, i * F2:(i + 1) * F2]
            A.wait(m, *l2f_free[b % 2])
            m = A.mark(act.activation(h, slot.ap[:, 0, 0:F2], ACT.Silu))
            V.wait(m)
            m = V.mark(dve.tensor_tensor(h, h, slot.ap[:, 1, 0:F2], ALU.mult))
            slot.freed = (m,)
        yield
        yield from fp4(hbuf, N2, [m], at)
        m = restored[at]
        yield
        for i, t in enumerate(tiles(b)):
            slot = yield from claim(one, PE)
            PE.wait(m)
            for j in range(F2J):
                n = min(P, F2 - j * P)
                mm = PE.mark(pe.transpose(slot.ap[0:n, j * P:(j + 1) * P],
                                          hbuf[:, i * F2 + j * P:i * F2 + j * P + n], ident))
            l2f_free[b % 2] = (mm,)
            hT = wk(6144 + (b % 2 * TPB + i) * F2J * P, F2J * P)
            A.wait(mm, *state["vaug_free"])
            A.mark(act.copy(hT[:, 0:2 * P], slot.ap[:, 0:2 * P]))
            mm = A.mark(act.copy(hT[0:F2 - 2 * P, 2 * P:3 * P], slot.ap[0:F2 - 2 * P, 2 * P:3 * P]))
            slot.freed = (mm,)
            yield
            slot = yield from claim(one, PE)
            PE.wait(mm)
            for j in range(F2J):
                n = min(P, F2 - j * P)
                mm = pe.matmul(slot.ap[:, 0:E], hT[0:n, j * P:(j + 1) * P], dT[0:n, j * P:(j + 1) * P],
                               start=(j == 0), stop=(j == F2J - 1))
            mm = PE.mark(mm)
            V.wait(mm)
            mm = V.mark(dve.tensor_tensor(x[:, t, :], slot.ap[:, 0:E], x[:, t, :], ALU.add))
            slot.freed = (mm,)
        release(at)
        state["x"][b] = mm
        prologue_done[b] = spawn(following(b))

    def per_batch(stage, following):
        for b in range(B):
            await_prologue(b)
            spawn(stage(b, following))
            tick()


    def l3a_batch(b):
        yield from norm(b)
        slot = yield from claim(misc, PE)
        for q, t in enumerate(tiles(b)):
            m = pe.matmul(slot.ap[:, 0:E], xn[:, t, :], xn[:, t, :], start=(q == 0), stop=(q == TPB - 1))
        m = PE.mark(m)
        V.wait(m)
        m = V.mark(dve.tensor_copy(l3_gram[:, b, :], slot.ap[:, 0:E]))
        slot.freed = (m,)
        yield
        slot = yield from claim(misc, PE)
        PE.wait(m)
        m = PE.mark(pe.matmul(slot.ap[:, 0:E], kp("L3a_q"), l3_gram[:, b, :], start=True, stop=True))
        V.wait(m)
        m = V.mark(dve.tensor_copy(l3_mix[:, b, :], slot.ap[:, 0:E]))
        slot.freed = (m,)
        yield
        slot = yield from claim(misc, PE)
        PE.wait(m, xnT_ready[b])
        for i, t in enumerate(tiles(b)):
            m = PE.mark(pe.matmul(slot.ap[:, i * P:(i + 1) * P], xnT[:, t * P:(t + 1) * P], l3_mix[:, b, :],
                                  start=True, stop=True))
        V.wait(m)
        xs = x[:, b * TPB:(b + 1) * TPB, :]
        m = V.mark(dve.tensor_tensor(xs, slot.ap.rearrange("p (t f) -> p t f", t=TPB), xs, ALU.add))
        slot.freed = (m,)
        state["x"][b] = m
        yield
        yield from l3x_batch(b)

    l3_gram = wk(11000, B * E).rearrange("p (b f) -> p b f", b=B)
    l3_mix = wk(11512, B * E).rearrange("p (b f) -> p b f", b=B)

    def l3x_penalty():
        raw = self_stack[:].rearrange("p h t -> p (h t)").bitcast(I32)[:, 0:NT * S2 // 4] \
            .rearrange("p (t k) -> p t k", t=NT)
        V.wait(t_mask3.done())
        V.step(dve.tensor_reduce(cm[:], raw, AX, ALU.max))
        V.step(dve.tensor_scalar(cm[:], cm[:], 3e38, 3e38, ALU.mult, ALU.mult))

    def l3x_batch(b):
        yield from norm(b)
        V.wait(xnT_ready[b])
        for t in tiles(b):
            m_res = V.mark(dve.scalar_tensor_tensor(xn[:, t, :], xn[:, t, :], cm[:, t:t + 1], rw("L3x_bo"),
                                                    ALU.add, ALU.add))
        yield from project_batch(b, qT, kp("L3x_qT"), kp("L3x_bq"), 1.0, xnT_ready[b])
        PE.wait(state["kv3"], projected[b])
        slot = yield from claim(misc, PE)
        m = PE.mark(pe.matmul(slot.ap, kv3[:, b, :], qT[:, cols(b)], start=True, stop=True))
        yield
        A.wait(m)
        m = A.mark(act.copy(xnT[:, cols(b)], slot.ap))
        slot.freed = (m,)
        slot = yield from claim(misc, PE)
        PE.wait(m)
        for i, t in enumerate(tiles(b)):
            m = PE.mark(pe.matmul(slot.ap[:, i * P:(i + 1) * P], xnT[:, t * P:(t + 1) * P], kp("L3x_oT"),
                                  start=True, stop=True))
        V.wait(m, m_res)
        xs = xn[:, b * TPB:(b + 1) * TPB, :]
        m = V.mark(dve.tensor_tensor(xs, slot.ap.rearrange("p (t f) -> p t f", t=TPB), xs, ALU.add))
        slot.freed = (m,)
        V.wait(m)
        m = statistics(xn, b)
        yield
        V.wait(normalised(xn, b, m))
        wide = lambda n: rw(n).unsqueeze(1).broadcast_to([P, TPB, E])
        V.step(dve.tensor_tensor(xs, xs, wide("L3x_g"), ALU.mult))
        V.step(dve.tensor_tensor(xs, xs, wide("L3x_b"), ALU.add))
        xb = x[:, b * TPB:(b + 1) * TPB, :]
        state["x"][b] = V.mark(dve.tensor_tensor(xb, xb, xs, ALU.add))
        yield
        yield from norm(b)

    def b1_of(name, e, j):
        return kp(name, e * FJ + j, 1) if e < NE else kp("L0f_bs1", j, 1)

    def run():
        Q.wait(m_mask)
        t_mrow.start(Q, m_scr[0], d["const_bf16"][2, 0:NC, :])
        t_mrow.start(Q, m_scr[1], maskrow[:])
        Q.wait(self_set, t_mrow.done())
        fill_mask_row(t_mrow, self_stack, m_scr[0])
        PE.wait(t_mrow.done())
        G.wait(t_rows.done())
        G.mark(pool.tensor_tensor(rw("L2a_bout"), rw("L2a_bout"), rw("L2a_lgamma"), ALU.mult))
        G.wait((G.sem, G.count))

        prologue_done[0] = spawn(l0a_prologue(0))
        finish(prologue_done[0])
        for b in range(1, B):
            prologue_done[b] = spawn(l0a_prologue(b))
        spawn(set_ctx_stack())
        prep = spawn(prepare_context())
        slow.append(prep)
        last = attention(self_stack, S,
                         lambda tile, h: va0[:, tile * 136 + h // 2 * 17:tile * 136 + h // 2 * 17 + COLS], DV0,
                         lambda b: k_filled[b], lambda b: va_ready[b], l0a_weigh, l0a_close,
                         cross_prologue("L0x_b", RSQRT128), pt_at=(8192, 3))
        state["self_free"] = (last,)
        finish(prep)
        Q.wait(t_kxwrite.done())
        cross(kp("L0x_fcT"), state["va0"], l0f_prologue, add_mask=(far_q, far_k))
        Q.wait(*state["ctx_free"])
        load_ctx_stack(kx_scr, 1, t_kxwrite.done())
        gelu_experts(kp("L0f_router"), None, NE + 1, 9 * FH, lambda e, j: b1_of("L0f_b1", e, j), t_w0, 0,
                     NE + 1, ffn_w, l1a_prologue)
        Q.wait(*state["ffn_free"])
        t_w1.start(Q, ffn_w[:, 0:F2_AT], d["L1f_w"][:, :])
        t_w2.start(Q, f2_raw, d["L2f_w"][:, :])
        lifter[0] = V
        l1_attention(cross_prologue("L1x_bo", RSQRT8, project="L1x_qT"))
        lifter[0] = A
        load_values(1)
        cross(kp("L1x_oT"), t_vload.done(), ffn_prologue)
        load_ctx_stack(c_scr, 0, t_cwrite.done())
        load_values(0)
        Q.wait(*state["self_free"])
        t_mask3.start(Q, self_stack[:].rearrange("p h t -> p (h t)").bitcast(I32)[:, 0:NT * S2 // 4]
                      .rearrange("p (t k) -> p t k", t=NT), d["mask_L3"].rearrange("b o (j p) k -> p (b o j) k", p=P))
        slow.append(spawn(l2f_weights()))
        swiglu_experts(t_w1, l2a_prologue)
        l2_attention(cross_prologue(None, RSQRT8))
        cross(kp("L2x_T"), t_vload.done(), l2f_prologue)
        w3 = ctx_stack[:].rearrange("p h t -> p (h t)").bitcast(F32)
        Q.wait(*state["ctx_free"])
        t_w3.start(Q, w3, d["L3f_w"][:, :])
        l3x_penalty()
        per_batch(l2f_batch, l3a_batch)
        gelu_experts(kp("L3f_router"), 1e-8, NE, NE * FH, lambda e, j: b1_of("L3f_b1", e, j), t_w3, 1, NE, w3, None)

    run()
    finish_out()


def shape_constants():
    k = np.arange(P)
    ident = np.eye(P, dtype=np.float32)
    blockdiag = (k[:, None] // D == k[None, :] // D).astype(np.float32)
    far = np.where(k[None, :] > k[:, None], np.float32(BIG), np.float32(0))
    rev = np.broadcast_to(np.arange(NE, 0, -1, dtype=np.float32), (P, NE))
    f32 = np.float32
    inv = f32(1.0) / f32(10000.0) ** (np.arange(0, D, 2, dtype=np.float32) / f32(D))
    pos = np.arange(S, dtype=np.float32)
    freqs = np.repeat(pos[:, None] * inv[None, :], 2, axis=-1)
    sv = (np.arange(0, D, 2, dtype=np.float32) + f32(0.4 * D)) / f32(1.4 * D)
    scale = sv[None, :] ** ((pos - S // 2) / f32(512.0))[:, None]
    scale = np.concatenate([scale, scale], axis=-1)
    sign = np.where(np.arange(D) % 2 == 0, f32(-1), f32(1))
    cos, sin = np.cos(freqs), np.sin(freqs) * sign
    tables = [cos * scale * D ** -0.5, sin * scale * D ** -0.5, cos / scale, sin / scale]
    tables = [np.tile(t.T.astype(np.float32), (H, 1)) for t in tables]
    return ident, blockdiag, far, rev, tables


def lay_out(inp):
    g = lambda n: np.asarray(inp[n])
    ident, blockdiag, far, rev, tables = shape_constants()

    def fill(at, n, parts):
        out = np.zeros((P, n), np.float32)
        assert set(parts) == set(at)
        for name, a in parts.items():
            lo, w = at[name]
            assert a.shape == (P, w), (name, a.shape, w)
            out[:, lo:lo + w] = a
        return out

    col = lambda a: a.reshape(-1, P).T
    keep = fill(KEEP_AT, KEEP_N, {
        "ident": ident, "blockdiag": blockdiag, "rev": rev,
        "L0x_fcT": g("L0_xattn_W_fc").T, "L0f_router": g("L0_ffn_w_router").T,
        "L1a_qkv": np.concatenate([g("L1_attn_W_qkv"), g("L1_attn_w_sur")[:, None]], 1),
        "L1a_out": g("L1_attn_W_out"), "L1x_qT": g("L1_xattn_Wq").T, "L1x_kT": g("L1_xattn_Wk").T,
        "L1x_vT": g("L1_xattn_Wv").T, "L1x_oT": g("L1_xattn_Wo").T, "L1f_router": g("L1_ffn_Wr"),
        "L2a_inT": g("L2_attn_in_proj_weight").T, "L2a_outT": g("L2_attn_out_proj_weight").T,
        "L2x_T": g("L2_xattn_w_concat").T, "L3a_q": g("L3_attn_queries"),
        "L3x_qT": g("L3_xattn_wq_w").T,
        "L3x_kvT": np.concatenate([g("L3_xattn_wk_w").T, g("L3_xattn_wv_w").T], 1),
        "L3x_oT": g("L3_xattn_wo_w").T, "L3f_router": g("L3_ffn_router_w").T,
        "L0f_b1": col(g("L0_ffn_b1")), "L0f_bs1": col(g("L0_ffn_bs1")), "L3f_b1": col(g("L3_ffn_b1")),
        "L1x_bq": g("L1_xattn_bq")[:, None], "L1x_bk": g("L1_xattn_bk")[:, None], "L3x_bq": g("L3_xattn_wq_b")[:, None],
    })
    swap = np.arange(E) ^ 1
    wq, wk_ = g("L0_attn_Wq").T, g("L0_attn_Wk").T
    l0a = fill(L0A_AT, L0A_N, {
        "qT": wq, "qpT": wq[:, swap], "kT": wk_, "kpT": wk_[:, swap], "vT": g("L0_attn_Wv").T,
        "oT": g("L0_attn_Wo").T, "qcos": tables[0], "qsin": tables[1], "kcos": tables[2], "ksin": tables[3]})
    r = {
        "L0x_b": g("L0_xattn_b_fc"), "L1a_bqkv": np.concatenate([g("L1_attn_b_qkv"), g("L1_attn_b_sur")[None]]),
        "L1a_bout": g("L1_attn_b_out"), "L1x_bv": g("L1_xattn_bv"), "L1x_bo": g("L1_xattn_bo"),
        "L2a_bin": g("L2_attn_in_proj_bias"), "L2a_gamma": g("L2_attn_gamma")[0, 0],
        "L2a_alpha": g("L2_attn_linear_alpha")[0, 0], "L2a_bout": g("L2_attn_out_proj_bias"),
        "L2a_lgamma": g("L2_attn_linear_gamma")[0, 0],
        "L3x_bkv": np.concatenate([g("L3_xattn_wk_b"), g("L3_xattn_wv_b")]), "L3x_bo": g("L3_xattn_wo_b"),
        "L3x_g": g("L3_xattn_ln_g"), "L3x_b": g("L3_xattn_ln_b"),
        "lq1": g("L0_attn_lambda_q1"), "lk1": g("L0_attn_lambda_k1"), "lq2": g("L0_attn_lambda_q2"),
        "lk2": g("L0_attn_lambda_k2"), "thr": g("L1_attn_threshold")[None],
    }
    rows = np.zeros((1, ROW_N), np.float32)
    for name, a in r.items():
        lo, w = ROW_AT[name]
        rows[0, lo:lo + w] = a

    def up(w):
        return w.transpose(2, 0, 1).reshape(E, -1)

    def dn(w):
        e, dd, f = w.shape
        return w.transpose(0, 2, 1).reshape(e, f // P, P, dd).transpose(2, 0, 1, 3).reshape(P, -1)

    def pad(w):
        a = np.zeros((F2J * P, E), np.float32)
        a[:F2] = w
        return a.reshape(F2J, P, E).transpose(1, 0, 2).reshape(P, -1)

    all0 = np.concatenate([g("L0_ffn_W1"), g("L0_ffn_Ws1")[None]]), np.concatenate([g("L0_ffn_W2"), g("L0_ffn_Ws2")[None]])
    l1 = [np.concatenate([g("L1_ffn_" + a), g("L1_ffn_" + b)[None]]) for a, b in (("Wg", "Sg"), ("Wu", "Su"), ("Wd", "Sd"))]
    arrays = {
        "const_bf16": np.stack([ident, far, np.zeros_like(ident)]).astype(mybir.dt.np(BF16)),
        "x": g("x"), "ctx_1024": g("ctx_1024"), "keep": keep, "l0a": l0a, "rows": rows,
        "mask_L0": g("mask_Bx1xSxS2_ik1"), "mask_keys": g("mask_BxS2_bf1").view(np.uint8),
        "mask_L3": g("mask_Bx1xSxS2_bf0").view(np.int32),
        "b2_L0": np.concatenate([g("L0_ffn_b2"), g("L0_ffn_bs2")[None]]), "b2_L3": g("L3_ffn_b2"),
        "L0f_w": np.concatenate([up(all0[0]), dn(all0[1])], 1),
        "L1f_w": np.concatenate([up(l1[0].transpose(0, 2, 1)), up(l1[1].transpose(0, 2, 1)),
                                 dn(l1[2].transpose(0, 2, 1))], 1),
        "L2f_w": np.concatenate([pad(g("L2_ffn_w_gate")), pad(g("L2_ffn_w_up")), g("L2_ffn_w_down")], 1),
        "L3f_w": np.concatenate([up(g("L3_ffn_w1")), dn(g("L3_ffn_w2"))], 1),
    }
    return {n: np.ascontiguousarray(a) for n, a in arrays.items()}


def kernel(**inputs):
    import concourse.bacc as bacc
    from concourse.bass_utils import run_bass_kernel_spmd

    nc = bacc.Bacc("TRN2", target_bir_lowering=False, num_devices=1)
    arrays = lay_out(inputs)
    d = {n: nc.dram_tensor("in_" + n, a.shape, mybir.dt.from_np(a.dtype), kind="ExternalInput").ap()
         for n, a in arrays.items()}
    out = nc.dram_tensor("out_x", (B, S, E), F32, kind="ExternalOutput").ap()
    decoder(nc, d, out)
    r = run_bass_kernel_spmd(nc, [{"in_" + n: a for n, a in arrays.items()}], core_ids=[0])
    return r.results[0]["out_x"]
```
